# Optimizing a Trainium2 kernel written in Bass

```python
import numpy as np
import jax
import jax.numpy as jnp

def _softmax(x, axis=-1):
    return jax.nn.softmax(x, axis=axis)

def _gelu(x):
    return jax.nn.gelu(x, approximate=True)

def _silu(x):
    return jax.nn.silu(x)

def _sigmoid(x):
    return jax.nn.sigmoid(x)

def _layernorm(x, axis=-1, eps=1e-05):
    m = jnp.mean(x, axis=axis, keepdims=True)
    v = jnp.var(x, axis=axis, keepdims=True)
    return (x - m) / jnp.sqrt(v + eps)

def _scatter_add(tgt, idx, src, axis=0):
    return tgt.at[idx].add(src)

def _segment_sum(src, seg, n):
    return jax.ops.segment_sum(src, seg, n)
kernel_name = 'mk_xattn_ffn_d1_seqx_r8_f9c058'

def setup_inputs(seed: int=0):
    np.random.seed(seed)
    _w = jnp.asarray

    def _rec_inputs():
        import jax
        import jax.numpy as jnp
        _rk = jax.random.key(seed)
        x = -0.0002928 + 1 * jax.random.normal(jax.random.fold_in(_rk, 1), (16, 56, 128), jnp.float32)
        _lenS = 56 - jax.random.randint(jax.random.fold_in(_rk, 7), (16,), 0, max(1, 56 // 4) + 1, jnp.int32)
        _lenS2 = 1500 - jax.random.randint(jax.random.fold_in(_rk, 8), (16,), 0, max(1, 1500 // 4) + 1, jnp.int32)
        _ctx_1024P = jax.random.normal(jax.random.fold_in(_rk, 11), (16, 16, 128), jnp.float32)
        _ctx_1024c = jax.random.dirichlet(jax.random.fold_in(_rk, 511), 0.3 * jnp.ones((16,), jnp.float32), (16, 1500))
        _ctx_1024t = jnp.einsum('bsk,bkd->bsd', _ctx_1024c, _ctx_1024P)
        _ctx_1024t = _ctx_1024t * jax.lax.rsqrt(jnp.mean(jnp.square(_ctx_1024t)) + 1e-12) * 0.953939
        ctx_1024 = -1.39393e-06 + 0.999914 * (_ctx_1024t + 0.3 * jax.random.normal(jax.random.fold_in(_rk, 611), (16, 1500, 128), jnp.float32))
        _validS = jnp.arange(56)[None, :] < _lenS[:, None]
        _validS2 = jnp.arange(1500)[None, :] < _lenS2[:, None]
        _causal = jnp.tril(jnp.ones((56, 56), dtype=bool))
        mask_BxSxS2_bf1 = jnp.ones((16, 56, 1500), dtype=bool)
        return (x, ctx_1024, mask_BxSxS2_bf1)
    x, ctx_1024, mask_BxSxS2_bf1 = _rec_inputs()

    def _L0_xattn_setup():
        import jax, jax.numpy as jnp
        import numpy as np
        B, S, D = (2, 256, 128)
        H, DQK, DV, DOUT = (16, 64, 64, 128)
        key = jax.random.key(seed)
        ks = jax.random.split(key, 8)
        query = jax.random.normal(ks[0], (B, S, D), dtype=jnp.float32)
        k_in = jax.random.normal(ks[1], (B, S, D), dtype=jnp.float32)
        value = jax.random.normal(ks[2], (B, S, D), dtype=jnp.float32)
        mask = jnp.ones((B, S, S), dtype=bool)
        Wq = jax.random.normal(ks[3], (H, D, DQK), dtype=jnp.float32) * np.sqrt(2.0 / (D + DQK))
        Wk = jax.random.normal(ks[4], (H, D, DQK), dtype=jnp.float32) * np.sqrt(2.0 / (D + DQK))
        Wv = jax.random.normal(ks[5], (H, D, DV), dtype=jnp.float32) * np.sqrt(2.0 / (D + DV))
        Wo = jax.random.normal(ks[6], (H * DV, DOUT), dtype=jnp.float32) * np.sqrt(2.0 / (H * DV + DOUT))
        return {'query': query, 'key': k_in, 'value': value, 'mask': mask, 'Wq': Wq, 'Wk': Wk, 'Wv': Wv, 'Wo': Wo}
    _L0_xattn_all = _L0_xattn_setup()
    _L0_xattn_in = {k: v for k, v in _L0_xattn_all.items() if k in ('Wq', 'Wk', 'Wv', 'Wo')}
    del _L0_xattn_all

    def _L0_ffn_setup():
        import jax, jax.numpy as jnp
        import numpy as np
        D = 128
        H = 16
        KV = 8
        HD = D // H
        M = 448
        E = 8
        TOPK = 2
        EPS = 1e-06
        ROPE_THETA = 10000.0

        def _rmsnorm(x, w, eps=EPS):
            xf = x.astype(jnp.float32)
            var = jnp.mean(xf * xf, axis=-1, keepdims=True)
            return (xf * jax.lax.rsqrt(var + eps)).astype(x.dtype) * w

        def _rope(q, k):
            S = q.shape[1]
            inv_freq = 1.0 / ROPE_THETA ** (jnp.arange(0, HD, 2, dtype=jnp.float32) / HD)
            ang = jnp.arange(S, dtype=jnp.float32)[:, None] * inv_freq[None, :]
            cos = jnp.concatenate([jnp.cos(ang), jnp.cos(ang)], axis=-1)[None, :, None, :]
            sin = jnp.concatenate([jnp.sin(ang), jnp.sin(ang)], axis=-1)[None, :, None, :]

            def rot_half(t):
                t1, t2 = jnp.split(t, 2, axis=-1)
                return jnp.concatenate([-t2, t1], axis=-1)
            return (q * cos + rot_half(q) * sin, k * cos + rot_half(k) * sin)
        key = jax.random.key(seed)
        ks = jax.random.split(key, 12)
        s = 0.02
        B, S = (2, 128)
        return {'x': jax.random.normal(ks[0], (B, S, D), jnp.float32), 'ln1_w': jnp.ones((D,), jnp.float32), 'ln2_w': jnp.ones((D,), jnp.float32), 'wq': jax.random.normal(ks[1], (D, H * HD), jnp.float32) * s, 'wk': jax.random.normal(ks[2], (D, KV * HD), jnp.float32) * s, 'wv': jax.random.normal(ks[3], (D, KV * HD), jnp.float32) * s, 'wo': jax.random.normal(ks[4], (H * HD, D), jnp.float32) * s, 'router_w': jax.random.normal(ks[5], (D, E), jnp.float32) * s, 'w_gate': jax.random.normal(ks[6], (E, D, M), jnp.float32) * s, 'w_up': jax.random.normal(ks[7], (E, D, M), jnp.float32) * s, 'w_down': jax.random.normal(ks[8], (E, M, D), jnp.float32) * s}
    _L0_ffn_all = _L0_ffn_setup()
    _L0_ffn_in = {k: v for k, v in _L0_ffn_all.items() if k in ('ln1_w', 'ln2_w', 'wq', 'wk', 'wv', 'wo', 'router_w', 'w_gate', 'w_up', 'w_down')}
    del _L0_ffn_all
    return {'x': x, 'ctx_1024': ctx_1024, 'mask_BxSxS2_bf1': mask_BxSxS2_bf1, 'L0_xattn_Wq': _L0_xattn_in['Wq'], 'L0_xattn_Wk': _L0_xattn_in['Wk'], 'L0_xattn_Wv': _L0_xattn_in['Wv'], 'L0_xattn_Wo': _L0_xattn_in['Wo'], 'L0_ffn_ln1_w': _L0_ffn_in['ln1_w'], 'L0_ffn_ln2_w': _L0_ffn_in['ln2_w'], 'L0_ffn_wq': _L0_ffn_in['wq'], 'L0_ffn_wk': _L0_ffn_in['wk'], 'L0_ffn_wv': _L0_ffn_in['wv'], 'L0_ffn_wo': _L0_ffn_in['wo'], 'L0_ffn_router_w': _L0_ffn_in['router_w'], 'L0_ffn_w_gate': _L0_ffn_in['w_gate'], 'L0_ffn_w_up': _L0_ffn_in['w_up'], 'L0_ffn_w_down': _L0_ffn_in['w_down']}

def reference(x, ctx_1024, mask_BxSxS2_bf1, L0_xattn_Wq, L0_xattn_Wk, L0_xattn_Wv, L0_xattn_Wo, L0_ffn_ln1_w, L0_ffn_ln2_w, L0_ffn_wq, L0_ffn_wk, L0_ffn_wv, L0_ffn_wo, L0_ffn_router_w, L0_ffn_w_gate, L0_ffn_w_up, L0_ffn_w_down):
    import jax
    import jax.numpy as jnp

    def _L0_xattn_ref(query, key, value, mask, Wq, Wk, Wv, Wo):
        import jax, jax.numpy as jnp
        import numpy as np
        B, S, D = (2, 256, 128)
        H, DQK, DV, DOUT = (16, 64, 64, 128)
        n_seq = query.shape[-2]
        q = jnp.einsum('...i,hio->...ho', query, Wq)
        k = jnp.einsum('...i,hio->...ho', key, Wk)
        v = jnp.einsum('...i,hio->...ho', value, Wv)
        scale = 1.0 / np.sqrt(n_seq).astype(np.float32)
        logits = jnp.einsum('...ihj,...khj->...hik', q, k) * scale
        neg_inf = jnp.where(mask, jnp.float32(0.0), -jnp.inf)
        logits = logits + neg_inf[..., None, :, :]
        probs = jax.nn.softmax(logits, axis=-1)
        out = jnp.einsum('...hij,...jhk->...ihk', probs, v)
        out = out.reshape(out.shape[:-2] + (H * DV,))
        return out @ Wo

    def _L0_ffn_ref(x, ln1_w, ln2_w, wq, wk, wv, wo, router_w, w_gate, w_up, w_down):
        import jax, jax.numpy as jnp
        import numpy as np
        D = 128
        H = 16
        KV = 8
        HD = D // H
        M = 448
        E = 8
        TOPK = 2
        EPS = 1e-06
        ROPE_THETA = 10000.0

        def _rmsnorm(x, w, eps=EPS):
            xf = x.astype(jnp.float32)
            var = jnp.mean(xf * xf, axis=-1, keepdims=True)
            return (xf * jax.lax.rsqrt(var + eps)).astype(x.dtype) * w

        def _rope(q, k):
            S = q.shape[1]
            inv_freq = 1.0 / ROPE_THETA ** (jnp.arange(0, HD, 2, dtype=jnp.float32) / HD)
            ang = jnp.arange(S, dtype=jnp.float32)[:, None] * inv_freq[None, :]
            cos = jnp.concatenate([jnp.cos(ang), jnp.cos(ang)], axis=-1)[None, :, None, :]
            sin = jnp.concatenate([jnp.sin(ang), jnp.sin(ang)], axis=-1)[None, :, None, :]

            def rot_half(t):
                t1, t2 = jnp.split(t, 2, axis=-1)
                return jnp.concatenate([-t2, t1], axis=-1)
            return (q * cos + rot_half(q) * sin, k * cos + rot_half(k) * sin)
        B, S, _ = x.shape
        h = _rmsnorm(x, ln1_w)
        q = (h @ wq).reshape(B, S, H, HD)
        k = (h @ wk).reshape(B, S, KV, HD)
        v = (h @ wv).reshape(B, S, KV, HD)
        q, k = _rope(q, k)
        rep = H // KV
        k = jnp.repeat(k, rep, axis=2)
        v = jnp.repeat(v, rep, axis=2)
        scores = jnp.einsum('bqhd,bkhd->bhqk', q, k) / jnp.sqrt(jnp.float32(HD))
        causal = jnp.tril(jnp.ones((S, S), bool))
        scores = jnp.where(causal[None, None], scores, jnp.finfo(scores.dtype).min)
        attn = jax.nn.softmax(scores, axis=-1)
        ao = jnp.einsum('bhqk,bkhd->bqhd', attn, v).reshape(B, S, H * HD)
        x = x + ao @ wo
        h = _rmsnorm(x, ln2_w)
        logits = h @ router_w
        probs = jax.nn.softmax(logits, axis=-1)
        topv, topi = jax.lax.top_k(probs, TOPK)
        topv = topv / jnp.sum(topv, axis=-1, keepdims=True)
        weights = jnp.sum(jax.nn.one_hot(topi, E, dtype=h.dtype) * topv[..., None], axis=-2)
        gate = jnp.einsum('bsd,edm->bsem', h, w_gate)
        up = jnp.einsum('bsd,edm->bsem', h, w_up)
        act = jax.nn.silu(gate) * up * weights[..., None]
        moe = jnp.einsum('bsem,emd->bsd', act, w_down)
        return x + moe
    x = x + _L0_xattn_ref(_layernorm(x, axis=-1), ctx_1024, ctx_1024, mask_BxSxS2_bf1, L0_xattn_Wq, L0_xattn_Wk, L0_xattn_Wv, L0_xattn_Wo)
    x = x + _L0_ffn_ref(_layernorm(x, axis=-1), L0_ffn_ln1_w, L0_ffn_ln2_w, L0_ffn_wq, L0_ffn_wk, L0_ffn_wv, L0_ffn_wo, L0_ffn_router_w, L0_ffn_w_gate, L0_ffn_w_up, L0_ffn_w_down)
    return x

_drawn_inputs = setup_inputs


def setup_inputs(seed=0):
    import zlib

    import numpy as np

    out = dict(_drawn_inputs(seed))
    spreads = {'L0_ffn_ln1_w': (1.0, 0.6), 'L0_ffn_ln2_w': (1.0, 0.6)}
    factors = {'L0_ffn_wq': 8.0,
     'L0_ffn_wk': 8.0,
     'L0_ffn_wv': 3.864,
     'L0_ffn_wo': 3.729,
     'L0_ffn_router_w': 8.0,
     'L0_ffn_w_gate': 8.0,
     'L0_ffn_w_up': 8.0,
     'L0_ffn_w_down': 8.0}
    for name, (base, spread) in spreads.items():
        noise = np.random.default_rng([zlib.crc32(name.encode()), seed]).standard_normal(out[name].shape)
        drawn = base * np.exp(spread * noise) if base else spread * noise
        out[name] = jnp.asarray(drawn.astype(out[name].dtype))
    for name, factor in factors.items():
        out[name] = (out[name] * factor).astype(out[name].dtype)
    return out
```

```python
from contextlib import ExitStack

import concourse.bass as bass
from concourse import mybir

ALU = mybir.AluOpType
ACT = mybir.ActivationFunctionType
AX_X = mybir.AxisListType.X
F32 = mybir.dt.float32
F32R = mybir.dt.float32r
BF16 = mybir.dt.bfloat16
I32 = mybir.dt.int32
U8 = mybir.dt.uint8

B, SQ, D = 16, 56, 128
SK = 1500
H, DH = 16, 64
KT = 125
NT = SK // KT
HALF = H // 2 * SQ
COLS = H * SQ
UNITS = 2 * NT
KV = 8
SMALL = 12
HA, DA, E, M = 16, 8, 8, 448
MT = 112
NM = M // MT
RMS_EPS = 1e-6
SCALE_A = float(1.0 / DA ** 0.5)
NP = 4
PAIRS = B // 2
ROW2 = 64
ROWS = ROW2 + SQ
CH = 500
NCH = SK // CH
HP = H // 2
MAXES = HP * NCH
BIG = 2.0 ** 100
SCALE = float(1.0 / SQ ** 0.5)
LN_EPS = 1e-5
DVE_TILES = (0, 3, 6, 9)
SPLIT_V = 512
MAX_FROM = 4
MAX_AT = {u: [d for d in range(MAXES) if MAX_FROM + d * 3 // 4 == u] for u in range(UNITS)}
RSQRT_SEED, NEWTON_STEPS = 0x5F3759DF, 3
GSETS = 6
FIRST_POOL_TILE = min(set(range(NT)) - set(DVE_TILES))
FOLD_AT, DEN_AT, PROJECT_AT = (1, 2), 8, (9, 11, 14, 17)
HEADS_FOLD = 4


def xattn_ffn_kernel(nc: bass.Bass, t, out):
    ctx, cross = ExitStack(), ExitStack()
    with ctx:
        def kept(name, shape, dtype=F32):
            return ctx.enter_context(nc.sbuf_tensor(name, shape, dtype))

        def sb(name, shape, dtype=F32):
            return cross.enter_context(nc.sbuf_tensor(name, shape, dtype))

        def sem(name):
            return ctx.enter_context(nc.semaphore(name))

        x_rows = kept("x_rows", [128, PAIRS, D])
        ident = kept("ident", [128, 128])
        stats = kept("stats", [128, PAIRS, 6])
        moments = kept("moments", [128, PAIRS, 2])
        nrm = kept("nrm", [128, 4, PAIRS])
        attn_w = {n: kept(f"attn_{n}", [D, D]) for n in ("q", "q_turned", "k", "k_turned", "v", "o")}
        router = kept("router", [D, E])
        ln_w = kept("ln_w", [D, 2])
        cos_t, sin_t = kept("cos_t", [D, ROW2]), kept("sin_t", [D, ROW2])
        head_sel = kept("head_sel", [D, HA])
        v_sel = kept("v_sel", [2 * SQ, D])
        ones = sb("ones", [128, 128])
        row_sel = sb("row_sel", [ROW2, COLS])
        pair_sel = sb("pair_sel", [ROW2 + HP, HP, 2 * SQ])
        w_left = sb("w_left", [2 * DH, H, D])
        w_right = sb("w_right", [2 * DH, H, D])
        wq, wv, wk, wo = w_left[0:DH], w_left[DH:2 * DH], w_right[0:DH], w_right[DH:2 * DH]
        a_w = sb("a_w", [D, H, D])
        b_w = sb("b_w", [D, H, D])
        xn = sb("xn", [128, PAIRS, D])
        xnT = sb("xnT", [128, PAIRS, D])
        xq = sb("xq", [D, SQ])
        raw_kT = sb("raw_kT", [D, SK])
        raw_v = sb("raw_v", [KT, NT * D])
        raw_mask = sb("raw_mask", [2 * SQ, SK], U8)
        kT_hi = [sb(f"kT_hi{i}", [D, SK], F32R) for i in range(2)]
        kT_lo = [sb(f"kT_lo{i}", [D, SK], F32R) for i in range(2)]
        v_hi = [sb(f"v_hi{i}", [KT, NT * D], F32R) for i in range(2)]
        v_lo = [sb(f"v_lo{i}", [KT, NT * D], F32R) for i in range(2)]
        bias_rows = sb("bias_rows", [2 * SQ, SK], BF16)
        bias_k = [sb(f"bias_k{i}", [ROW2 + HP, SK], F32R) for i in range(2)]
        shift = [sb(f"shift{i}", [ROW2 + HP, COLS], F32R) for i in range(2)]
        q_hi = [sb(f"q_hi{i}", [D, COLS], F32R) for i in range(2)]
        q_lo = [sb(f"q_lo{i}", [D, COLS], F32R) for i in range(2)]
        masked = [sb(f"masked{i}", [2 * SQ, CH], BF16) for i in range(2)]
        max_part = sb("max_part", [2 * SQ, HP, NCH])
        max_all = sb("max_all", [2 * SQ, HP])
        p = [sb(f"p{i}", [KT, HALF]) for i in range(NP)]
        p_hi = [sb(f"p_hi{i}", [KT, HALF], F32R) for i in range(NP)]
        p_lo = [sb(f"p_lo{i}", [KT, HALF], F32R) for i in range(NP)]
        zeros = sb("zeros", [KT, HALF])
        acc_v = [sb(f"acc_v{i}", [KT, COLS]) for i in range(2)]
        acc_g = [sb(f"acc_g{i}", [KT, COLS]) for i in range(2)]
        total = sb("total", [KT, COLS])
        o_pair = sb("o_pair", [D, H, 128])
        inv = sb("inv", [128, H])
        y_rows = sb("y_rows", [128, D])

        cross.close()

        causal_f = kept("causal_f", [SQ, COLS])
        causal = kept("causal", [SQ, COLS], BF16)
        ident_b = kept("ident_b", [SQ, SQ], BF16)
        rank_tri = kept("rank_tri", [128, E, E])
        expert_sel_f = kept("expert_sel_f", [E, E, 128])
        expert_sel = kept("expert_sel", [E, E, 128], F32R)
        z = kept("z", [128, PAIRS, D])
        zn = kept("zn", [128, PAIRS, D])
        junk = kept("junk", [128, D])
        hT = kept("hT", [D, PAIRS * 128])
        hT_twice = kept("hT_twice", [D, B, 2 * SQ])
        turn_a, turn_b = kept("turn_a", [D, 512]), kept("turn_b", [D, 512])
        qT, kT = kept("qT", [D, PAIRS * 128]), kept("kT", [D, PAIRS * 128])
        v_heads = kept("v_heads", [2 * SQ, B, D])
        k_heads = [kept(f"k_heads{i}", [D, HA, SQ]) for i in range(4)]
        att_max = kept("att_max", [128, PAIRS, HA])
        att_den = kept("att_den", [128, PAIRS, HA])
        att_inv = kept("att_inv", [128, PAIRS, HA])
        att = [kept(f"att{i}", [128, HA, SQ]) for i in range(3)]
        attT = [kept(f"attT{i}", [2 * SQ, HA // 2, ROWS]) for i in range(2)]
        ao = [kept(f"ao{i}", [128, D]) for i in range(2)]
        aoT = [kept(f"aoT{i}", [D, ROWS]) for i in range(2)]
        h_hi, h_lo = kept("h_hi", [D, PAIRS * 128], F32R), kept("h_lo", [D, PAIRS * 128], F32R)
        gates = kept("gates", [128, PAIRS, E])
        gate_max, gate_sum = kept("gate_max", [128, PAIRS]), kept("gate_sum", [128, PAIRS])
        above, same = kept("above", [128, PAIRS, E, E]), kept("same", [128, PAIRS, E, E])
        rank = kept("rank", [128, PAIRS, E])
        gateT_hi, gateT_lo = kept("gateT_hi", [E, PAIRS * 128], F32R), kept("gateT_lo", [E, PAIRS * 128], F32R)
        up_raw = [kept(f"up_raw{i}", [D, 2, M]) for i in range(2)]
        up_hi = [kept(f"up_hi{i}", [D, 2, M], F32R) for i in range(2)]
        up_lo = [kept(f"up_lo{i}", [D, 2, M], F32R) for i in range(2)]
        down_raw = [kept(f"down_raw{i}", [MT, NM, D]) for i in range(2)]
        down_hi = [kept(f"down_hi{i}", [MT, NM, D], F32R) for i in range(2)]
        down_lo = [kept(f"down_lo{i}", [MT, NM, D], F32R) for i in range(2)]
        gate_cols = [kept(f"gate_cols{i}", [MT, HALF]) for i in range(2)]
        silu = [kept(f"silu{i}", [MT, HALF]) for i in range(3)]
        up = [kept(f"up{i}", [MT, HALF]) for i in range(3)]
        act_f = [kept(f"act_f{i}", [MT, HALF]) for i in range(3)]
        act_hi = [kept(f"act_hi{i}", [MT, HALF], F32R) for i in range(3)]
        act_lo = [kept(f"act_lo{i}", [MT, HALF], F32R) for i in range(3)]
        moeT = kept("moeT", [D, PAIRS * 128])

        def bank(name):
            return ctx.enter_context(nc.psum_tensor(name, [128, 512], F32))

        scores = [bank(f"scores{i}") for i in range(2)]
        outT = [bank(f"outT{i}") for i in range(2)]
        maxs = [bank(f"maxs{i}") for i in range(2)]
        misc = [bank(f"misc{i}") for i in range(2)]

        s_x = sem("s_x")
        s_wqk, s_wvo, s_const = sem("s_wqk"), sem("s_wvo"), sem("s_const")
        s_set = sem("s_set")
        s_gset = sem("s_gset")
        s_shset = sem("s_shset")
        s_fold = sem("s_fold")
        s_folded = sem("s_folded")
        s_ln = sem("s_ln")
        s_xn = sem("s_xn")
        s_xT, s_xT_used = sem("s_xT"), sem("s_xT_used")
        s_raw_kT, s_raw_v, s_raw_mask = sem("s_raw_kT"), sem("s_raw_v"), sem("s_raw_mask")
        s_kT_hi, s_kT_lo, s_v_hi, s_v_lo = sem("s_kT_hi"), sem("s_kT_lo"), sem("s_v_hi"), sem("s_v_lo")
        s_bias_rows, s_bias_k = sem("s_bias_rows"), sem("s_bias_k")
        s_xq, s_q, s_q_hi, s_q_lo = sem("s_xq"), sem("s_q"), sem("s_q_hi"), sem("s_q_lo")
        s_max, s_max_used, s_max_all = sem("s_max"), sem("s_max_used"), sem("s_max_all")
        s_max_seen = sem("s_max_seen")
        s_maxT, s_shift = sem("s_maxT"), sem("s_shift")
        s_scores, s_p, s_p_lo = sem("s_scores"), sem("s_p"), sem("s_p_lo")
        s_pv = sem("s_pv")
        s_acc_v, s_acc_g, s_total = sem("s_acc_v"), sem("s_acc_g"), sem("s_total")
        s_den, s_inv, s_o = sem("s_den"), sem("s_inv"), sem("s_o")
        s_y, s_y_add = sem("s_y"), sem("s_y_add")
        s_out = sem("s_out")
        s_small, s_mixed = sem("s_small"), sem("s_mixed")
        s_cast, s_twice = sem("s_cast"), sem("s_twice")
        s_step = sem("s_step")
        s_zn, s_hT, s_hT_sb = sem("s_zn"), sem("s_hT"), sem("s_hT_sb")
        s_qk, s_rope, s_v, s_v_sb = sem("s_qk"), sem("s_rope"), sem("s_v"), sem("s_v_sb")
        s_kh, s_att, s_att_sub, s_att_exp = sem("s_kh"), sem("s_att"), sem("s_att_sub"), sem("s_att_exp")
        s_attT, s_attT_sb, s_ao, s_ao_sb = sem("s_attT"), sem("s_attT_sb"), sem("s_ao"), sem("s_ao_sb")
        s_aoT, s_aoT_sb, s_wo, s_z = sem("s_aoT"), sem("s_aoT_sb"), sem("s_wo"), sem("s_z")
        s_z2, s_zn2, s_h2, s_h_hi, s_h_lo = sem("s_z2"), sem("s_zn2"), sem("s_h2"), sem("s_h_hi"), sem("s_h_lo")
        s_h2_sb = sem("s_h2_sb")
        s_logits, s_lmax, s_lexp, s_gates = sem("s_logits"), sem("s_lmax"), sem("s_lexp"), sem("s_gates")
        s_gT, s_gT_hi, s_gT_lo = sem("s_gT"), sem("s_gT_hi"), sem("s_gT_lo")
        s_up_raw = [sem(f"s_up_raw{i}") for i in range(2)]
        s_down_raw = [sem(f"s_down_raw{i}") for i in range(2)]
        s_w_hi, s_w_lo = sem("s_w_hi"), sem("s_w_lo")
        s_gc, s_gc_sb = sem("s_gc"), sem("s_gc_sb")
        s_gate, s_up, s_silu, s_upw, s_actf = sem("s_gate"), sem("s_up"), sem("s_silu"), sem("s_upw"), sem("s_actf")
        s_act_hi, s_act_lo, s_down = sem("s_act_hi"), sem("s_act_lo"), sem("s_down")
        s_moeT, s_moe, s_res, s_final = sem("s_moeT"), sem("s_moe"), sem("s_res"), sem("s_final")

        def on_vector(u):
            return (u // 2) % NT in DVE_TILES

        def sums_done(b, u, vector):
            each = sum(on_vector(w) == vector for w in range(UNITS))
            return each * b + sum(on_vector(w) == vector for w in range(u + 1))

        block = ctx.enter_context(nc.Block())

        @block.sync
        def _(sp):
            sp.wait_ge(s_set, 1)
            for half in range(2):
                sp.dma_start(x_rows[ROW2 * half:ROW2 * half + SQ, :, :],
                             t["x"].rearrange("(t two) q d -> two q t d", two=2)[half]).then_inc(s_x, 16)
            for w, name in ((wq, "wqT"), (wk, "wkT")):
                sp.dma_start(w, t[name]).then_inc(s_wqk, 16)
            for c, name in ((ident, "ident"), (row_sel, "row_sel")):
                sp.dma_start(c[:], t[name]).then_inc(s_const, 16)
            sp.dma_start(pair_sel[ROW2:ROW2 + HP], t["pair_sel"]).then_inc(s_const, 16)

            def load(b):
                sp.dma_start(raw_kT[:], t["ctxT"][b]).then_inc(s_raw_kT, 16)
                for half in range(2):
                    sp.dma_start(raw_mask[SQ * half:SQ * half + SQ], t["mask"][b]).then_inc(s_raw_mask, 16)
                sp.dma_start(raw_v[:], t["ctx"][b]).then_inc(s_raw_v, 16)

            load(0)
            for w, name in ((wv, "wvT"), (wo, "wo")):
                sp.dma_start(w, t[name]).then_inc(s_wvo, 16)
            sp.wait_ge(s_bias_k, NCH)
            for n, w in attn_w.items():
                sp.dma_start(w[:], t[f"attn_{n}"]).then_inc(s_small, 16)
            for c, name in ((router, "router"), (ln_w, "ln_w"), (cos_t, "cos"), (sin_t, "sin"),
                            (head_sel, "head_sel"), (v_sel, "v_sel")):
                sp.dma_start(c[:], t[name]).then_inc(s_small, 16)
            with sp.Fori(1, B) as b:
                sp.wait_ge(s_kT_lo, NCH * b)
                sp.dma_start(raw_kT[:], t["ctxT"][bass.ds(b, 1)].rearrange("o p n -> (o p) n")).then_inc(s_raw_kT, 16)
                for half in range(2):
                    sp.dma_start(raw_mask[SQ * half:SQ * half + SQ],
                                 t["mask"][bass.ds(b, 1)].rearrange("o p n -> (o p) n")).then_inc(s_raw_mask, 16)
                sp.wait_ge(s_v_lo, NCH * b)
                sp.dma_start(raw_v[:], t["ctx"][bass.ds(b, 1)].rearrange("o p n -> (o p) n")).then_inc(s_raw_v, 16)
            sp.wait_ge(s_y_add, H * PAIRS)
            for c, name in ((causal_f, "causal"), (rank_tri, "rank_tri"), (expert_sel_f, "expert_sel")):
                sp.dma_start(c[:], t[name]).then_inc(s_mixed, 16)
            for e in range(E):
                if e >= 2:
                    sp.wait_ge(s_w_lo, 3 * (e - 1))
                sp.dma_start(up_raw[e % 2][:], t["w_up"][e]).then_inc(s_up_raw[e % 2], 16)
                sp.dma_start(down_raw[e % 2][:], t["w_down"][e]).then_inc(s_down_raw[e % 2], 16)
            for i in range(PAIRS):
                sp.wait_ge(s_final, i + 1)
                for half in range(2):
                    sp.dma_start(out[2 * i + half], z[ROW2 * half:ROW2 * half + SQ, i, :]).then_inc(s_out, 16)
            sp.wait_ge(s_out, 32 * PAIRS)

        @block.tensor
        def _(pe):
            banks = scores + outT
            for which, (w1, w2, loaded) in enumerate(((wq, wk, s_wqk), (wv, wo, s_wvo))):
                pe.wait_ge(loaded, 32)
                for g, bank_ in enumerate(banks):
                    if which:
                        pe.wait_ge(s_folded, g + 1)
                    for k in range(HEADS_FOLD):
                        mm = nc.tensor.matmul(bank_[:, k * D:(k + 1) * D], w1[:, HEADS_FOLD * g + k, :],
                                              w2[:, HEADS_FOLD * g + k, :], start=True, stop=True)
                    mm.then_inc(s_fold, 1)
                if not which:
                    pe.wait_ge(s_const, 48)
                    for i in range(PAIRS):
                        pe.wait_ge(s_xn, i + 1)
                        mm = nc.tensor.transpose(maxs[i // 4][:, (i % 4) * D:(i % 4) * D + D], xn[:, i, :], ident[:])
                        if i % 4 == 3:
                            mm.then_inc(s_xT, 1)

            def fold_queries(b, half):
                pe.wait_ge(s_xq, b + 1)
                for k in range(HP):
                    mm = nc.tensor.matmul(misc[half][:, k * SQ:(k + 1) * SQ], a_w[:, HP * half + k, :], xq[:],
                                          start=True, stop=True)
                mm.then_inc(s_q, 1)

            def max_scores(b, q, d, first=False):
                r, c = d // NCH, d % NCH
                if first and d < NCH:
                    pe.wait_ge(s_kT_hi, c + 1)
                if d % (MAXES // 2) == 0:
                    pe.wait_ge(s_q_hi, 2 * b + 1 + d // (MAXES // 2))
                if not (first and d < 2):
                    pe.wait_ge(s_max_used, MAXES * b + d - 1)
                nc.tensor.matmul(maxs[d % 2][0:2 * SQ, 0:CH], q_hi[q][:, r * 2 * SQ:(r + 1) * 2 * SQ],
                                 kT_hi[q][:, c * CH:(c + 1) * CH], start=True, stop=True).then_inc(s_max, 1)

            def turn_maxima(b):
                pe.wait_ge(s_max_all, b + 1)
                nc.tensor.matmul(misc[1][ROW2:ROW2 + HP, 0:2 * SQ], max_all[:], ident[0:2 * SQ, 0:2 * SQ],
                                 start=True, stop=True).then_inc(s_maxT, 1)

            def score(b, q, u, first):
                ks, cs, out_ = slice(u // 2 * KT, u // 2 * KT + KT), slice(u % 2 * HALF, u % 2 * HALF + HALF), \
                    scores[u % 2][0:KT, 0:HALF]
                if first and u == 0:
                    pe.wait_ge(s_kT_lo, NCH)
                    pe.wait_ge(s_q_lo, 2)
                    pe.wait_ge(s_bias_k, NCH)
                if not (first and u < 2):
                    pe.wait_ge(s_p, UNITS * b + u - 1)
                nc.tensor.matmul(out_, kT_hi[q][:, ks], q_hi[q][:, cs], start=True, stop=False)
                nc.tensor.matmul(out_, kT_hi[q][:, ks], q_lo[q][:, cs], start=False, stop=False)
                nc.tensor.matmul(out_, kT_lo[q][:, ks], q_hi[q][:, cs], start=False, stop=False)
                if u == 0:
                    pe.wait_ge(s_shift, b + 1)
                nc.tensor.matmul(out_, bias_k[q][:, ks], shift[q][:, cs], start=False, stop=True).then_inc(s_scores, 1)

            def weigh(b, q, u, first):
                j, half = u // 2, u % 2
                vs, out_ = slice(j * D, (j + 1) * D), outT[half][:, 0:HALF]
                if first and u == 0:
                    pe.wait_ge(s_v_lo, NCH)
                if j == 0 and not first:
                    pe.wait_ge(s_o, 2 * b - 1 + half)
                pe.wait_ge(s_p_lo, UNITS * b + u + 1)
                nc.tensor.matmul(out_, v_hi[q][:, vs], p_hi[u % NP][:], start=(j == 0), stop=False)
                nc.tensor.matmul(out_, v_hi[q][:, vs], p_lo[u % NP][:], start=False, stop=False)
                nc.tensor.matmul(out_, v_lo[q][:, vs], p_hi[u % NP][:], start=False, stop=(j == NT - 1)) \
                    .then_inc(s_pv, 1)

            def denominators(b, q):
                pe.wait_ge(s_total, 2 * (b + 1))
                for h in range(H):
                    mm = nc.tensor.matmul(misc[1][ROW2 * q:ROW2 * q + SQ, h:h + 1], total[:, h * SQ:(h + 1) * SQ],
                                          ones[0:KT, 0:1], start=True, stop=True)
                mm.then_inc(s_den, 1)

            def project(pair, g):
                for k in range(HEADS_FOLD):
                    h = HEADS_FOLD * g + k
                    mm = nc.tensor.matmul(misc[g % 2][0:ROWS, k * D:(k + 1) * D], o_pair[:, h, 0:ROWS], b_w[:, h, :],
                                          start=True, stop=True)
                mm.then_inc(s_y, 1)

            def step(b, q, pair=0, first=False, last=False):
                for u in range(UNITS):
                    score(b, q, u, first)
                    if u >= 2:
                        weigh(b, q, u - 2, first)
                    elif not first:
                        weigh(b - 1, 1 - q, UNITS - 2 + u, False)
                    if not last:
                        if u in FOLD_AT:
                            fold_queries(b + 1, FOLD_AT.index(u))
                        for d in MAX_AT[u]:
                            max_scores(b + 1, 1 - q, d)
                    if u == DEN_AT and not first:
                        denominators(b - 1, 1 - q)
                    if u in PROJECT_AT and q == 0 and not first:
                        project(pair, PROJECT_AT.index(u))
                    if u == UNITS - 1 and not last:
                        turn_maxima(b + 1)

            pe.wait_ge(s_folded, 2 * len(banks))
            pe.wait_ge(s_xT_used, 2)
            fold_queries(0, 0)
            fold_queries(0, 1)
            for d in range(MAXES):
                max_scores(0, 0, d, first=True)
            pe.wait_ge(s_q_lo, 2)
            turn_maxima(0)
            step(0, 0, first=True)
            with pe.Fori(0, PAIRS - 1) as i:
                step(2 * i + 1, 1)
                step(2 * i + 2, 0, pair=i)
            step(B - 1, 1, last=True)
            for u in (UNITS - 2, UNITS - 1):
                weigh(B - 1, 1, u, False)
            denominators(B - 1, 1)
            pe.wait_ge(s_o, 2 * B)
            for g in range(H // HEADS_FOLD):
                if g == 1:
                    pe.wait_ge(s_inv, B)
                elif g > 1:
                    pe.wait_ge(s_y_add, H * (PAIRS - 1) + HEADS_FOLD * (g - 1))
                project(PAIRS - 1, g)

            bank = scores + outT + maxs + misc

            def batch(tile, b):
                return tile[:, ROW2 * b:ROW2 * b + SQ]

            def turn_rows(rows, done, sem_, free=None):
                for i in range(PAIRS):
                    pe.wait_ge(done, i + 1)
                    mm = nc.tensor.transpose(bank[4 + i // 4][:, i % 4 * 128:i % 4 * 128 + 128], rows[:, i, :], ident[:])
                    if i % 4 == 3:
                        mm.then_inc(sem_, 1)

            turn_rows(zn, s_zn, s_hT)
            pe.wait_ge(s_small, 16 * SMALL)
            for c in range(2):
                pe.wait_ge(s_hT_sb, c + 1)
                for k, n in enumerate(("q", "q_turned", "k", "k_turned")):
                    if c:
                        pe.wait_ge(s_rope, 3 * (k // 2) + k % 2 + 1)
                    nc.tensor.matmul(bank[k][:], attn_w[n][:], hT[:, 512 * c:512 * c + 512],
                                     start=True, stop=True).then_inc(s_qk, 1)
            pe.wait_ge(s_twice, 2)
            for b in range(B):
                if b % 4 == 0 and b >= 8:
                    pe.wait_ge(s_v_sb, b // 4 - 1)
                mm = nc.tensor.matmul(bank[6 + b // 4 % 2][0:2 * SQ, b % 4 * D:b % 4 * D + D],
                                      hT_twice[:, b, :], attn_w["v"][:],
                                      start=True, stop=True)
                if b % 4 == 3:
                    mm.then_inc(s_v, 1)

            def attend(i):
                if i < 2:
                    pe.wait_ge(s_rope, 12)
                    pe.wait_ge(s_cast, 2)
                else:
                    pe.wait_ge(s_att_sub, i - 1)
                for h in range(2):
                    b = 2 * i + h
                    pe.wait_ge(s_kh, b + 1)
                    for c in range(2):
                        o = bank[2 * (i % 2) + c][ROW2 * h:ROW2 * h + SQ, 0:HALF]
                        nc.tensor.matmul(o, batch(qT, b), k_heads[b % 4][:, HP * c:HP * (c + 1), :],
                                         start=True, stop=False)
                        mm = nc.tensor.matmul(o, ident_b[:], causal[:, c * HALF:(c + 1) * HALF], start=False, stop=True)
                mm.then_inc(s_att, 1)

            def turn_attention(i):
                pe.wait_ge(s_att_exp, i + 1)
                if i:
                    pe.wait_ge(s_attT_sb, 2 * i)
                for hp in range(HA // 2):
                    mm = nc.tensor.transpose(bank[4 + hp // 4][0:2 * SQ, hp % 4 * ROWS:hp % 4 * ROWS + ROWS],
                                             att[i % 3][0:ROWS, 2 * hp:2 * hp + 2, :], ident[0:ROWS, 0:ROWS])
                mm.then_inc(s_attT, 1)

            def weigh_values(i):
                pe.wait_ge(s_attT_sb, 2 * (i + 1))
                pe.wait_ge(s_v_sb, 4)
                if i:
                    pe.wait_ge(s_ao_sb, i)
                for hp in range(HA // 2):
                    for h in range(2):
                        mm = nc.tensor.matmul(bank[6][ROW2 * h:ROW2 * h + SQ, 16 * hp:16 * hp + 16],
                                              attT[i % 2][:, hp, ROW2 * h:ROW2 * h + SQ],
                                              v_heads[:, 2 * i + h, 16 * hp:16 * hp + 16], start=True, stop=True)
                mm.then_inc(s_ao, 1)

            def turn_output(i):
                pe.wait_ge(s_ao_sb, i + 1)
                if i:
                    pe.wait_ge(s_z, i)
                nc.tensor.transpose(bank[7][:, 0:ROWS], ao[i % 2][0:ROWS, :], ident[0:ROWS, 0:ROWS]).then_inc(s_aoT, 1)

            def project_output(i):
                pe.wait_ge(s_aoT_sb, i + 1)
                nc.tensor.matmul(bank[7][0:ROWS, 128:256], aoT[i % 2][:], attn_w["o"][:], start=True, stop=True) \
                    .then_inc(s_wo, 1)

            for i in range(PAIRS + 3):
                if i < PAIRS:
                    attend(i)
                if 1 <= i <= PAIRS:
                    turn_attention(i - 1)
                if 3 <= i:
                    project_output(i - 3)
                if 2 <= i <= PAIRS + 1:
                    weigh_values(i - 2)
                    turn_output(i - 2)

            turn_rows(zn, s_zn2, s_h2)
            for i in range(PAIRS):
                pe.wait_ge(s_h2_sb, i // 4 + 1)
                mm = nc.tensor.matmul(bank[6][0:ROWS, E * i:E * i + E], hT[:, 128 * i:128 * i + ROWS], router[:],
                                      start=True, stop=True)
            mm.then_inc(s_logits, 1)
            pe.wait_ge(s_gates, 1)
            for i in range(PAIRS):
                mm = nc.tensor.transpose(bank[i // 4][0:E, i % 4 * 128:i % 4 * 128 + ROWS], gates[0:ROWS, i, :],
                                         ident[0:ROWS, 0:ROWS])
                if i % 4 == 3:
                    mm.then_inc(s_gT, 1)

            def columns(tile, half):
                return tile[:, half * 512:half * 512 + 512].rearrange("p (b n) -> p b n", n=ROW2)[:, :, 0:SQ]

            def spread_gates(e, half):
                pe.wait_ge(s_gT_lo, 2)
                if 2 * e + half >= 1:
                    pe.wait_ge(s_gc_sb, 2 * e + half)
                nc.tensor.matmul(bank[6][0:MT, 0:HALF], expert_sel[:, e, 0:MT], columns(gateT_hi, half),
                                 start=True, stop=False)
                nc.tensor.matmul(bank[6][0:MT, 0:HALF], expert_sel[:, e, 0:MT], columns(gateT_lo, half),
                                 start=False, stop=True).then_inc(s_gc, 1)

            def hidden(n):
                e, half, m = n // (2 * NM), n // NM % 2, n % NM
                ms = slice(MT * m, MT * m + MT)
                if n % (2 * NM) == 0:
                    pe.wait_ge(s_w_lo, 3 * (e + 1))
                    pe.wait_ge(s_h_lo, 2)
                if n % NM == 0:
                    spread_gates(e, half)
                for k, (sem_, used) in enumerate(((s_gate, s_silu), (s_up, s_upw))):
                    if n >= 2:
                        pe.wait_ge(used, n - 1)
                    elif n == 0:
                        pe.wait_ge(s_gT_hi, 2)
                    o = bank[2 * k + n % 2][0:MT, 0:HALF]
                    nc.tensor.matmul(o, up_hi[e % 2][:, k, ms], columns(h_hi, half), start=True, stop=False)
                    nc.tensor.matmul(o, up_hi[e % 2][:, k, ms], columns(h_lo, half), start=False, stop=False)
                    nc.tensor.matmul(o, up_lo[e % 2][:, k, ms], columns(h_hi, half), start=False, stop=True) \
                        .then_inc(sem_, 1)

            def down(n):
                e, half, m = n // (2 * NM), n // NM % 2, n % NM
                pe.wait_ge(s_act_lo, n + 1)
                o = bank[4 + half][:, 0:HALF]
                first, last = e == 0 and m == 0, e == E - 1 and m == NM - 1
                nc.tensor.matmul(o, down_hi[e % 2][:, m, :], act_hi[n % 3][:], start=first, stop=False)
                nc.tensor.matmul(o, down_hi[e % 2][:, m, :], act_lo[n % 3][:], start=False, stop=False)
                nc.tensor.matmul(o, down_lo[e % 2][:, m, :], act_hi[n % 3][:], start=False, stop=last) \
                    .then_inc(s_down, 1)

            steps = E * 2 * NM
            for n in range(steps + 2):
                if n < steps:
                    hidden(n)
                if n >= 2:
                    down(n - 2)

            for i in range(PAIRS):
                pe.wait_ge(s_moeT, i // 4 + 1)
                if i >= 4:
                    pe.wait_ge(s_final, i - 3)
                nc.tensor.transpose(bank[i % 4][0:ROWS, 0:D], moeT[:, 128 * i:128 * i + ROWS], ident[:]) \
                    .then_inc(s_moe, 1)

        @block.scalar
        def _(act):
            banks = scores + outT
            for which, w in enumerate((a_w, b_w)):
                for g, bank_ in enumerate(banks):
                    act.wait_ge(s_fold, len(banks) * which + g + 1)
                    nc.scalar.copy(w[:, HEADS_FOLD * g:HEADS_FOLD * (g + 1), :], bank_[:]).then_inc(s_folded, 1)

            def split_keys(b, q, c):
                if c == 0:
                    act.wait_ge(s_raw_kT, 16 * (b + 1))
                nc.scalar.copy(kT_hi[q][:, c * CH:(c + 1) * CH], raw_kT[:, c * CH:(c + 1) * CH]).then_inc(s_kT_hi, 1)

            def split_values(b, q, c):
                if c == 0:
                    act.wait_ge(s_raw_v, 16 * (b + 1))
                nc.scalar.copy(v_hi[q][:, c * SPLIT_V:(c + 1) * SPLIT_V], raw_v[:, c * SPLIT_V:(c + 1) * SPLIT_V]) \
                    .then_inc(s_v_hi, 1)

            def mask_rows(b, c):
                if c == 0:
                    act.wait_ge(s_raw_mask, 32 * (b + 1))
                nc.scalar.activation(bias_rows[:, c * CH:(c + 1) * CH], raw_mask[:, c * CH:(c + 1) * CH], ACT.Copy,
                                     bias=-BIG, scale=BIG).then_inc(s_bias_rows, 1)

            def mask_keys(b, q, c, first=False):
                if first and c == 0:
                    act.wait_ge(s_gset, GSETS)
                nc.scalar.activation(bias_k[q][0:SQ, c * CH:(c + 1) * CH], raw_mask[0:SQ, c * CH:(c + 1) * CH],
                                     ACT.Copy, bias=-BIG, scale=BIG).then_inc(s_bias_k, 1)

            def take_queries(b, q, half, first=False):
                if first:
                    act.wait_ge(s_q, 2 * b + half + 1)
                nc.scalar.copy(q_hi[q][:, half * HALF:(half + 1) * HALF], misc[half][:, 0:HALF]).then_inc(s_q_hi, 1)

            def exponentials(b, u, first):
                act.wait_ge(s_scores, UNITS * b + u + 1)
                nc.scalar.activation(p_hi[u % NP][:], scores[u % 2][0:KT, 0:HALF], ACT.Exp, scale=SCALE)
                w = (b, u - NP) if u >= NP else (b - 1, u - NP + UNITS)
                if not (first and u < NP) and not on_vector(w[1]):
                    act.wait_ge(s_acc_g, sums_done(*w, False))
                nc.scalar.activation(p[u % NP][:], scores[u % 2][0:KT, 0:HALF], ACT.Exp, scale=SCALE).then_inc(s_p, 1)

            def take_output(b, q, half):
                act.wait_ge(s_pv, UNITS * b + UNITS - 1 + half)
                nc.scalar.copy(o_pair[:, HP * half:HP * (half + 1), ROW2 * q:ROW2 * q + SQ],
                               outT[half][:, 0:HALF].rearrange("p (h n) -> p h n", h=HP)).then_inc(s_o, 1)

            def step(b, q, first=False, last=False):
                n = 1 - q
                for u in range(UNITS):
                    exponentials(b, u, first)
                    if u < 2 and not first:
                        take_output(b - 1, n, u)
                    if last:
                        continue
                    if u < 3:
                        split_keys(b + 1, n, u)
                    if u in (1, 2, 3):
                        mask_rows(b + 1, u - 1)
                    if u in (3, 4):
                        take_queries(b + 1, n, u - 3)
                    if u in (5, 6, 7):
                        mask_keys(b + 1, n, u - 5)
                    if u in (8, 10, 12):
                        split_values(b + 1, n, (u - 8) // 2)

            for c in range(NCH):
                split_keys(0, 0, c)
            for half in range(2):
                take_queries(0, 0, half, first=True)
            for c in range(NCH):
                mask_rows(0, c)
            for c in range(NCH):
                mask_keys(0, 0, c, first=True)
            for c in range(NCH):
                split_values(0, 0, c)
            step(0, 0, first=True)
            with act.Fori(0, PAIRS - 1) as i:
                step(2 * i + 1, 1)
                step(2 * i + 2, 0)
            step(B - 1, 1, last=True)
            for half in range(2):
                take_output(B - 1, 1, half)

            bank = scores + outT + maxs + misc
            act.wait_ge(s_mixed, 48)
            nc.scalar.copy(causal[:], causal_f[:]).then_inc(s_cast, 1)
            nc.scalar.copy(ident_b[:], ident[0:SQ, 0:SQ]).then_inc(s_cast, 1)
            nc.scalar.copy(expert_sel[:], expert_sel_f[:]).then_inc(s_cast, 1)

            act.wait_ge(s_hT_sb, 2)
            for c in range(2):
                nc.scalar.copy(hT_twice[:, :, SQ * c:SQ * c + SQ],
                               hT[:].rearrange("p (b n) -> p b n", n=ROW2)[:, :, 0:SQ]).then_inc(s_twice, 1)

            def exponentials_a(i):
                act.wait_ge(s_att_sub, i + 1)
                nc.scalar.activation(att[i % 3][0:ROWS], att[i % 3][0:ROWS], ACT.Exp, scale=SCALE_A).then_inc(s_att_exp, 1)

            def take_attT(i):
                act.wait_ge(s_attT, i + 1)
                if i >= 2:
                    act.wait_ge(s_ao, i - 1)
                for c in range(2):
                    nc.scalar.copy(attT[i % 2][:, 4 * c:4 * c + 4, :],
                                   bank[4 + c][0:2 * SQ, 0:4 * ROWS].rearrange("p (h n) -> p h n", h=4)) \
                        .then_inc(s_attT_sb, 1)

            def take_aoT(i):
                act.wait_ge(s_aoT, i + 1)
                if i >= 2:
                    act.wait_ge(s_wo, i - 1)
                nc.scalar.copy(aoT[i % 2][:], bank[7][:, 0:ROWS]).then_inc(s_aoT_sb, 1)

            for i in range(PAIRS + 3):
                if i < PAIRS:
                    exponentials_a(i)
                if 1 <= i <= PAIRS:
                    take_attT(i - 1)
                if 2 <= i <= PAIRS + 1:
                    take_aoT(i - 2)

            for c in range(2):
                act.wait_ge(s_h2_sb, c + 1)
                nc.scalar.copy(h_hi[:, 512 * c:512 * c + 512], hT[:, 512 * c:512 * c + 512]).then_inc(s_h_hi, 1)
            act.wait_ge(s_lmax, 1)
            nc.scalar.activation(gates[0:ROWS], gates[0:ROWS], ACT.Exp).then_inc(s_lexp, 1)
            for c in range(2):
                act.wait_ge(s_gT, c + 1)
                nc.scalar.copy(gateT_hi[:, 512 * c:512 * c + 512].rearrange("p (b n) -> p b n", n=128)[:, :, 0:ROWS],
                               bank[c][0:E, :].rearrange("p (b n) -> p b n", n=128)[:, :, 0:ROWS]).then_inc(s_gT_hi, 1)

            def split_expert(e):
                act.wait_ge(s_up_raw[e % 2], 16 * (e // 2 + 1))
                act.wait_ge(s_down_raw[e % 2], 16 * (e // 2 + 1))
                if e >= 2:
                    act.wait_ge(s_down, 2 * NM * (e - 1))
                for k in range(2):
                    nc.scalar.copy(up_hi[e % 2][:, k, :], up_raw[e % 2][:, k, :]).then_inc(s_w_hi, 1)
                nc.scalar.copy(down_hi[e % 2][:], down_raw[e % 2][:]).then_inc(s_w_hi, 1)

            def take_gates(e, half):
                n = 2 * e + half
                act.wait_ge(s_gc, n + 1)
                if n >= 2:
                    act.wait_ge(s_upw, NM * (n - 1))
                nc.scalar.copy(gate_cols[n % 2][:], bank[6][0:MT, 0:HALF]).then_inc(s_gc_sb, 1)

            def silu_of(n):
                act.wait_ge(s_gate, n + 1)
                if n >= 3:
                    act.wait_ge(s_actf, n - 2)
                nc.scalar.activation(silu[n % 3][:], bank[n % 2][0:MT, 0:HALF], ACT.Silu).then_inc(s_silu, 1)

            def high(n):
                act.wait_ge(s_actf, n + 1)
                if n >= 3:
                    act.wait_ge(s_down, n - 2)
                nc.scalar.copy(act_hi[n % 3][:], act_f[n % 3][:]).then_inc(s_act_hi, 1)

            steps = E * 2 * NM
            split_expert(0)
            split_expert(1)
            for n in range(steps + 1):
                if n < steps:
                    if n % NM == 0:
                        take_gates(n // (2 * NM), n // NM % 2)
                    silu_of(n)
                    if n % (2 * NM) == 3 and 1 <= n // (2 * NM) < E - 1:
                        split_expert(n // (2 * NM) + 1)
                if n >= 1:
                    high(n - 1)
            for c in range(2):
                act.wait_ge(s_down, steps - (1 - c) * NM)
                nc.scalar.copy(moeT[:, 512 * c:512 * c + 512].rearrange("p (b n) -> p b n", n=ROW2)[:, :, 0:SQ],
                               bank[4 + c][:, 0:HALF].rearrange("p (b n) -> p b n", n=SQ)).then_inc(s_moeT, 1)

        @block.vector
        def _(dve):
            nc.vector.memset(x_rows[:], 0.0).then_inc(s_set, 1)
            nc.vector.memset(ones[:], 1.0).then_inc(s_set, 1)
            nc.vector.memset(zeros[:], 0.0).then_inc(s_set, 1)
            chain = [0]

            def link(ins):
                chain[0] += 1
                ins.then_inc(s_ln, 1)
                dve.wait_ge(s_ln, chain[0])

            def rsqrt(v, y, a):
                vi, yi, ai = (z.bitcast(I32) for z in (v, y, a))
                link(nc.vector.tensor_scalar(ai, vi, 1, None, ALU.logical_shift_right))
                link(nc.vector.tensor_scalar(yi, ai, -1, RSQRT_SEED, ALU.mult, ALU.add))
                for _ in range(NEWTON_STEPS):
                    link(nc.vector.scalar_tensor_tensor(out=a, in0=y, scalar=-0.5, in1=y, op0=ALU.mult, op1=ALU.mult))
                    link(nc.vector.tensor_tensor(a, a, v, ALU.mult))
                    link(nc.vector.scalar_tensor_tensor(out=y, in0=a, scalar=1.5, in1=y, op0=ALU.add, op1=ALU.mult))

            dve.wait_ge(s_x, 32)
            for i in range(PAIRS):
                last = nc.vector.bn_stats(stats[:, i, :], x_rows[:, i, :])
            link(last)
            for i in range(PAIRS):
                last = nc.vector.bn_aggr(moments[:, i, :], stats[:, i, :])
            link(last)
            var, rstd = nrm[:, 0, :], nrm[:, 1, :]
            link(nc.vector.tensor_scalar(var, moments[:, :, 1], LN_EPS, None, ALU.add))
            rsqrt(var, rstd, nrm[:, 2, :])
            for i in range(PAIRS):
                nc.vector.tensor_scalar(xn[:, i, :], x_rows[:, i, :], moments[:, i, 0:1], nrm[:, 1, i:i + 1],
                                        ALU.subtract, ALU.mult).then_inc(s_xn, 1)
            for half in range(2):
                dve.wait_ge(s_xT, half + 1)
                nc.vector.tensor_copy(xnT[:, 4 * half:4 * half + 4, :], maxs[half][:]).then_inc(s_xT_used, 1)
            dve.wait_ge(s_const, 48)
            for q in range(2):
                nc.vector.tensor_copy(shift[q][0:ROW2, :], row_sel[:]).then_inc(s_shset, 1)

            def pick_queries(b, pair, half, first=False):
                if first:
                    dve.wait_ge(s_xT_used, 2)
                nc.vector.tensor_copy(xq[:], xnT[:, bass.ds(pair, 1), ROW2 * half:ROW2 * half + SQ]
                                      .rearrange("p o n -> p (o n)")).then_inc(s_xq, 1)

            def split_queries(b, q, half, first=False):
                if first:
                    dve.wait_ge(s_q_hi, half + 1)
                nc.vector.tensor_tensor(q_lo[q][:, half * HALF:(half + 1) * HALF], misc[half][:, 0:HALF],
                                        q_hi[q][:, half * HALF:(half + 1) * HALF], ALU.subtract).then_inc(s_q_lo, 1)

            def split_keys(b, q, c, first=False):
                if first:
                    dve.wait_ge(s_kT_hi, c + 1)
                nc.vector.tensor_tensor(kT_lo[q][:, c * CH:(c + 1) * CH], raw_kT[:, c * CH:(c + 1) * CH],
                                        kT_hi[q][:, c * CH:(c + 1) * CH], ALU.subtract).then_inc(s_kT_lo, 1)

            def take_maxima(b, d, first=False):
                r, c = d // NCH, d % NCH
                if first:
                    dve.wait_ge(s_max, d + 1)
                    dve.wait_ge(s_bias_rows, NCH)
                    if d > 1:
                        dve.wait_ge(s_max_used, d - 1)
                nc.vector.tensor_tensor_reduce(out=masked[d % 2][:], in0=maxs[d % 2][0:2 * SQ, 0:CH],
                                               in1=bias_rows[:, c * CH:(c + 1) * CH], scale=1.0, scalar=-BIG / 2,
                                               op0=ALU.add, op1=ALU.max, accum_out=max_part[:, r, c:c + 1]) \
                    .then_inc(s_max_used, 1)

            def join_maxima(b):
                dve.wait_ge(s_max_used, MAXES * (b + 1))
                nc.vector.tensor_reduce(max_all[:], max_part[:], AX_X, ALU.max).then_inc(s_max_all, 1)

            def shift_rows(b, q, first=False):
                dve.wait_ge(s_maxT, b + 1)
                nc.vector.tensor_tensor(
                    shift[q][ROW2:ROW2 + HP, :].rearrange("p (r n) -> p r n", r=HP), pair_sel[ROW2:ROW2 + HP],
                    misc[1][ROW2:ROW2 + HP, 0:2 * SQ].unsqueeze(1).to_broadcast([HP, HP, 2 * SQ]), ALU.mult) \
                    .then_inc(s_shift, 1)

            def split_probabilities(b, u, first):
                dve.wait_ge(s_p, UNITS * b + u + 1)
                nc.vector.tensor_tensor(p_lo[u % NP][:], p[u % NP][:], p_hi[u % NP][:], ALU.subtract) \
                    .then_inc(s_p_lo, 1)

            def sum_probabilities(b, q, u):
                acc = acc_v[q][:, u % 2 * HALF:u % 2 * HALF + HALF]
                if u // 2 == DVE_TILES[0]:
                    nc.vector.tensor_copy(acc, p[u % NP][:]).then_inc(s_acc_v, 1)
                else:
                    dve.wait_ge(s_acc_v, sums_done(b, u, True) - 2)
                    nc.vector.tensor_tensor(acc, acc, p[u % NP][:], ALU.add).then_inc(s_acc_v, 1)

            def join_sums(b, q, half):
                if half == 0:
                    dve.wait_ge(s_acc_v, sums_done(b, UNITS - 1, True))
                    dve.wait_ge(s_acc_g, sums_done(b, UNITS - 1, False))
                cs = slice(half * HALF, half * HALF + HALF)
                nc.vector.tensor_tensor(total[:, cs], acc_v[q][:, cs], acc_g[q][:, cs], ALU.add).then_inc(s_total, 1)

            def invert(b, q, last=False):
                if last:
                    dve.wait_ge(s_den, b + 1)
                rows = slice(ROW2 * q, ROW2 * q + SQ)
                nc.vector.reciprocal(inv[rows, :], misc[1][rows, 0:H]).then_inc(s_inv, 1)

            def add_heads(pair, g, last=False):
                rows = x_rows[0:ROWS, bass.ds(pair, 1), :].rearrange("p o n -> p (o n)")
                if last:
                    dve.wait_ge(s_y, H // HEADS_FOLD * pair + g + 1)
                for k in range(HEADS_FOLD):
                    h = HEADS_FOLD * g + k
                    if h == 0:
                        dve.wait_ge(s_inv, 2 * (pair + 1))
                    else:
                        dve.wait_ge(s_y_add, H * pair + h)
                    ins = nc.vector.scalar_tensor_tensor(
                        out=rows if h == H - 1 else y_rows[0:ROWS, :], in0=misc[g % 2][0:ROWS, k * D:(k + 1) * D],
                        scalar=inv[0:ROWS, h:h + 1], in1=y_rows[0:ROWS, :] if h else rows,
                        op0=ALU.mult, op1=ALU.add)
                    ins.then_inc(s_y_add, 1)

            def step(b, q, pair=0, next_pair=0, first=False, last=False):
                n = 1 - q
                for u in range(UNITS):
                    if u == 0 and not last:
                        pick_queries(b + 1, next_pair, n)
                    chunks = MAX_AT[u - 1] if u and not last else []
                    if chunks:
                        dve.wait_ge(s_max, MAXES * (b + 1) + chunks[-1] + 1)
                        dve.sem_inc(s_max_seen, 1)
                    for d in chunks:
                        take_maxima(b + 1, d)
                    split_probabilities(b, u, first)
                    if on_vector(u):
                        sum_probabilities(b, q, u)
                    if not first:
                        if u in (3, 4):
                            join_sums(b - 1, n, u - 3)
                        if u == DEN_AT + 1:
                            invert(b - 1, n)
                        if u - 1 in PROJECT_AT and q == 0:
                            add_heads(pair, PROJECT_AT.index(u - 1))
                    if last:
                        continue
                    if u in (4, 5):
                        split_queries(b + 1, n, u - 4)
                    if u in (10, 12, 13):
                        split_keys(b + 1, n, (10, 12, 13).index(u))
                    if u == UNITS - 1:
                        join_maxima(b + 1)
                        shift_rows(b + 1, n)

            pick_queries(0, 0, 0, first=True)
            for half in range(2):
                split_queries(0, 0, half, first=True)
            for c in range(NCH):
                split_keys(0, 0, c, first=True)
            for d in range(MAXES):
                take_maxima(0, d, first=True)
            join_maxima(0)
            shift_rows(0, 0)
            step(0, 0, next_pair=0, first=True)
            with dve.Fori(0, PAIRS - 1) as i:
                step(2 * i + 1, 1, pair=i, next_pair=i + 1)
                step(2 * i + 2, 0, pair=i, next_pair=i + 1)
            step(B - 1, 1, pair=PAIRS - 1, last=True)
            for half in range(2):
                join_sums(B - 1, 1, half)
            invert(B - 1, 1, last=True)
            for g in range(H // HEADS_FOLD):
                add_heads(PAIRS - 1, g, last=True)

            bank = scores + outT + maxs + misc
            chained = [0]

            def then(ins, *more):
                for x in (ins, *more):
                    chained[0] += 1
                    x.then_inc(s_step, 1)
                dve.wait_ge(s_step, chained[0])

            link = then
            mean_sq, inv_rms = nrm[:, 2, :], nrm[:, 3, :]

            def rmsnorm(sem_):
                for i in range(PAIRS):
                    then(nc.vector.tensor_tensor_reduce(out=junk[:], in0=z[:, i, :], in1=z[:, i, :], scale=1.0,
                                                        scalar=0.0, op0=ALU.mult, op1=ALU.add,
                                                        accum_out=nrm[:, 2, i:i + 1]))
                then(nc.vector.tensor_scalar(mean_sq, mean_sq, 1.0 / D, RMS_EPS, ALU.mult, ALU.add))
                rsqrt2(mean_sq, inv_rms, nrm[:, 0, :])
                for i in range(PAIRS):
                    nc.vector.tensor_scalar(zn[:, i, :], z[:, i, :], nrm[:, 3, i:i + 1], None, ALU.mult).then_inc(sem_, 1)

            def rsqrt2(v, y, a):
                vi, yi, ai = (w.bitcast(I32) for w in (v, y, a))
                then(nc.vector.tensor_scalar(ai, vi, 1, None, ALU.logical_shift_right))
                then(nc.vector.tensor_scalar(yi, ai, -1, RSQRT_SEED, ALU.mult, ALU.add))
                for _ in range(NEWTON_STEPS):
                    then(nc.vector.scalar_tensor_tensor(out=a, in0=y, scalar=-0.5, in1=y, op0=ALU.mult, op1=ALU.mult))
                    then(nc.vector.tensor_tensor(a, a, v, ALU.mult))
                    then(nc.vector.scalar_tensor_tensor(out=y, in0=a, scalar=1.5, in1=y, op0=ALU.add, op1=ALU.mult))

            dve.wait_ge(s_y_add, H * PAIRS)
            for c in range(2):
                then(nc.vector.memset(ao[c][:], 0.0))
            for w in att:
                then(nc.vector.memset(w[:], 0.0))
            then(nc.vector.memset(moeT[:], 0.0))
            then(*[nc.vector.bn_stats(stats[:, i, :], x_rows[:, i, :]) for i in range(PAIRS)])
            then(*[nc.vector.bn_aggr(moments[:, i, :], stats[:, i, :]) for i in range(PAIRS)])
            then(nc.vector.tensor_scalar(var, moments[:, :, 1], LN_EPS, None, ALU.add))
            rsqrt2(var, rstd, nrm[:, 2, :])
            then(*[nc.vector.tensor_scalar(z[:, i, :], x_rows[:, i, :], moments[:, i, 0:1], nrm[:, 1, i:i + 1],
                                           ALU.subtract, ALU.mult) for i in range(PAIRS)])
            rmsnorm(s_zn)

            def take_turned(which, done, sem_):
                for c in range(2):
                    dve.wait_ge(done, c + 1)
                    nc.vector.tensor_scalar(hT[:, 512 * c:512 * c + 512], bank[4 + c][:], ln_w[:, which:which + 1], None,
                                            ALU.mult).then_inc(sem_, 1)

            dve.wait_ge(s_small, 16 * SMALL)
            take_turned(0, s_hT, s_hT_sb)
            rope = 0
            for c in range(2):
                for k, dst in enumerate((qT, kT)):
                    dve.wait_ge(s_qk, 4 * c + 2 * k + 2)
                    for o, table, src in ((turn_a, cos_t, bank[2 * k]), (turn_b, sin_t, bank[2 * k + 1])):
                        if rope:
                            dve.wait_ge(s_rope, rope)
                        nc.vector.tensor_tensor(o[:].rearrange("p (b n) -> p b n", n=ROW2),
                                                src[:].rearrange("p (b n) -> p b n", n=ROW2),
                                                table[:].unsqueeze(1).to_broadcast([D, 8, ROW2]), ALU.mult) \
                            .then_inc(s_rope, 1)
                        rope += 1
                    dve.wait_ge(s_rope, rope)
                    nc.vector.tensor_tensor(dst[:, 512 * c:512 * c + 512], turn_a[:], turn_b[:], ALU.add) \
                        .then_inc(s_rope, 1)
                    rope += 1
            for g in range(B // 4):
                dve.wait_ge(s_v, g + 1)
                nc.vector.tensor_tensor(v_heads[:, 4 * g:4 * g + 4, :],
                                        bank[6 + g % 2][0:2 * SQ, :].rearrange("p (b n) -> p b n", b=4),
                                        v_sel[:].unsqueeze(1).to_broadcast([2 * SQ, 4, D]), ALU.mult).then_inc(s_v_sb, 1)

            def subtract_max(i):
                dve.wait_ge(s_att, i + 1)
                s_ = [bank[2 * (i % 2) + c][0:ROWS, 0:HALF].rearrange("p (h n) -> p h n", h=HP) for c in range(2)]
                then(*[nc.vector.tensor_reduce(att_max[0:ROWS, i, HP * c:HP * c + HP], s_[c], AX_X, ALU.max)
                       for c in range(2)])
                if i >= 3:
                    dve.wait_ge(s_attT, i - 2)
                for c in range(2):
                    ins = nc.vector.tensor_tensor(
                        att[i % 3][0:ROWS, HP * c:HP * c + HP, :], s_[c],
                        att_max[0:ROWS, i, HP * c:HP * c + HP].unsqueeze(2).to_broadcast([ROWS, HP, SQ]), ALU.subtract)
                ins.then_inc(s_att_sub, 1)

            def sum_attention(i):
                dve.wait_ge(s_att_exp, i + 1)
                then(nc.vector.tensor_reduce(att_den[0:ROWS, i, :], att[i % 3][0:ROWS], AX_X, ALU.add))
                then(nc.vector.reciprocal(att_inv[0:ROWS, i, :], att_den[0:ROWS, i, :]))

            def take_ao(i):
                dve.wait_ge(s_ao, i + 1)
                if i >= 2:
                    dve.wait_ge(s_aoT, i - 1)
                nc.vector.tensor_tensor(ao[i % 2][0:ROWS, :].rearrange("p (h d) -> p h d", h=HA),
                                        bank[6][0:ROWS, 0:D].rearrange("p (h d) -> p h d", h=HA),
                                        att_inv[0:ROWS, i, :].unsqueeze(2).to_broadcast([ROWS, HA, DA]), ALU.mult) \
                    .then_inc(s_ao_sb, 1)

            def add_attention(i):
                dve.wait_ge(s_wo, i + 1)
                nc.vector.tensor_tensor(z[0:ROWS, i, :], bank[7][0:ROWS, 128:256], z[0:ROWS, i, :], ALU.add) \
                    .then_inc(s_z, 1)

            for i in range(PAIRS + 3):
                if i < PAIRS:
                    subtract_max(i)
                if 1 <= i <= PAIRS:
                    sum_attention(i - 1)
                if 3 <= i:
                    add_attention(i - 3)
                if 2 <= i <= PAIRS + 1:
                    take_ao(i - 2)

            dve.wait_ge(s_z, PAIRS)
            rmsnorm(s_zn2)
            take_turned(1, s_h2, s_h2_sb)
            for c in range(2):
                dve.wait_ge(s_h_hi, c + 1)
                nc.vector.tensor_tensor(h_lo[:, 512 * c:512 * c + 512], hT[:, 512 * c:512 * c + 512],
                                        h_hi[:, 512 * c:512 * c + 512], ALU.subtract).then_inc(s_h_lo, 1)
            dve.wait_ge(s_logits, 1)
            logits = bank[6][0:ROWS, 0:PAIRS * E].rearrange("p (t e) -> p t e", e=E)
            R = [ROWS, PAIRS, E]
            then(nc.vector.tensor_reduce(gate_max[0:ROWS], logits, AX_X, ALU.max))
            nc.vector.tensor_tensor(gates[0:ROWS], logits, gate_max[0:ROWS].unsqueeze(2).to_broadcast(R),
                                    ALU.subtract).then_inc(s_lmax, 1)
            dve.wait_ge(s_lexp, 1)
            dve.wait_ge(s_mixed, 48)
            R4 = [ROWS, PAIRS, E, E]
            mine = gates[0:ROWS].unsqueeze(3).to_broadcast(R4)
            others = gates[0:ROWS].unsqueeze(2).to_broadcast(R4)
            then(nc.vector.tensor_tensor(above[0:ROWS], others, mine, ALU.is_gt),
                 nc.vector.tensor_tensor(same[0:ROWS], others, mine, ALU.is_equal))
            then(nc.vector.tensor_tensor(same[0:ROWS], same[0:ROWS],
                                         rank_tri[0:ROWS].unsqueeze(1).to_broadcast(R4), ALU.mult))
            then(nc.vector.tensor_tensor(above[0:ROWS], above[0:ROWS], same[0:ROWS], ALU.add))
            then(nc.vector.tensor_reduce(rank[0:ROWS], above[0:ROWS], AX_X, ALU.add))
            then(nc.vector.scalar_tensor_tensor(out=rank[0:ROWS], in0=rank[0:ROWS], scalar=1.5, in1=gates[0:ROWS],
                                                op0=ALU.is_lt, op1=ALU.mult))
            then(nc.vector.tensor_reduce(gate_sum[0:ROWS], rank[0:ROWS], AX_X, ALU.add))
            then(nc.vector.reciprocal(gate_sum[0:ROWS], gate_sum[0:ROWS]))
            nc.vector.tensor_tensor(gates[0:ROWS], rank[0:ROWS], gate_sum[0:ROWS].unsqueeze(2).to_broadcast(R),
                                    ALU.mult).then_inc(s_gates, 1)
            for c in range(2):
                dve.wait_ge(s_gT_hi, c + 1)
                cols = slice(512 * c, 512 * c + 512)
                pick = lambda w: w.rearrange("p (b n) -> p b n", n=128)[:, :, 0:ROWS]
                nc.vector.tensor_tensor(pick(gateT_lo[:, cols]), pick(bank[c][0:E, :]), pick(gateT_hi[:, cols]),
                                        ALU.subtract).then_inc(s_gT_lo, 1)
            for i in range(PAIRS):
                nc.vector.tensor_tensor(z[0:ROWS, i, :], z[0:ROWS, i, :], x_rows[0:ROWS, i, :], ALU.add) \
                    .then_inc(s_res, 1)

            steps = E * 2 * NM
            for n in range(steps + 1):
                if n < steps:
                    dve.wait_ge(s_up, n + 1)
                    dve.wait_ge(s_gc_sb, n // NM + 1)
                    nc.vector.tensor_tensor(up[n % 3][:], bank[2 + n % 2][0:MT, 0:HALF], gate_cols[n // NM % 2][:],
                                            ALU.mult).then_inc(s_upw, 1)
                    dve.wait_ge(s_upw, n + 1)
                    dve.wait_ge(s_silu, n + 1)
                    if n >= 3:
                        dve.wait_ge(s_act_lo, n - 2)
                    nc.vector.tensor_tensor(act_f[n % 3][:], up[n % 3][:], silu[n % 3][:], ALU.mult).then_inc(s_actf, 1)
            for i in range(PAIRS):
                dve.wait_ge(s_moe, i + 1)
                dve.wait_ge(s_res, PAIRS)
                nc.vector.tensor_tensor(z[0:ROWS, i, :], bank[i % 4][0:ROWS, 0:D], z[0:ROWS, i, :], ALU.add) \
                    .then_inc(s_final, 1)

        @block.gpsimd
        def _(pool):
            for q in range(2):
                nc.gpsimd.memset(bias_k[q][0:ROW2, :].bitcast(F32), 0.0).then_inc(s_gset, 1)
                nc.gpsimd.memset(bias_k[q][ROW2:ROW2 + HP, :].bitcast(F32), 1.0).then_inc(s_gset, 1)
            pool.wait_ge(s_gset, GSETS - 2)
            nc.gpsimd.memset(o_pair[:], 0.0).then_inc(s_gset, 1)
            nc.gpsimd.memset(inv[:], 0.0).then_inc(s_gset, 1)

            def split_values(b, q, c):
                pool.wait_ge(s_v_hi, NCH * b + c + 1)
                cs = slice(c * SPLIT_V, (c + 1) * SPLIT_V)
                nc.gpsimd.tensor_tensor(v_lo[q][:, cs], raw_v[:, cs], v_hi[q][:, cs], ALU.subtract).then_inc(s_v_lo, 1)

            def sum_probabilities(b, q, u):
                acc = acc_g[q][:, u % 2 * HALF:u % 2 * HALF + HALF]
                at = sums_done(b, u, False)
                pool.wait_ge(s_p, UNITS * b + u + 1)
                if u // 2 == FIRST_POOL_TILE:
                    nc.gpsimd.tensor_tensor(acc, zeros[:], p[u % NP][:], ALU.add).then_inc(s_acc_g, 1)
                else:
                    pool.wait_ge(s_acc_g, at - 2)
                    nc.gpsimd.tensor_tensor(acc, acc, p[u % NP][:], ALU.add).then_inc(s_acc_g, 1)

            def step(b, q, last=False):
                for u in range(UNITS):
                    if not on_vector(u):
                        sum_probabilities(b, q, u)
                    if u in (9, 11, 13) and not last:
                        split_values(b + 1, 1 - q, (u - 9) // 2)

            for c in range(NCH):
                split_values(0, 0, c)
            pool.wait_ge(s_set, 3)
            step(0, 0)
            with pool.Fori(0, PAIRS - 1) as i:
                step(2 * i + 1, 1)
                step(2 * i + 2, 0)
            step(B - 1, 1, last=True)

            pool.wait_ge(s_rope, 12)
            for b in range(B):
                if b >= 4:
                    pool.wait_ge(s_att, (b - 4) // 2 + 1)
                nc.gpsimd.tensor_tensor(k_heads[b % 4][:],
                                        kT[:, ROW2 * b:ROW2 * b + SQ].unsqueeze(1).to_broadcast([D, HA, SQ]),
                                        head_sel[:].unsqueeze(2).to_broadcast([D, HA, SQ]), ALU.mult).then_inc(s_kh, 1)

            def split_expert(e):
                for k in range(2):
                    pool.wait_ge(s_w_hi, 3 * e + k + 1)
                    nc.gpsimd.tensor_tensor(up_lo[e % 2][:, k, :], up_raw[e % 2][:, k, :], up_hi[e % 2][:, k, :],
                                            ALU.subtract).then_inc(s_w_lo, 1)
                pool.wait_ge(s_w_hi, 3 * e + 3)
                nc.gpsimd.tensor_tensor(down_lo[e % 2][:], down_raw[e % 2][:], down_hi[e % 2][:],
                                        ALU.subtract).then_inc(s_w_lo, 1)

            steps = E * 2 * NM
            split_expert(0)
            split_expert(1)
            for n in range(steps):
                pool.wait_ge(s_act_hi, n + 1)
                if n >= 3:
                    pool.wait_ge(s_down, n - 2)
                nc.gpsimd.tensor_tensor(act_lo[n % 3][:], act_f[n % 3][:], act_hi[n % 3][:], ALU.subtract) \
                    .then_inc(s_act_lo, 1)
                if n % (2 * NM) == 3 and 1 <= n // (2 * NM) < E - 1:
                    split_expert(n // (2 * NM) + 1)


def _constants():
    import numpy as np
    row_sel = np.zeros((ROW2, H, SQ), np.float32)
    row_sel[np.arange(SQ), :, np.arange(SQ)] = 1.0
    pair_sel = np.zeros((HP, HP, 2 * SQ), np.float32)
    pair_sel[np.arange(HP), np.arange(HP)] = -1.0
    place = np.arange(ROW2, dtype=np.float32)[:, None]
    freq = (np.float32(1.0) / np.float32(10000.0) ** (np.arange(0, DA, 2, dtype=np.float32) / np.float32(DA)))
    angle = (place * freq[None, :].astype(np.float32)).astype(np.float32)
    cos = np.tile(np.cos(angle), (1, 2 * HA)).T
    sin = np.tile(np.concatenate([-np.sin(angle), np.sin(angle)], axis=1), (1, HA)).T
    causal = np.where(np.arange(SQ)[None, :] > np.arange(SQ)[:, None], np.float32(-BIG), np.float32(0.0))
    v_sel = np.zeros((2, SQ, HA // 2, 2, DA), np.float32)
    v_sel[0, :, :, 0], v_sel[1, :, :, 1] = 1.0, 1.0
    expert_sel = np.zeros((E, E, 128), np.float32)
    expert_sel[np.arange(E), np.arange(E)] = 1.0
    return {"cos": cos.astype(np.float32), "sin": sin.astype(np.float32),
            "causal": np.tile(causal, (1, HA)).astype(np.float32), "v_sel": v_sel.reshape(2 * SQ, D),
            "head_sel": np.repeat(np.eye(HA, dtype=np.float32), DA, axis=0), "expert_sel": expert_sel,
            "rank_tri": np.broadcast_to(np.tril(np.ones((E, E), np.float32), -1), (128, E, E)).copy(),
            "ident": np.eye(128, dtype=np.float32), "row_sel": row_sel.reshape(ROW2, COLS), "pair_sel": pair_sel}


def kernel(x, ctx_1024, mask_BxSxS2_bf1, L0_xattn_Wq, L0_xattn_Wk, L0_xattn_Wv, L0_xattn_Wo, L0_ffn_ln1_w,
           L0_ffn_ln2_w, L0_ffn_wq, L0_ffn_wk, L0_ffn_wv, L0_ffn_wo, L0_ffn_router_w, L0_ffn_w_gate, L0_ffn_w_up,
           L0_ffn_w_down):
    import numpy as np
    import concourse.bacc as bacc
    from concourse.bass_utils import run_bass_kernel_spmd

    c = np.ascontiguousarray
    ctx = np.asarray(ctx_1024)
    wk = np.asarray(L0_ffn_wk)
    turned = np.arange(D) // DA * DA + (np.arange(D) + DA // 2) % DA
    arrays = {
        "x": c(x),
        "ctxT": c(ctx.transpose(0, 2, 1)),
        "ctx": c(ctx.reshape(B, NT, KT, D).transpose(0, 2, 1, 3)).reshape(B, KT, NT * D),
        "mask": c(mask_BxSxS2_bf1).view(np.uint8),
        "wqT": c(np.asarray(L0_xattn_Wq).transpose(2, 0, 1)),
        "wkT": c(np.asarray(L0_xattn_Wk).transpose(2, 0, 1)),
        "wvT": c(np.asarray(L0_xattn_Wv).transpose(2, 0, 1)),
        "wo": c(np.asarray(L0_xattn_Wo).reshape(H, DH, D).transpose(1, 0, 2)),
        "attn_q": c(L0_ffn_wq),
        "attn_q_turned": c(np.asarray(L0_ffn_wq)[:, turned]),
        "attn_k": c(np.repeat(wk.reshape(D, KV, DA), HA // KV, axis=1).reshape(D, D)),
        "attn_k_turned": c(np.repeat(wk.reshape(D, KV, DA), HA // KV, axis=1).reshape(D, D)[:, turned]),
        "attn_v": c(np.repeat(np.asarray(L0_ffn_wv).reshape(D, KV, DA), HA // KV, axis=1).reshape(D, D)),
        "attn_o": c(L0_ffn_wo),
        "router": c(L0_ffn_router_w),
        "ln_w": c(np.stack([np.asarray(L0_ffn_ln1_w), np.asarray(L0_ffn_ln2_w)], axis=1)),
        "w_up": c(np.stack([np.asarray(L0_ffn_w_gate), np.asarray(L0_ffn_w_up)], axis=2)),
        "w_down": c(np.asarray(L0_ffn_w_down).reshape(E, NM, MT, D).transpose(0, 2, 1, 3)),
        **_constants(),
    }
    nc = bacc.Bacc("TRN2", target_bir_lowering=False, num_devices=1)
    t = {n: nc.dram_tensor(f"in_{n}", a.shape, mybir.dt.from_np(a.dtype), kind="ExternalInput").ap()
         for n, a in arrays.items()}
    out = nc.dram_tensor("out", (B, SQ, D), F32, kind="ExternalOutput").ap()
    xattn_ffn_kernel(nc, t, out)
    r = run_bass_kernel_spmd(nc, [{f"in_{n}": a for n, a in arrays.items()}], core_ids=[0])
    return r.results[0]["out"]
```

```python
from contextlib import ExitStack

import concourse.bass as bass
from concourse import mybir

ALU = mybir.AluOpType
ACT = mybir.ActivationFunctionType
AX_X = mybir.AxisListType.X
F32 = mybir.dt.float32
F32R = mybir.dt.float32r
BF16 = mybir.dt.bfloat16
I32 = mybir.dt.int32
U8 = mybir.dt.uint8

B, SQ, D = 16, 56, 128
SK = 1500
H, DH = 16, 64
KT = 125
NT = SK // KT
HALF = H // 2 * SQ
COLS = H * SQ
UNITS = 2 * NT
KV = 8
SMALL = 12
HA, DA, E, M = 16, 8, 8, 448
MT = 112
NM = M // MT
STEPS = E * 2 * NM
NA, LAG_E = 4, 3
SPLIT_AT = (2, 3, 5)
RMS_EPS = 1e-6
SCALE_A = float(1.0 / DA ** 0.5)
NP = 6
LAG = 3
PAIRS = B // 2
ROW2 = 64
ROWS = ROW2 + SQ
CH = 500
NCH = SK // CH
HP = H // 2
MAXES = HP * NCH
BIG = 2.0 ** 100
SCALE = float(1.0 / SQ ** 0.5)
LN_EPS = 1e-5
SPLIT_V = 512
MAX_COUNT = (0, 0, 0, 0, 0, 2, 2, 2, 2, 2, 1, 2, 1, 1, 2, 1, 2, 1, 1, 2, 0, 0, 0, 0)
MAX_AT = [range(sum(MAX_COUNT[:u]), sum(MAX_COUNT[:u + 1])) for u in range(UNITS)]
RSQRT_SEED, NEWTON_STEPS = 0x5F3759DF, 3
GSETS = 6
FOLD_AT, DEN_AT, PROJECT_AT, TURN_AT = (1, 2), 8, (9, 11, 12, 14, 16, 17, 19, 21), 21
HEADS_FOLD = 4
HEADS_OUT = 2


def xattn_ffn_kernel(nc: bass.Bass, t, out):
    ctx, cross = ExitStack(), ExitStack()
    with ctx:
        def kept(name, shape, dtype=F32):
            return ctx.enter_context(nc.sbuf_tensor(name, shape, dtype))

        def sb(name, shape, dtype=F32):
            return cross.enter_context(nc.sbuf_tensor(name, shape, dtype))

        def sem(name):
            return ctx.enter_context(nc.semaphore(name))

        x_rows = kept("x_rows", [128, PAIRS, D])
        ident = kept("ident", [128, 128])
        stats = kept("stats", [128, PAIRS, 6])
        moments = kept("moments", [128, PAIRS, 2])
        nrm = kept("nrm", [128, 4, PAIRS])
        attn_w = {n: kept(f"attn_{n}", [D, D]) for n in ("q", "q_turned", "k", "k_turned", "v", "o")}
        router = kept("router", [D, E])
        ln_w = kept("ln_w", [D, 2])
        cos_t, sin_t = kept("cos_t", [D, ROW2]), kept("sin_t", [D, ROW2])
        head_sel = kept("head_sel", [D, HA])
        v_sel = kept("v_sel", [2 * SQ, D])
        ones = sb("ones", [128, 128])
        row_sel = sb("row_sel", [ROW2, COLS])
        pair_sel = sb("pair_sel", [ROW2 + HP, HP, 2 * SQ])
        w_left = sb("w_left", [2 * DH, H, D])
        w_right = sb("w_right", [2 * DH, H, D])
        wq, wv, wk, wo = w_left[0:DH], w_left[DH:2 * DH], w_right[0:DH], w_right[DH:2 * DH]
        a_w = sb("a_w", [D, H, D])
        b_w = sb("b_w", [D, H, D])
        xn = sb("xn", [128, PAIRS, D])
        xnT = sb("xnT", [128, PAIRS, D])
        xq = sb("xq", [D, SQ])
        raw_kT = sb("raw_kT", [D, SK])
        raw_v = sb("raw_v", [KT, NT * D])
        raw_mask = sb("raw_mask", [2 * SQ, SK], U8)
        kT_hi = [sb(f"kT_hi{i}", [D, SK], F32R) for i in range(2)]
        kT_lo = [sb(f"kT_lo{i}", [D, SK], F32R) for i in range(2)]
        v_hi = [sb(f"v_hi{i}", [KT, NT * D], F32R) for i in range(2)]
        v_lo = [sb(f"v_lo{i}", [KT, NT * D], F32R) for i in range(2)]
        bias_rows = sb("bias_rows", [2 * SQ, SK], BF16)
        bias_k = [sb(f"bias_k{i}", [ROW2 + HP, SK], F32R) for i in range(2)]
        shift = [sb(f"shift{i}", [ROW2 + HP, COLS], F32R) for i in range(2)]
        q_hi = [sb(f"q_hi{i}", [D, COLS], F32R) for i in range(2)]
        q_lo = [sb(f"q_lo{i}", [D, COLS], F32R) for i in range(2)]
        masked = [sb(f"masked{i}", [2 * SQ, CH], BF16) for i in range(2)]
        max_part = sb("max_part", [2 * SQ, HP, NCH])
        max_all = sb("max_all", [2 * SQ, HP])
        p = [sb(f"p{i}", [KT, HALF]) for i in range(NP)]
        p_hi = [sb(f"p_hi{i}", [KT, HALF], F32R) for i in range(NP)]
        p_lo = [sb(f"p_lo{i}", [KT, HALF], F32R) for i in range(NP)]
        zeros = sb("zeros", [KT, HALF])
        sums = [sb(f"sums{i}", [KT, COLS]) for i in range(2)]
        o_pair = sb("o_pair", [D, H, 128])
        inv = sb("inv", [128, H])
        y_rows = sb("y_rows", [128, D])

        cross.close()

        causal_f = kept("causal_f", [SQ, COLS])
        causal = kept("causal", [SQ, COLS], BF16)
        ident_b = kept("ident_b", [SQ, SQ], BF16)
        rank_tri = kept("rank_tri", [128, E, E])
        expert_sel_f = kept("expert_sel_f", [E, E, 128])
        expert_sel = kept("expert_sel", [E, E, 128], F32R)
        z = kept("z", [128, PAIRS, D])
        zn = kept("zn", [128, PAIRS, D])
        junk = kept("junk", [128, D])
        hT = kept("hT", [D, PAIRS * 128])
        hT_twice = kept("hT_twice", [D, B, 2 * SQ])
        turn_a, turn_b = kept("turn_a", [D, 512]), kept("turn_b", [D, 512])
        qT, kT = kept("qT", [D, PAIRS * 128]), kept("kT", [D, PAIRS * 128])
        v_heads = kept("v_heads", [2 * SQ, B, D])
        k_heads = [kept(f"k_heads{i}", [D, HA, SQ]) for i in range(4)]
        att_max = kept("att_max", [128, PAIRS, HA])
        att_den = kept("att_den", [128, PAIRS, HA])
        att_inv = kept("att_inv", [128, PAIRS, HA])
        att = [kept(f"att{i}", [128, HA, SQ]) for i in range(3)]
        attT = [kept(f"attT{i}", [2 * SQ, HA // 2, ROWS]) for i in range(2)]
        ao = [kept(f"ao{i}", [128, D]) for i in range(2)]
        aoT = [kept(f"aoT{i}", [D, ROWS]) for i in range(2)]
        h_hi, h_lo = kept("h_hi", [D, PAIRS * 128], F32R), kept("h_lo", [D, PAIRS * 128], F32R)
        gates = kept("gates", [128, PAIRS, E])
        gate_max, gate_sum = kept("gate_max", [128, PAIRS]), kept("gate_sum", [128, PAIRS])
        above, same = kept("above", [128, PAIRS, E, E]), kept("same", [128, PAIRS, E, E])
        rank = kept("rank", [128, PAIRS, E])
        gateT_hi, gateT_lo = kept("gateT_hi", [E, PAIRS * 128], F32R), kept("gateT_lo", [E, PAIRS * 128], F32R)
        up_raw = [kept(f"up_raw{i}", [D, 2, M]) for i in range(2)]
        up_hi = [kept(f"up_hi{i}", [D, 2, M], F32R) for i in range(2)]
        up_lo = [kept(f"up_lo{i}", [D, 2, M], F32R) for i in range(2)]
        down_raw = [kept(f"down_raw{i}", [MT, NM, D]) for i in range(2)]
        down_hi = [kept(f"down_hi{i}", [MT, NM, D], F32R) for i in range(2)]
        down_lo = [kept(f"down_lo{i}", [MT, NM, D], F32R) for i in range(2)]
        gate_cols = [kept(f"gate_cols{i}", [MT, HALF]) for i in range(2)]
        silu = [kept(f"silu{i}", [MT, HALF]) for i in range(NA)]
        up = [kept(f"up{i}", [MT, HALF]) for i in range(NA)]
        act_f = [kept(f"act_f{i}", [MT, HALF]) for i in range(NA)]
        act_hi = [kept(f"act_hi{i}", [MT, HALF], F32R) for i in range(NA)]
        act_lo = [kept(f"act_lo{i}", [MT, HALF], F32R) for i in range(NA)]
        moeT = kept("moeT", [D, PAIRS * 128])

        def bank(name):
            return ctx.enter_context(nc.psum_tensor(name, [128, 512], F32))

        scores = [bank(f"scores{i}") for i in range(2)]
        outT = [bank(f"outT{i}") for i in range(2)]
        maxs = [bank(f"maxs{i}") for i in range(2)]
        misc = [bank(f"misc{i}") for i in range(2)]

        s_x = sem("s_x")
        s_wqk, s_wvo, s_const = sem("s_wqk"), sem("s_wvo"), sem("s_const")
        s_set = sem("s_set")
        s_gset = sem("s_gset")
        s_shset = sem("s_shset")
        s_fold = sem("s_fold")
        s_folded = sem("s_folded")
        s_ln = sem("s_ln")
        s_xn = sem("s_xn")
        s_xT, s_xT_used = sem("s_xT"), sem("s_xT_used")
        s_raw_kT, s_raw_v, s_raw_mask = sem("s_raw_kT"), sem("s_raw_v"), sem("s_raw_mask")
        s_kT_hi, s_kT_lo, s_v_hi, s_v_lo = sem("s_kT_hi"), sem("s_kT_lo"), sem("s_v_hi"), sem("s_v_lo")
        s_bias_rows, s_bias_k = sem("s_bias_rows"), sem("s_bias_k")
        s_xq, s_q, s_q_hi, s_q_lo = sem("s_xq"), sem("s_q"), sem("s_q_hi"), sem("s_q_lo")
        s_max, s_max_used, s_max_all = sem("s_max"), sem("s_max_used"), sem("s_max_all")
        s_max_seen = sem("s_max_seen")
        s_maxT, s_shift = sem("s_maxT"), sem("s_shift")
        s_scores, s_p, s_p_lo = sem("s_scores"), sem("s_p"), sem("s_p_lo")
        s_pv = sem("s_pv")
        s_sum = sem("s_sum")
        s_den, s_inv, s_o = sem("s_den"), sem("s_inv"), sem("s_o")
        s_y, s_y_add = sem("s_y"), sem("s_y_add")
        s_out = sem("s_out")
        s_small, s_mixed = sem("s_small"), sem("s_mixed")
        s_cast, s_twice = sem("s_cast"), sem("s_twice")
        s_step = sem("s_step")
        s_zn, s_hT, s_hT_sb = sem("s_zn"), sem("s_hT"), sem("s_hT_sb")
        s_qk, s_rope, s_v, s_v_sb = sem("s_qk"), sem("s_rope"), sem("s_v"), sem("s_v_sb")
        s_kh, s_att, s_att_sub, s_att_exp = sem("s_kh"), sem("s_att"), sem("s_att_sub"), sem("s_att_exp")
        s_attT, s_attT_sb, s_ao, s_ao_sb = sem("s_attT"), sem("s_attT_sb"), sem("s_ao"), sem("s_ao_sb")
        s_aoT, s_aoT_sb, s_wo, s_z = sem("s_aoT"), sem("s_aoT_sb"), sem("s_wo"), sem("s_z")
        s_z2, s_zn2, s_h2, s_h_hi, s_h_lo = sem("s_z2"), sem("s_zn2"), sem("s_h2"), sem("s_h_hi"), sem("s_h_lo")
        s_h2_sb = sem("s_h2_sb")
        s_logits, s_lmax, s_lexp, s_gates = sem("s_logits"), sem("s_lmax"), sem("s_lexp"), sem("s_gates")
        s_gT, s_gT_hi, s_gT_lo = sem("s_gT"), sem("s_gT_hi"), sem("s_gT_lo")
        s_up_raw = [sem(f"s_up_raw{i}") for i in range(2)]
        s_down_raw = [sem(f"s_down_raw{i}") for i in range(2)]
        s_w_hi, s_w_lo = sem("s_w_hi"), sem("s_w_lo")
        s_gc, s_gc_sb = sem("s_gc"), sem("s_gc_sb")
        s_gate, s_up, s_silu, s_upw, s_actf = sem("s_gate"), sem("s_up"), sem("s_silu"), sem("s_upw"), sem("s_actf")
        s_act_hi, s_act_lo, s_down = sem("s_act_hi"), sem("s_act_lo"), sem("s_down")
        s_moeT, s_moe, s_res, s_final = sem("s_moeT"), sem("s_moe"), sem("s_res"), sem("s_final")

        block = ctx.enter_context(nc.Block())

        @block.sync
        def _(sp):
            sp.wait_ge(s_set, 1)
            for half in range(2):
                sp.dma_start(x_rows[ROW2 * half:ROW2 * half + SQ, :, :],
                             t["x"].rearrange("(t two) q d -> two q t d", two=2)[half]).then_inc(s_x, 16)
            for w, name in ((wq, "wqT"), (wk, "wkT")):
                sp.dma_start(w, t[name]).then_inc(s_wqk, 16)
            for c, name in ((ident, "ident"), (row_sel, "row_sel")):
                sp.dma_start(c[:], t[name]).then_inc(s_const, 16)
            sp.dma_start(pair_sel[ROW2:ROW2 + HP], t["pair_sel"]).then_inc(s_const, 16)

            def load(b):
                sp.dma_start(raw_kT[:], t["ctxT"][b]).then_inc(s_raw_kT, 16)
                for half in range(2):
                    sp.dma_start(raw_mask[SQ * half:SQ * half + SQ], t["mask"][b]).then_inc(s_raw_mask, 16)
                sp.dma_start(raw_v[:], t["ctx"][b]).then_inc(s_raw_v, 16)

            load(0)
            for w, name in ((wv, "wvT"), (wo, "wo")):
                sp.dma_start(w, t[name]).then_inc(s_wvo, 16)
            sp.wait_ge(s_bias_k, NCH)
            for n, w in attn_w.items():
                sp.dma_start(w[:], t[f"attn_{n}"]).then_inc(s_small, 16)
            for c, name in ((router, "router"), (ln_w, "ln_w"), (cos_t, "cos"), (sin_t, "sin"),
                            (head_sel, "head_sel"), (v_sel, "v_sel")):
                sp.dma_start(c[:], t[name]).then_inc(s_small, 16)
            with sp.Fori(1, B) as b:
                sp.wait_ge(s_kT_lo, NCH * b)
                sp.dma_start(raw_kT[:], t["ctxT"][bass.ds(b, 1)].rearrange("o p n -> (o p) n")).then_inc(s_raw_kT, 16)
                sp.wait_ge(s_v_lo, NCH * b)
                sp.dma_start(raw_v[:], t["ctx"][bass.ds(b, 1)].rearrange("o p n -> (o p) n")).then_inc(s_raw_v, 16)
                for half in range(2):
                    sp.dma_start(raw_mask[SQ * half:SQ * half + SQ],
                                 t["mask"][bass.ds(b, 1)].rearrange("o p n -> (o p) n")).then_inc(s_raw_mask, 16)
            sp.wait_ge(s_y_add, H * PAIRS)
            for c, name in ((causal_f, "causal"), (rank_tri, "rank_tri"), (expert_sel_f, "expert_sel")):
                sp.dma_start(c[:], t[name]).then_inc(s_mixed, 16)
            for e in range(E):
                if e >= 2:
                    sp.wait_ge(s_w_lo, 3 * (e - 1))
                sp.dma_start(up_raw[e % 2][:], t["w_up"][e]).then_inc(s_up_raw[e % 2], 16)
                sp.dma_start(down_raw[e % 2][:], t["w_down"][e]).then_inc(s_down_raw[e % 2], 16)
            for i in range(PAIRS):
                sp.wait_ge(s_final, i + 1)
                for half in range(2):
                    sp.dma_start(out[2 * i + half], z[ROW2 * half:ROW2 * half + SQ, i, :]).then_inc(s_out, 16)
            sp.wait_ge(s_out, 32 * PAIRS)

        @block.tensor
        def _(pe):
            banks = scores + outT
            for which, (w1, w2, loaded) in enumerate(((wq, wk, s_wqk), (wv, wo, s_wvo))):
                pe.wait_ge(loaded, 32)
                for g, bank_ in enumerate(banks):
                    if which:
                        pe.wait_ge(s_folded, g + 1)
                    for k in range(HEADS_FOLD):
                        mm = nc.tensor.matmul(bank_[:, k * D:(k + 1) * D], w1[:, HEADS_FOLD * g + k, :],
                                              w2[:, HEADS_FOLD * g + k, :], start=True, stop=True)
                    mm.then_inc(s_fold, 1)
                if not which:
                    pe.wait_ge(s_const, 48)
                    for i in range(PAIRS):
                        pe.wait_ge(s_xn, i + 1)
                        mm = nc.tensor.transpose(maxs[i // 4][:, (i % 4) * D:(i % 4) * D + D], xn[:, i, :], ident[:])
                        if i % 4 == 3:
                            mm.then_inc(s_xT, 1)

            def fold_queries(b, half):
                pe.wait_ge(s_xq, b + 1)
                for k in range(HP):
                    mm = nc.tensor.matmul(misc[half][:, k * SQ:(k + 1) * SQ], a_w[:, HP * half + k, :], xq[:],
                                          start=True, stop=True)
                mm.then_inc(s_q, 1)

            def max_scores(b, q, d, first=False):
                c, r = d // HP, d % HP
                if first and r == 0:
                    pe.wait_ge(s_kT_hi, c + 1)
                if d in (0, HP // 2):
                    pe.wait_ge(s_q_hi, 2 * b + 1 + d // (HP // 2))
                if not (first and d < 2):
                    pe.wait_ge(s_max_used, MAXES * b + d - 1)
                nc.tensor.matmul(maxs[d % 2][0:2 * SQ, 0:CH], q_hi[q][:, r * 2 * SQ:(r + 1) * 2 * SQ],
                                 kT_hi[q][:, c * CH:(c + 1) * CH], start=True, stop=True).then_inc(s_max, 1)

            def turn_maxima(b):
                pe.wait_ge(s_max_all, b + 1)
                nc.tensor.matmul(misc[0][ROW2:ROW2 + HP, 0:2 * SQ], max_all[:], ident[0:2 * SQ, 0:2 * SQ],
                                 start=True, stop=True).then_inc(s_maxT, 1)

            def score(b, q, u, first):
                ks, cs, out_ = slice(u // 2 * KT, u // 2 * KT + KT), slice(u % 2 * HALF, u % 2 * HALF + HALF), \
                    scores[u % 2][0:KT, 0:HALF]
                if first and u == 0:
                    pe.wait_ge(s_kT_lo, NCH)
                    pe.wait_ge(s_q_lo, 2)
                    pe.wait_ge(s_bias_k, NCH)
                if not (first and u < 2):
                    pe.wait_ge(s_p, UNITS * b + u - 1)
                nc.tensor.matmul(out_, kT_hi[q][:, ks], q_hi[q][:, cs], start=True, stop=False)
                nc.tensor.matmul(out_, kT_hi[q][:, ks], q_lo[q][:, cs], start=False, stop=False)
                nc.tensor.matmul(out_, kT_lo[q][:, ks], q_hi[q][:, cs], start=False, stop=False)
                if u < 2:
                    pe.wait_ge(s_shift, 2 * b + u + 1)
                nc.tensor.matmul(out_, bias_k[q][:, ks], shift[q][:, cs], start=False, stop=True).then_inc(s_scores, 1)

            def weigh(b, q, u, first):
                j, half = u // 2, u % 2
                vs, out_ = slice(j * D, (j + 1) * D), outT[half][:, 0:HALF]
                if first and u == 0:
                    pe.wait_ge(s_v_lo, NCH)
                if j == 0 and not first:
                    pe.wait_ge(s_o, 2 * b - 1 + half)
                pe.wait_ge(s_p_lo, UNITS * b + u + 1)
                nc.tensor.matmul(out_, v_hi[q][:, vs], p_hi[u % NP][:], start=(j == 0), stop=False)
                nc.tensor.matmul(out_, v_hi[q][:, vs], p_lo[u % NP][:], start=False, stop=False)
                nc.tensor.matmul(out_, v_lo[q][:, vs], p_hi[u % NP][:], start=False, stop=(j == NT - 1)) \
                    .then_inc(s_pv, 1)

            def denominators(b, q):
                pe.wait_ge(s_sum, UNITS * (b + 1))
                for h in range(H):
                    mm = nc.tensor.matmul(misc[1][ROW2 * q:ROW2 * q + SQ, h:h + 1], sums[q][:, h * SQ:(h + 1) * SQ],
                                          ones[0:KT, 0:1], start=True, stop=True)
                mm.then_inc(s_den, 1)

            def project(pair, g):
                if g == 1:
                    pe.wait_ge(s_inv, 2 * pair + 2)
                elif g > 1:
                    pe.wait_ge(s_y_add, H * pair + HEADS_OUT * (g - 1))
                for k in range(HEADS_OUT):
                    h = HEADS_OUT * g + k
                    mm = nc.tensor.matmul(misc[g % 2][0:ROWS, k * D:(k + 1) * D], o_pair[:, h, 0:ROWS], b_w[:, h, :],
                                          start=True, stop=True)
                mm.then_inc(s_y, 1)

            def step(b, q, pair=0, first=False, last=False):
                for u in range(UNITS):
                    score(b, q, u, first)
                    if u >= LAG:
                        weigh(b, q, u - LAG, first)
                    elif not first:
                        weigh(b - 1, 1 - q, UNITS - LAG + u, False)
                    if not last:
                        if u in FOLD_AT:
                            fold_queries(b + 1, FOLD_AT.index(u))
                        for d in MAX_AT[u]:
                            max_scores(b + 1, 1 - q, d)
                    if u == DEN_AT and not first:
                        denominators(b - 1, 1 - q)
                    if u in PROJECT_AT and q == 0 and not first:
                        project(pair, PROJECT_AT.index(u))
                    if u == TURN_AT and not last:
                        turn_maxima(b + 1)

            pe.wait_ge(s_folded, 2 * len(banks))
            pe.wait_ge(s_xT_used, 2)
            fold_queries(0, 0)
            fold_queries(0, 1)
            for d in range(MAXES):
                max_scores(0, 0, d, first=True)
            pe.wait_ge(s_q_lo, 2)
            turn_maxima(0)
            step(0, 0, first=True)
            with pe.Fori(0, PAIRS - 1) as i:
                step(2 * i + 1, 1)
                step(2 * i + 2, 0, pair=i)
            step(B - 1, 1, last=True)
            for u in range(UNITS - LAG, UNITS):
                weigh(B - 1, 1, u, False)
            denominators(B - 1, 1)
            pe.wait_ge(s_o, 2 * B)
            for g in range(H // HEADS_OUT):
                project(PAIRS - 1, g)

            bank = scores + outT + maxs + misc

            def batch(tile, b):
                return tile[:, ROW2 * b:ROW2 * b + SQ]

            def turn_rows(rows, done, sem_, free=None):
                for i in range(PAIRS):
                    pe.wait_ge(done, i + 1)
                    mm = nc.tensor.transpose(bank[4 + i // 4][:, i % 4 * 128:i % 4 * 128 + 128], rows[:, i, :], ident[:])
                    if i % 4 == 3:
                        mm.then_inc(sem_, 1)

            turn_rows(zn, s_zn, s_hT)
            pe.wait_ge(s_small, 16 * SMALL)
            for c in range(2):
                pe.wait_ge(s_hT_sb, c + 1)
                for k, n in enumerate(("q", "q_turned", "k", "k_turned")):
                    if c:
                        pe.wait_ge(s_rope, 3 * (k // 2) + k % 2 + 1)
                    nc.tensor.matmul(bank[k][:], attn_w[n][:], hT[:, 512 * c:512 * c + 512],
                                     start=True, stop=True).then_inc(s_qk, 1)
            pe.wait_ge(s_twice, 2)
            for b in range(B):
                if b % 4 == 0 and b >= 8:
                    pe.wait_ge(s_v_sb, b // 4 - 1)
                mm = nc.tensor.matmul(bank[6 + b // 4 % 2][0:2 * SQ, b % 4 * D:b % 4 * D + D],
                                      hT_twice[:, b, :], attn_w["v"][:],
                                      start=True, stop=True)
                if b % 4 == 3:
                    mm.then_inc(s_v, 1)

            def attend(i):
                if i < 2:
                    pe.wait_ge(s_rope, 12)
                    pe.wait_ge(s_cast, 2)
                else:
                    pe.wait_ge(s_att_sub, i - 1)
                for h in range(2):
                    b = 2 * i + h
                    pe.wait_ge(s_kh, b + 1)
                    for c in range(2):
                        o = bank[2 * (i % 2) + c][ROW2 * h:ROW2 * h + SQ, 0:HALF]
                        nc.tensor.matmul(o, batch(qT, b), k_heads[b % 4][:, HP * c:HP * (c + 1), :],
                                         start=True, stop=False)
                        mm = nc.tensor.matmul(o, ident_b[:], causal[:, c * HALF:(c + 1) * HALF], start=False, stop=True)
                mm.then_inc(s_att, 1)

            def turn_attention(i):
                pe.wait_ge(s_att_exp, i + 1)
                if i:
                    pe.wait_ge(s_attT_sb, 2 * i)
                for hp in range(HA // 2):
                    mm = nc.tensor.transpose(bank[4 + hp // 4][0:2 * SQ, hp % 4 * ROWS:hp % 4 * ROWS + ROWS],
                                             att[i % 3][0:ROWS, 2 * hp:2 * hp + 2, :], ident[0:ROWS, 0:ROWS])
                mm.then_inc(s_attT, 1)

            def weigh_values(i):
                pe.wait_ge(s_attT_sb, 2 * (i + 1))
                pe.wait_ge(s_v_sb, 4)
                if i:
                    pe.wait_ge(s_ao_sb, i)
                for hp in range(HA // 2):
                    for h in range(2):
                        mm = nc.tensor.matmul(bank[6][ROW2 * h:ROW2 * h + SQ, 16 * hp:16 * hp + 16],
                                              attT[i % 2][:, hp, ROW2 * h:ROW2 * h + SQ],
                                              v_heads[:, 2 * i + h, 16 * hp:16 * hp + 16], start=True, stop=True)
                mm.then_inc(s_ao, 1)

            def turn_output(i):
                pe.wait_ge(s_ao_sb, i + 1)
                if i:
                    pe.wait_ge(s_z, i)
                nc.tensor.transpose(bank[7][:, 0:ROWS], ao[i % 2][0:ROWS, :], ident[0:ROWS, 0:ROWS]).then_inc(s_aoT, 1)

            def project_output(i):
                pe.wait_ge(s_aoT_sb, i + 1)
                nc.tensor.matmul(bank[7][0:ROWS, 128:256], aoT[i % 2][:], attn_w["o"][:], start=True, stop=True) \
                    .then_inc(s_wo, 1)

            for i in range(PAIRS + 3):
                if i < PAIRS:
                    attend(i)
                if 1 <= i <= PAIRS:
                    turn_attention(i - 1)
                if 3 <= i:
                    project_output(i - 3)
                if 2 <= i <= PAIRS + 1:
                    weigh_values(i - 2)
                    turn_output(i - 2)

            turn_rows(zn, s_zn2, s_h2)
            for i in range(PAIRS):
                pe.wait_ge(s_h2_sb, i // 4 + 1)
                mm = nc.tensor.matmul(bank[6][0:ROWS, E * i:E * i + E], hT[:, 128 * i:128 * i + ROWS], router[:],
                                      start=True, stop=True)
            mm.then_inc(s_logits, 1)
            pe.wait_ge(s_gates, 1)
            for i in range(PAIRS):
                mm = nc.tensor.transpose(bank[i // 4][0:E, i % 4 * 128:i % 4 * 128 + ROWS], gates[0:ROWS, i, :],
                                         ident[0:ROWS, 0:ROWS])
                if i % 4 == 3:
                    mm.then_inc(s_gT, 1)

            def columns(tile, half):
                return tile[:, half * 512:half * 512 + 512].rearrange("p (b n) -> p b n", n=ROW2)[:, :, 0:SQ]

            def spread_gates(e, half):
                pe.wait_ge(s_gT_lo, 2)
                if 2 * e + half >= 1:
                    pe.wait_ge(s_gc_sb, 2 * e + half)
                nc.tensor.matmul(bank[6][0:MT, 0:HALF], expert_sel[:, e, 0:MT], columns(gateT_hi, half),
                                 start=True, stop=False)
                nc.tensor.matmul(bank[6][0:MT, 0:HALF], expert_sel[:, e, 0:MT], columns(gateT_lo, half),
                                 start=False, stop=True).then_inc(s_gc, 1)

            def hidden(n):
                e, half, m = n // (2 * NM), n // NM % 2, n % NM
                ms = slice(MT * m, MT * m + MT)
                if n % (2 * NM) == 0:
                    pe.wait_ge(s_w_lo, 3 * e + 2)
                    pe.wait_ge(s_h_lo, 2)
                if n % NM == 0:
                    spread_gates(e, half)
                for k, (sem_, used) in enumerate(((s_gate, s_silu), (s_up, s_upw))):
                    if n >= 2:
                        pe.wait_ge(used, n - 1)
                    elif n == 0:
                        pe.wait_ge(s_gT_hi, 2)
                    o = bank[2 * k + n % 2][0:MT, 0:HALF]
                    nc.tensor.matmul(o, up_hi[e % 2][:, k, ms], columns(h_hi, half), start=True, stop=False)
                    nc.tensor.matmul(o, up_hi[e % 2][:, k, ms], columns(h_lo, half), start=False, stop=False)
                    nc.tensor.matmul(o, up_lo[e % 2][:, k, ms], columns(h_hi, half), start=False, stop=True) \
                        .then_inc(sem_, 1)

            def down(n):
                e, half, m = n // (2 * NM), n // NM % 2, n % NM
                pe.wait_ge(s_w_lo, 3 * (e + 1))
                pe.wait_ge(s_act_lo, n + 1)
                o = bank[4 + half][:, 0:HALF]
                first, last = e == 0 and m == 0, e == E - 1 and m == NM - 1
                nc.tensor.matmul(o, down_hi[e % 2][:, m, :], act_hi[n % NA][:], start=first, stop=False)
                nc.tensor.matmul(o, down_hi[e % 2][:, m, :], act_lo[n % NA][:], start=False, stop=False)
                nc.tensor.matmul(o, down_lo[e % 2][:, m, :], act_hi[n % NA][:], start=False, stop=last) \
                    .then_inc(s_down, 1)

            for n in range(STEPS + LAG_E):
                if n < STEPS:
                    hidden(n)
                if n >= LAG_E:
                    down(n - LAG_E)

            for i in range(PAIRS):
                pe.wait_ge(s_moeT, i // 4 + 1)
                if i >= 4:
                    pe.wait_ge(s_final, i - 3)
                nc.tensor.transpose(bank[i % 4][0:ROWS, 0:D], moeT[:, 128 * i:128 * i + ROWS], ident[:]) \
                    .then_inc(s_moe, 1)

        @block.scalar
        def _(act):
            banks = scores + outT
            for which, w in enumerate((a_w, b_w)):
                for g, bank_ in enumerate(banks):
                    act.wait_ge(s_fold, len(banks) * which + g + 1)
                    nc.scalar.copy(w[:, HEADS_FOLD * g:HEADS_FOLD * (g + 1), :], bank_[:]).then_inc(s_folded, 1)

            def split_keys(b, q, c):
                if c == 0:
                    act.wait_ge(s_raw_kT, 16 * (b + 1))
                nc.scalar.copy(kT_hi[q][:, c * CH:(c + 1) * CH], raw_kT[:, c * CH:(c + 1) * CH]).then_inc(s_kT_hi, 1)

            def split_values(b, q, c):
                if c == 0:
                    act.wait_ge(s_raw_v, 16 * (b + 1))
                nc.scalar.copy(v_hi[q][:, c * SPLIT_V:(c + 1) * SPLIT_V], raw_v[:, c * SPLIT_V:(c + 1) * SPLIT_V]) \
                    .then_inc(s_v_hi, 1)

            def mask_rows(b, c):
                if c == 0:
                    act.wait_ge(s_raw_mask, 32 * (b + 1))
                nc.scalar.activation(bias_rows[:, c * CH:(c + 1) * CH], raw_mask[:, c * CH:(c + 1) * CH], ACT.Copy,
                                     bias=-BIG, scale=BIG).then_inc(s_bias_rows, 1)

            def mask_keys(b, q, c, first=False):
                if first and c == 0:
                    act.wait_ge(s_gset, GSETS)
                nc.scalar.activation(bias_k[q][0:SQ, c * CH:(c + 1) * CH], raw_mask[0:SQ, c * CH:(c + 1) * CH],
                                     ACT.Copy, bias=-BIG, scale=BIG).then_inc(s_bias_k, 1)

            def take_queries(b, q, half, first=False):
                if first:
                    act.wait_ge(s_q, 2 * b + half + 1)
                nc.scalar.copy(q_hi[q][:, half * HALF:(half + 1) * HALF], misc[half][:, 0:HALF]).then_inc(s_q_hi, 1)

            def exponentials(b, u, first):
                act.wait_ge(s_scores, UNITS * b + u + 1)
                nc.scalar.activation(p_hi[u % NP][:], scores[u % 2][0:KT, 0:HALF], ACT.Exp, scale=SCALE)
                if not (first and u < NP):
                    act.wait_ge(s_sum, UNITS * b + u - NP + 1)
                nc.scalar.activation(p[u % NP][:], scores[u % 2][0:KT, 0:HALF], ACT.Exp, scale=SCALE).then_inc(s_p, 1)

            def take_output(b, q, half):
                act.wait_ge(s_pv, UNITS * b + UNITS - 1 + half)
                nc.scalar.copy(o_pair[:, HP * half:HP * (half + 1), ROW2 * q:ROW2 * q + SQ],
                               outT[half][:, 0:HALF].rearrange("p (h n) -> p h n", h=HP)).then_inc(s_o, 1)

            def step(b, q, first=False, last=False):
                n = 1 - q
                for u in range(UNITS):
                    exponentials(b, u, first)
                    if u in (LAG - 2, LAG - 1) and not first:
                        take_output(b - 1, n, u - LAG + 2)
                    if last:
                        continue
                    if u in (0, 5, 7):
                        split_keys(b + 1, n, (0, 5, 7).index(u))
                    if u in (3, 4):
                        take_queries(b + 1, n, u - 3)
                    if u in (0, 6, 8):
                        mask_rows(b + 1, (0, 6, 8).index(u))
                    if u in (9, 10, 11):
                        mask_keys(b + 1, n, u - 9)
                    if u in (13, 15, 17):
                        split_values(b + 1, n, (u - 13) // 2)

            for c in range(NCH):
                split_keys(0, 0, c)
            for half in range(2):
                take_queries(0, 0, half, first=True)
            for c in range(NCH):
                mask_rows(0, c)
            for c in range(NCH):
                mask_keys(0, 0, c, first=True)
            for c in range(NCH):
                split_values(0, 0, c)
            step(0, 0, first=True)
            with act.Fori(0, PAIRS - 1) as i:
                step(2 * i + 1, 1)
                step(2 * i + 2, 0)
            step(B - 1, 1, last=True)
            for half in range(2):
                take_output(B - 1, 1, half)

            bank = scores + outT + maxs + misc
            act.wait_ge(s_mixed, 48)
            nc.scalar.copy(causal[:], causal_f[:]).then_inc(s_cast, 1)
            nc.scalar.copy(ident_b[:], ident[0:SQ, 0:SQ]).then_inc(s_cast, 1)
            nc.scalar.copy(expert_sel[:], expert_sel_f[:]).then_inc(s_cast, 1)

            act.wait_ge(s_hT_sb, 2)
            for c in range(2):
                nc.scalar.copy(hT_twice[:, :, SQ * c:SQ * c + SQ],
                               hT[:].rearrange("p (b n) -> p b n", n=ROW2)[:, :, 0:SQ]).then_inc(s_twice, 1)

            def exponentials_a(i):
                act.wait_ge(s_att_sub, i + 1)
                nc.scalar.activation(att[i % 3][0:ROWS], att[i % 3][0:ROWS], ACT.Exp, scale=SCALE_A).then_inc(s_att_exp, 1)

            def take_attT(i):
                act.wait_ge(s_attT, i + 1)
                if i >= 2:
                    act.wait_ge(s_ao, i - 1)
                for c in range(2):
                    nc.scalar.copy(attT[i % 2][:, 4 * c:4 * c + 4, :],
                                   bank[4 + c][0:2 * SQ, 0:4 * ROWS].rearrange("p (h n) -> p h n", h=4)) \
                        .then_inc(s_attT_sb, 1)

            def take_aoT(i):
                act.wait_ge(s_aoT, i + 1)
                if i >= 2:
                    act.wait_ge(s_wo, i - 1)
                nc.scalar.copy(aoT[i % 2][:], bank[7][:, 0:ROWS]).then_inc(s_aoT_sb, 1)

            for i in range(PAIRS + 3):
                if i < PAIRS:
                    exponentials_a(i)
                if 1 <= i <= PAIRS:
                    take_attT(i - 1)
                if 2 <= i <= PAIRS + 1:
                    take_aoT(i - 2)

            for c in range(2):
                act.wait_ge(s_h2_sb, c + 1)
                nc.scalar.copy(h_hi[:, 512 * c:512 * c + 512], hT[:, 512 * c:512 * c + 512]).then_inc(s_h_hi, 1)
            act.wait_ge(s_lmax, 1)
            nc.scalar.activation(gates[0:ROWS], gates[0:ROWS], ACT.Exp).then_inc(s_lexp, 1)
            for c in range(2):
                act.wait_ge(s_gT, c + 1)
                nc.scalar.copy(gateT_hi[:, 512 * c:512 * c + 512].rearrange("p (b n) -> p b n", n=128)[:, :, 0:ROWS],
                               bank[c][0:E, :].rearrange("p (b n) -> p b n", n=128)[:, :, 0:ROWS]).then_inc(s_gT_hi, 1)

            def split_expert(e, k):
                act.wait_ge((s_up_raw, s_up_raw, s_down_raw)[k][e % 2], 16 * (e // 2 + 1))
                if e >= 2:
                    act.wait_ge(s_down if k == 2 else s_up, 2 * NM * (e - 1))
                if k < 2:
                    nc.scalar.copy(up_hi[e % 2][:, k, :], up_raw[e % 2][:, k, :]).then_inc(s_w_hi, 1)
                else:
                    nc.scalar.copy(down_hi[e % 2][:], down_raw[e % 2][:]).then_inc(s_w_hi, 1)

            def take_gates(e, half):
                n = 2 * e + half
                act.wait_ge(s_gc, n + 1)
                if n >= 2:
                    act.wait_ge(s_upw, NM * (n - 1))
                nc.scalar.copy(gate_cols[n % 2][:], bank[6][0:MT, 0:HALF]).then_inc(s_gc_sb, 1)

            def silu_of(n):
                act.wait_ge(s_gate, n + 1)
                if n >= NA:
                    act.wait_ge(s_actf, n - NA + 1)
                nc.scalar.activation(silu[n % NA][:], bank[n % 2][0:MT, 0:HALF], ACT.Silu).then_inc(s_silu, 1)

            def high(n):
                act.wait_ge(s_actf, n + 1)
                if n >= NA:
                    act.wait_ge(s_down, n - NA + 1)
                nc.scalar.copy(act_hi[n % NA][:], act_f[n % NA][:]).then_inc(s_act_hi, 1)

            for k in range(3):
                split_expert(0, k)
            for n in range(STEPS + 1):
                if n < STEPS:
                    if n % NM == 0:
                        take_gates(n // (2 * NM), n // NM % 2)
                    silu_of(n)
                if n >= 1:
                    high(n - 1)
                if n % (2 * NM) in SPLIT_AT and n // (2 * NM) < E - 1:
                    split_expert(n // (2 * NM) + 1, SPLIT_AT.index(n % (2 * NM)))
            for c in range(2):
                act.wait_ge(s_down, STEPS - (1 - c) * NM)
                nc.scalar.copy(moeT[:, 512 * c:512 * c + 512].rearrange("p (b n) -> p b n", n=ROW2)[:, :, 0:SQ],
                               bank[4 + c][:, 0:HALF].rearrange("p (b n) -> p b n", n=SQ)).then_inc(s_moeT, 1)

        @block.vector
        def _(dve):
            nc.vector.memset(x_rows[:], 0.0).then_inc(s_set, 1)
            nc.vector.memset(ones[:], 1.0).then_inc(s_set, 1)
            nc.vector.memset(zeros[:], 0.0).then_inc(s_set, 1)
            chain = [0]

            def link(ins):
                chain[0] += 1
                ins.then_inc(s_ln, 1)
                dve.wait_ge(s_ln, chain[0])

            def rsqrt(v, y, a):
                vi, yi, ai = (z.bitcast(I32) for z in (v, y, a))
                link(nc.vector.tensor_scalar(ai, vi, 1, None, ALU.logical_shift_right))
                link(nc.vector.tensor_scalar(yi, ai, -1, RSQRT_SEED, ALU.mult, ALU.add))
                for _ in range(NEWTON_STEPS):
                    link(nc.vector.scalar_tensor_tensor(out=a, in0=y, scalar=-0.5, in1=y, op0=ALU.mult, op1=ALU.mult))
                    link(nc.vector.tensor_tensor(a, a, v, ALU.mult))
                    link(nc.vector.scalar_tensor_tensor(out=y, in0=a, scalar=1.5, in1=y, op0=ALU.add, op1=ALU.mult))

            dve.wait_ge(s_x, 32)
            for i in range(PAIRS):
                last = nc.vector.bn_stats(stats[:, i, :], x_rows[:, i, :])
            link(last)
            for i in range(PAIRS):
                last = nc.vector.bn_aggr(moments[:, i, :], stats[:, i, :])
            link(last)
            var, rstd = nrm[:, 0, :], nrm[:, 1, :]
            link(nc.vector.tensor_scalar(var, moments[:, :, 1], LN_EPS, None, ALU.add))
            rsqrt(var, rstd, nrm[:, 2, :])
            for i in range(PAIRS):
                nc.vector.tensor_scalar(xn[:, i, :], x_rows[:, i, :], moments[:, i, 0:1], nrm[:, 1, i:i + 1],
                                        ALU.subtract, ALU.mult).then_inc(s_xn, 1)
            for half in range(2):
                dve.wait_ge(s_xT, half + 1)
                nc.vector.tensor_copy(xnT[:, 4 * half:4 * half + 4, :], maxs[half][:]).then_inc(s_xT_used, 1)
            dve.wait_ge(s_const, 48)
            for q in range(2):
                nc.vector.tensor_copy(shift[q][0:ROW2, :], row_sel[:]).then_inc(s_shset, 1)

            def pick_queries(b, pair, half, first=False):
                if first:
                    dve.wait_ge(s_xT_used, 2)
                nc.vector.tensor_copy(xq[:], xnT[:, bass.ds(pair, 1), ROW2 * half:ROW2 * half + SQ]
                                      .rearrange("p o n -> p (o n)")).then_inc(s_xq, 1)

            def split_queries(b, q, half, first=False):
                if first:
                    dve.wait_ge(s_q_hi, half + 1)
                nc.vector.tensor_tensor(q_lo[q][:, half * HALF:(half + 1) * HALF], misc[half][:, 0:HALF],
                                        q_hi[q][:, half * HALF:(half + 1) * HALF], ALU.subtract).then_inc(s_q_lo, 1)

            def take_maxima(b, d, first=False):
                c, r = d // HP, d % HP
                if first:
                    dve.wait_ge(s_max, d + 1)
                    dve.wait_ge(s_bias_rows, NCH)
                    if d > 1:
                        dve.wait_ge(s_max_used, d - 1)
                nc.vector.tensor_tensor_reduce(out=masked[d % 2][:], in0=maxs[d % 2][0:2 * SQ, 0:CH],
                                               in1=bias_rows[:, c * CH:(c + 1) * CH], scale=1.0, scalar=-BIG / 2,
                                               op0=ALU.add, op1=ALU.max, accum_out=max_part[:, r, c:c + 1]) \
                    .then_inc(s_max_used, 1)

            def join_maxima(b):
                dve.wait_ge(s_max_used, MAXES * (b + 1))
                nc.vector.tensor_reduce(max_all[:], max_part[:], AX_X, ALU.max).then_inc(s_max_all, 1)

            def shift_rows(b, q):
                dve.wait_ge(s_maxT, b + 1)
                for half in range(2):
                    nc.vector.tensor_tensor(
                        shift[q][ROW2:ROW2 + HP, half * HALF:half * HALF + HALF].rearrange("p (r n) -> p r n", n=2 * SQ),
                        pair_sel[ROW2:ROW2 + HP, HP // 2 * half:HP // 2 * (half + 1)],
                        misc[0][ROW2:ROW2 + HP, 0:2 * SQ].unsqueeze(1).to_broadcast([HP, HP // 2, 2 * SQ]), ALU.mult) \
                        .then_inc(s_shift, 1)

            def split_probabilities(b, u, first):
                dve.wait_ge(s_p, UNITS * b + u + 1)
                nc.vector.tensor_tensor(p_lo[u % NP][:], p[u % NP][:], p_hi[u % NP][:], ALU.subtract) \
                    .then_inc(s_p_lo, 1)

            def invert(b, q, last=False):
                if last:
                    dve.wait_ge(s_den, b + 1)
                rows = slice(ROW2 * q, ROW2 * q + SQ)
                nc.vector.reciprocal(inv[rows, :], misc[1][rows, 0:H]).then_inc(s_inv, 1)

            def add_heads(pair, g, last=False):
                rows = x_rows[0:ROWS, bass.ds(pair, 1), :].rearrange("p o n -> p (o n)")
                if last:
                    dve.wait_ge(s_y, H // HEADS_OUT * pair + g + 1)
                for k in range(HEADS_OUT):
                    h = HEADS_OUT * g + k
                    if h == 0:
                        dve.wait_ge(s_inv, 2 * (pair + 1))
                    else:
                        dve.wait_ge(s_y_add, H * pair + h)
                    ins = nc.vector.scalar_tensor_tensor(
                        out=rows if h == H - 1 else y_rows[0:ROWS, :], in0=misc[g % 2][0:ROWS, k * D:(k + 1) * D],
                        scalar=inv[0:ROWS, h:h + 1], in1=y_rows[0:ROWS, :] if h else rows,
                        op0=ALU.mult, op1=ALU.add)
                    ins.then_inc(s_y_add, 1)

            def step(b, q, pair=0, next_pair=0, first=False, last=False):
                n = 1 - q
                for u in range(UNITS):
                    if u == 0 and not last:
                        pick_queries(b + 1, next_pair, n)
                    split_probabilities(b, u, first)
                    if MAX_AT[u] and not last:
                        dve.wait_ge(s_max, MAXES * (b + 1) + MAX_AT[u][-1] + 1)
                        dve.sem_inc(s_max_seen, 1)
                        for d in MAX_AT[u]:
                            take_maxima(b + 1, d)
                    if u == TURN_AT + 1 and not last:
                        shift_rows(b + 1, n)
                    if not first:
                        if u == DEN_AT + 1:
                            invert(b - 1, n)
                        if u - 1 in PROJECT_AT and q == 0:
                            add_heads(pair, PROJECT_AT.index(u - 1))
                    if last:
                        continue
                    if u in (4, 5):
                        split_queries(b + 1, n, u - 4)
                    if u == TURN_AT - 1:
                        join_maxima(b + 1)

            pick_queries(0, 0, 0, first=True)
            for half in range(2):
                split_queries(0, 0, half, first=True)
            for d in range(MAXES):
                take_maxima(0, d, first=True)
            join_maxima(0)
            shift_rows(0, 0)
            step(0, 0, next_pair=0, first=True)
            with dve.Fori(0, PAIRS - 1) as i:
                step(2 * i + 1, 1, pair=i, next_pair=i + 1)
                step(2 * i + 2, 0, pair=i, next_pair=i + 1)
            step(B - 1, 1, pair=PAIRS - 1, last=True)
            invert(B - 1, 1, last=True)
            for g in range(H // HEADS_OUT):
                add_heads(PAIRS - 1, g, last=True)

            bank = scores + outT + maxs + misc
            chained = [0]

            def then(ins, *more):
                for x in (ins, *more):
                    chained[0] += 1
                    x.then_inc(s_step, 1)
                dve.wait_ge(s_step, chained[0])

            link = then
            mean_sq, inv_rms = nrm[:, 2, :], nrm[:, 3, :]

            def rmsnorm(sem_):
                for i in range(PAIRS):
                    then(nc.vector.tensor_tensor_reduce(out=junk[:], in0=z[:, i, :], in1=z[:, i, :], scale=1.0,
                                                        scalar=0.0, op0=ALU.mult, op1=ALU.add,
                                                        accum_out=nrm[:, 2, i:i + 1]))
                then(nc.vector.tensor_scalar(mean_sq, mean_sq, 1.0 / D, RMS_EPS, ALU.mult, ALU.add))
                rsqrt2(mean_sq, inv_rms, nrm[:, 0, :])
                for i in range(PAIRS):
                    nc.vector.tensor_scalar(zn[:, i, :], z[:, i, :], nrm[:, 3, i:i + 1], None, ALU.mult).then_inc(sem_, 1)

            def rsqrt2(v, y, a):
                vi, yi, ai = (w.bitcast(I32) for w in (v, y, a))
                then(nc.vector.tensor_scalar(ai, vi, 1, None, ALU.logical_shift_right))
                then(nc.vector.tensor_scalar(yi, ai, -1, RSQRT_SEED, ALU.mult, ALU.add))
                for _ in range(NEWTON_STEPS):
                    then(nc.vector.scalar_tensor_tensor(out=a, in0=y, scalar=-0.5, in1=y, op0=ALU.mult, op1=ALU.mult))
                    then(nc.vector.tensor_tensor(a, a, v, ALU.mult))
                    then(nc.vector.scalar_tensor_tensor(out=y, in0=a, scalar=1.5, in1=y, op0=ALU.add, op1=ALU.mult))

            dve.wait_ge(s_y_add, H * PAIRS)
            for c in range(2):
                then(nc.vector.memset(ao[c][:], 0.0))
            for w in att:
                then(nc.vector.memset(w[:], 0.0))
            then(nc.vector.memset(moeT[:], 0.0))
            then(*[nc.vector.bn_stats(stats[:, i, :], x_rows[:, i, :]) for i in range(PAIRS)])
            then(*[nc.vector.bn_aggr(moments[:, i, :], stats[:, i, :]) for i in range(PAIRS)])
            then(nc.vector.tensor_scalar(var, moments[:, :, 1], LN_EPS, None, ALU.add))
            rsqrt2(var, rstd, nrm[:, 2, :])
            then(*[nc.vector.tensor_scalar(z[:, i, :], x_rows[:, i, :], moments[:, i, 0:1], nrm[:, 1, i:i + 1],
                                           ALU.subtract, ALU.mult) for i in range(PAIRS)])
            rmsnorm(s_zn)

            def take_turned(which, done, sem_):
                for c in range(2):
                    dve.wait_ge(done, c + 1)
                    nc.vector.tensor_scalar(hT[:, 512 * c:512 * c + 512], bank[4 + c][:], ln_w[:, which:which + 1], None,
                                            ALU.mult).then_inc(sem_, 1)

            dve.wait_ge(s_small, 16 * SMALL)
            take_turned(0, s_hT, s_hT_sb)
            rope = 0
            for c in range(2):
                for k, dst in enumerate((qT, kT)):
                    dve.wait_ge(s_qk, 4 * c + 2 * k + 2)
                    for o, table, src in ((turn_a, cos_t, bank[2 * k]), (turn_b, sin_t, bank[2 * k + 1])):
                        if rope:
                            dve.wait_ge(s_rope, rope)
                        nc.vector.tensor_tensor(o[:].rearrange("p (b n) -> p b n", n=ROW2),
                                                src[:].rearrange("p (b n) -> p b n", n=ROW2),
                                                table[:].unsqueeze(1).to_broadcast([D, 8, ROW2]), ALU.mult) \
                            .then_inc(s_rope, 1)
                        rope += 1
                    dve.wait_ge(s_rope, rope)
                    nc.vector.tensor_tensor(dst[:, 512 * c:512 * c + 512], turn_a[:], turn_b[:], ALU.add) \
                        .then_inc(s_rope, 1)
                    rope += 1
            for g in range(B // 4):
                dve.wait_ge(s_v, g + 1)
                nc.vector.tensor_tensor(v_heads[:, 4 * g:4 * g + 4, :],
                                        bank[6 + g % 2][0:2 * SQ, :].rearrange("p (b n) -> p b n", b=4),
                                        v_sel[:].unsqueeze(1).to_broadcast([2 * SQ, 4, D]), ALU.mult).then_inc(s_v_sb, 1)

            def subtract_max(i):
                dve.wait_ge(s_att, i + 1)
                s_ = [bank[2 * (i % 2) + c][0:ROWS, 0:HALF].rearrange("p (h n) -> p h n", h=HP) for c in range(2)]
                then(*[nc.vector.tensor_reduce(att_max[0:ROWS, i, HP * c:HP * c + HP], s_[c], AX_X, ALU.max)
                       for c in range(2)])
                if i >= 3:
                    dve.wait_ge(s_attT, i - 2)
                for c in range(2):
                    ins = nc.vector.tensor_tensor(
                        att[i % 3][0:ROWS, HP * c:HP * c + HP, :], s_[c],
                        att_max[0:ROWS, i, HP * c:HP * c + HP].unsqueeze(2).to_broadcast([ROWS, HP, SQ]), ALU.subtract)
                ins.then_inc(s_att_sub, 1)

            def sum_attention(i):
                dve.wait_ge(s_att_exp, i + 1)
                then(nc.vector.tensor_reduce(att_den[0:ROWS, i, :], att[i % 3][0:ROWS], AX_X, ALU.add))
                then(nc.vector.reciprocal(att_inv[0:ROWS, i, :], att_den[0:ROWS, i, :]))

            def take_ao(i):
                dve.wait_ge(s_ao, i + 1)
                if i >= 2:
                    dve.wait_ge(s_aoT, i - 1)
                nc.vector.tensor_tensor(ao[i % 2][0:ROWS, :].rearrange("p (h d) -> p h d", h=HA),
                                        bank[6][0:ROWS, 0:D].rearrange("p (h d) -> p h d", h=HA),
                                        att_inv[0:ROWS, i, :].unsqueeze(2).to_broadcast([ROWS, HA, DA]), ALU.mult) \
                    .then_inc(s_ao_sb, 1)

            def add_attention(i):
                dve.wait_ge(s_wo, i + 1)
                nc.vector.tensor_tensor(z[0:ROWS, i, :], bank[7][0:ROWS, 128:256], z[0:ROWS, i, :], ALU.add) \
                    .then_inc(s_z, 1)

            for i in range(PAIRS + 3):
                if i < PAIRS:
                    subtract_max(i)
                if 1 <= i <= PAIRS:
                    sum_attention(i - 1)
                if 3 <= i:
                    add_attention(i - 3)
                if 2 <= i <= PAIRS + 1:
                    take_ao(i - 2)

            dve.wait_ge(s_z, PAIRS)
            rmsnorm(s_zn2)
            take_turned(1, s_h2, s_h2_sb)
            for c in range(2):
                dve.wait_ge(s_h_hi, c + 1)
                nc.vector.tensor_tensor(h_lo[:, 512 * c:512 * c + 512], hT[:, 512 * c:512 * c + 512],
                                        h_hi[:, 512 * c:512 * c + 512], ALU.subtract).then_inc(s_h_lo, 1)
            dve.wait_ge(s_logits, 1)
            logits = bank[6][0:ROWS, 0:PAIRS * E].rearrange("p (t e) -> p t e", e=E)
            R = [ROWS, PAIRS, E]
            then(nc.vector.tensor_reduce(gate_max[0:ROWS], logits, AX_X, ALU.max))
            nc.vector.tensor_tensor(gates[0:ROWS], logits, gate_max[0:ROWS].unsqueeze(2).to_broadcast(R),
                                    ALU.subtract).then_inc(s_lmax, 1)
            dve.wait_ge(s_lexp, 1)
            dve.wait_ge(s_mixed, 48)
            R4 = [ROWS, PAIRS, E, E]
            mine = gates[0:ROWS].unsqueeze(3).to_broadcast(R4)
            others = gates[0:ROWS].unsqueeze(2).to_broadcast(R4)
            then(nc.vector.tensor_tensor(above[0:ROWS], others, mine, ALU.is_gt),
                 nc.vector.tensor_tensor(same[0:ROWS], others, mine, ALU.is_equal))
            then(nc.vector.tensor_tensor(same[0:ROWS], same[0:ROWS],
                                         rank_tri[0:ROWS].unsqueeze(1).to_broadcast(R4), ALU.mult))
            then(nc.vector.tensor_tensor(above[0:ROWS], above[0:ROWS], same[0:ROWS], ALU.add))
            then(nc.vector.tensor_reduce(rank[0:ROWS], above[0:ROWS], AX_X, ALU.add))
            then(nc.vector.scalar_tensor_tensor(out=rank[0:ROWS], in0=rank[0:ROWS], scalar=1.5, in1=gates[0:ROWS],
                                                op0=ALU.is_lt, op1=ALU.mult))
            then(nc.vector.tensor_reduce(gate_sum[0:ROWS], rank[0:ROWS], AX_X, ALU.add))
            then(nc.vector.reciprocal(gate_sum[0:ROWS], gate_sum[0:ROWS]))
            nc.vector.tensor_tensor(gates[0:ROWS], rank[0:ROWS], gate_sum[0:ROWS].unsqueeze(2).to_broadcast(R),
                                    ALU.mult).then_inc(s_gates, 1)
            for c in range(2):
                dve.wait_ge(s_gT_hi, c + 1)
                cols = slice(512 * c, 512 * c + 512)
                pick = lambda w: w.rearrange("p (b n) -> p b n", n=128)[:, :, 0:ROWS]
                nc.vector.tensor_tensor(pick(gateT_lo[:, cols]), pick(bank[c][0:E, :]), pick(gateT_hi[:, cols]),
                                        ALU.subtract).then_inc(s_gT_lo, 1)
            for i in range(PAIRS):
                nc.vector.tensor_tensor(z[0:ROWS, i, :], z[0:ROWS, i, :], x_rows[0:ROWS, i, :], ALU.add) \
                    .then_inc(s_res, 1)

            def split_expert(e, k):
                dve.wait_ge(s_w_hi, 3 * e + k + 1)
                if k < 2:
                    nc.vector.tensor_tensor(up_lo[e % 2][:, k, :], up_raw[e % 2][:, k, :], up_hi[e % 2][:, k, :],
                                            ALU.subtract).then_inc(s_w_lo, 1)
                else:
                    nc.vector.tensor_tensor(down_lo[e % 2][:], down_raw[e % 2][:], down_hi[e % 2][:],
                                            ALU.subtract).then_inc(s_w_lo, 1)

            for k in range(3):
                split_expert(0, k)
            for n in range(STEPS):
                if n < STEPS:
                    dve.wait_ge(s_up, n + 1)
                    dve.wait_ge(s_gc_sb, n // NM + 1)
                    nc.vector.tensor_tensor(up[n % NA][:], bank[2 + n % 2][0:MT, 0:HALF], gate_cols[n // NM % 2][:],
                                            ALU.mult).then_inc(s_upw, 1)
                    dve.wait_ge(s_upw, n + 1)
                    dve.wait_ge(s_silu, n + 1)
                    if n >= NA:
                        dve.wait_ge(s_act_lo, n - NA + 1)
                    nc.vector.tensor_tensor(act_f[n % NA][:], up[n % NA][:], silu[n % NA][:], ALU.mult).then_inc(s_actf, 1)
                    if n % (2 * NM) in SPLIT_AT and n // (2 * NM) < E - 1:
                        split_expert(n // (2 * NM) + 1, SPLIT_AT.index(n % (2 * NM)))
            for i in range(PAIRS):
                dve.wait_ge(s_moe, i + 1)
                dve.wait_ge(s_res, PAIRS)
                nc.vector.tensor_tensor(z[0:ROWS, i, :], bank[i % 4][0:ROWS, 0:D], z[0:ROWS, i, :], ALU.add) \
                    .then_inc(s_final, 1)

        @block.gpsimd
        def _(pool):
            for q in range(2):
                nc.gpsimd.memset(bias_k[q][0:ROW2, :].bitcast(F32), 0.0).then_inc(s_gset, 1)
                nc.gpsimd.memset(bias_k[q][ROW2:ROW2 + HP, :].bitcast(F32), 1.0).then_inc(s_gset, 1)
            pool.wait_ge(s_gset, GSETS - 2)
            nc.gpsimd.memset(o_pair[:], 0.0).then_inc(s_gset, 1)
            nc.gpsimd.memset(inv[:], 0.0).then_inc(s_gset, 1)

            def split_values(b, q, c):
                pool.wait_ge(s_v_hi, NCH * b + c + 1)
                cs = slice(c * SPLIT_V, (c + 1) * SPLIT_V)
                nc.gpsimd.tensor_tensor(v_lo[q][:, cs], raw_v[:, cs], v_hi[q][:, cs], ALU.subtract).then_inc(s_v_lo, 1)

            def split_keys(b, q, c):
                pool.wait_ge(s_kT_hi, NCH * b + c + 1)
                nc.gpsimd.tensor_tensor(kT_lo[q][:, c * CH:(c + 1) * CH], raw_kT[:, c * CH:(c + 1) * CH],
                                        kT_hi[q][:, c * CH:(c + 1) * CH], ALU.subtract).then_inc(s_kT_lo, 1)

            def sum_probabilities(b, q, u):
                acc = sums[q][:, u % 2 * HALF:u % 2 * HALF + HALF]
                pool.wait_ge(s_p, UNITS * b + u + 1)
                if u < 2:
                    nc.gpsimd.tensor_tensor(acc, zeros[:], p[u % NP][:], ALU.add).then_inc(s_sum, 1)
                else:
                    pool.wait_ge(s_sum, UNITS * b + u - 1)
                    nc.gpsimd.tensor_tensor(acc, acc, p[u % NP][:], ALU.add).then_inc(s_sum, 1)

            def step(b, q, last=False):
                for u in range(UNITS):
                    sum_probabilities(b, q, u)
                    if u in (7, 9, 11) and not last:
                        split_keys(b + 1, 1 - q, (u - 7) // 2)
                    if u in (14, 16, 18) and not last:
                        split_values(b + 1, 1 - q, (u - 14) // 2)

            for c in range(NCH):
                split_keys(0, 0, c)
            for c in range(NCH):
                split_values(0, 0, c)
            pool.wait_ge(s_set, 3)
            step(0, 0)
            with pool.Fori(0, PAIRS - 1) as i:
                step(2 * i + 1, 1)
                step(2 * i + 2, 0)
            step(B - 1, 1, last=True)

            pool.wait_ge(s_rope, 12)
            for b in range(B):
                if b >= 4:
                    pool.wait_ge(s_att, (b - 4) // 2 + 1)
                nc.gpsimd.tensor_tensor(k_heads[b % 4][:],
                                        kT[:, ROW2 * b:ROW2 * b + SQ].unsqueeze(1).to_broadcast([D, HA, SQ]),
                                        head_sel[:].unsqueeze(2).to_broadcast([D, HA, SQ]), ALU.mult).then_inc(s_kh, 1)

            for n in range(STEPS):
                pool.wait_ge(s_act_hi, n + 1)
                if n >= NA:
                    pool.wait_ge(s_down, n - NA + 1)
                nc.gpsimd.tensor_tensor(act_lo[n % NA][:], act_f[n % NA][:], act_hi[n % NA][:], ALU.subtract) \
                    .then_inc(s_act_lo, 1)


def _constants():
    import numpy as np
    row_sel = np.zeros((ROW2, H, SQ), np.float32)
    row_sel[np.arange(SQ), :, np.arange(SQ)] = 1.0
    pair_sel = np.zeros((HP, HP, 2 * SQ), np.float32)
    pair_sel[np.arange(HP), np.arange(HP)] = -1.0
    place = np.arange(ROW2, dtype=np.float32)[:, None]
    freq = (np.float32(1.0) / np.float32(10000.0) ** (np.arange(0, DA, 2, dtype=np.float32) / np.float32(DA)))
    angle = (place * freq[None, :].astype(np.float32)).astype(np.float32)
    cos = np.tile(np.cos(angle), (1, 2 * HA)).T
    sin = np.tile(np.concatenate([-np.sin(angle), np.sin(angle)], axis=1), (1, HA)).T
    causal = np.where(np.arange(SQ)[None, :] > np.arange(SQ)[:, None], np.float32(-BIG), np.float32(0.0))
    v_sel = np.zeros((2, SQ, HA // 2, 2, DA), np.float32)
    v_sel[0, :, :, 0], v_sel[1, :, :, 1] = 1.0, 1.0
    expert_sel = np.zeros((E, E, 128), np.float32)
    expert_sel[np.arange(E), np.arange(E)] = 1.0
    return {"cos": cos.astype(np.float32), "sin": sin.astype(np.float32),
            "causal": np.tile(causal, (1, HA)).astype(np.float32), "v_sel": v_sel.reshape(2 * SQ, D),
            "head_sel": np.repeat(np.eye(HA, dtype=np.float32), DA, axis=0), "expert_sel": expert_sel,
            "rank_tri": np.broadcast_to(np.tril(np.ones((E, E), np.float32), -1), (128, E, E)).copy(),
            "ident": np.eye(128, dtype=np.float32), "row_sel": row_sel.reshape(ROW2, COLS), "pair_sel": pair_sel}


def kernel(x, ctx_1024, mask_BxSxS2_bf1, L0_xattn_Wq, L0_xattn_Wk, L0_xattn_Wv, L0_xattn_Wo, L0_ffn_ln1_w,
           L0_ffn_ln2_w, L0_ffn_wq, L0_ffn_wk, L0_ffn_wv, L0_ffn_wo, L0_ffn_router_w, L0_ffn_w_gate, L0_ffn_w_up,
           L0_ffn_w_down):
    import numpy as np
    import concourse.bacc as bacc
    from concourse.bass_utils import run_bass_kernel_spmd

    c = np.ascontiguousarray
    ctx = np.asarray(ctx_1024)
    wk = np.asarray(L0_ffn_wk)
    turned = np.arange(D) // DA * DA + (np.arange(D) + DA // 2) % DA
    arrays = {
        "x": c(x),
        "ctxT": c(ctx.transpose(0, 2, 1)),
        "ctx": c(ctx.reshape(B, NT, KT, D).transpose(0, 2, 1, 3)).reshape(B, KT, NT * D),
        "mask": c(mask_BxSxS2_bf1).view(np.uint8),
        "wqT": c(np.asarray(L0_xattn_Wq).transpose(2, 0, 1)),
        "wkT": c(np.asarray(L0_xattn_Wk).transpose(2, 0, 1)),
        "wvT": c(np.asarray(L0_xattn_Wv).transpose(2, 0, 1)),
        "wo": c(np.asarray(L0_xattn_Wo).reshape(H, DH, D).transpose(1, 0, 2)),
        "attn_q": c(L0_ffn_wq),
        "attn_q_turned": c(np.asarray(L0_ffn_wq)[:, turned]),
        "attn_k": c(np.repeat(wk.reshape(D, KV, DA), HA // KV, axis=1).reshape(D, D)),
        "attn_k_turned": c(np.repeat(wk.reshape(D, KV, DA), HA // KV, axis=1).reshape(D, D)[:, turned]),
        "attn_v": c(np.repeat(np.asarray(L0_ffn_wv).reshape(D, KV, DA), HA // KV, axis=1).reshape(D, D)),
        "attn_o": c(L0_ffn_wo),
        "router": c(L0_ffn_router_w),
        "ln_w": c(np.stack([np.asarray(L0_ffn_ln1_w), np.asarray(L0_ffn_ln2_w)], axis=1)),
        "w_up": c(np.stack([np.asarray(L0_ffn_w_gate), np.asarray(L0_ffn_w_up)], axis=2)),
        "w_down": c(np.asarray(L0_ffn_w_down).reshape(E, NM, MT, D).transpose(0, 2, 1, 3)),
        **_constants(),
    }
    nc = bacc.Bacc("TRN2", target_bir_lowering=False, num_devices=1)
    t = {n: nc.dram_tensor(f"in_{n}", a.shape, mybir.dt.from_np(a.dtype), kind="ExternalInput").ap()
         for n, a in arrays.items()}
    out = nc.dram_tensor("out", (B, SQ, D), F32, kind="ExternalOutput").ap()
    xattn_ffn_kernel(nc, t, out)
    r = run_bass_kernel_spmd(nc, [{f"in_{n}": a for n, a in arrays.items()}], core_ids=[0])
    return r.results[0]["out"]
```

```python
from contextlib import ExitStack

import concourse.bass as bass
from concourse import mybir

ALU = mybir.AluOpType
ACT = mybir.ActivationFunctionType
AX_X = mybir.AxisListType.X
F32 = mybir.dt.float32
F32R = mybir.dt.float32r
BF16 = mybir.dt.bfloat16
I32 = mybir.dt.int32
U8 = mybir.dt.uint8

B, SQ, D = 16, 56, 128
SK = 1500
H, DH = 16, 64
KT = 125
NT = SK // KT
HALF = H // 2 * SQ
COLS = H * SQ
UNITS = 2 * NT
SUMS = UNITS - 2
KV = 8
SMALL = 12
HA, DA, E, M = 16, 8, 8, 448
DUOS, WIDE = E // 2, 2 * M
MT = 128
NM = WIDE // MT
STEPS = DUOS * 2 * NM
SPREAD_AT = (0, M // MT, M // MT + 1)
SPREADS = len(SPREAD_AT)
LOW = 32
WEIGHTS_AT = (4, 5, 6)
NA, LAG_E = 5, 4
AW = 2 * (2 * DA + 2)
EARLY = 4
SPLIT_AT = (3, 6, 9)
RMS_EPS = 1e-6
SCALE_A = float(1.0 / DA ** 0.5)
NP = 6
LAG = 4
PAIRS = B // 2
ROW2 = 64
ROWS = ROW2 + SQ
CH = 500
NCH = SK // CH
HP = H // 2
MAXES = HP * NCH
BIG = 2.0 ** 100
SCALE = float(1.0 / SQ ** 0.5)
LN_EPS = 1e-5
SPLIT_V = 512
MAX_COUNT = ((0, 0, 0, 0, 1, 1, 2, 2, 2, 2, 1, 2, 1, 1, 2, 1, 2, 1, 1, 2, 0, 0, 0, 0),
             (0, 0, 0, 0, 0, 1, 2, 1, 2, 2, 1, 2, 1, 2, 2, 1, 2, 1, 2, 2, 0, 0, 0, 0))
MAX_AT = [[range(sum(c[:u]), sum(c[:u + 1])) for u in range(UNITS)] for c in MAX_COUNT]
RSQRT_SEED, NEWTON_STEPS = 0x5F3759DF, 3
GSETS = 6
FOLD_AT, DEN_AT, PROJECT_AT, TURN_AT = (1, 2, 3, 4), 8, (9, 11, 12, 14, 16, 17, 19, 21), 21
TURN_ROWS_AT, QK_AT = 17, (19, 20, 21, 22)
QK_BANKS = (5, 6, 7, 4)
HEADS_FOLD = 4
HEADS_OUT = 2


def xattn_ffn_kernel(nc: bass.Bass, t, out):
    ctx, cross, attention = ExitStack(), ExitStack(), ExitStack()
    with ctx:
        def kept(name, shape, dtype=F32):
            return ctx.enter_context(nc.sbuf_tensor(name, shape, dtype))

        def sb(name, shape, dtype=F32):
            return cross.enter_context(nc.sbuf_tensor(name, shape, dtype))

        def own(name, shape, dtype=F32):
            return attention.enter_context(nc.sbuf_tensor(name, shape, dtype))

        def sem(name):
            return ctx.enter_context(nc.semaphore(name))

        x_rows = kept("x_rows", [128, PAIRS, D])
        ident = kept("ident", [128, 128])
        stats = kept("stats", [128, PAIRS, 6])
        moments = kept("moments", [128, PAIRS, 2])
        nrm = kept("nrm", [128, 4, PAIRS])
        attn_w = {n: kept(f"attn_{n}", [D, D]) for n in ("q", "q_turned", "k", "k_turned", "v", "o")}
        router = kept("router", [D, E])
        ln_w = kept("ln_w", [D, 2])
        cos_t, sin_t = kept("cos_t", [D, ROW2]), kept("sin_t", [D, ROW2])
        head_sel = kept("head_sel", [D, HA])
        v_sel = kept("v_sel", [2 * SQ, D])
        w_left = sb("w_left", [2 * DH, H, D])
        w_right = sb("w_right", [2 * DH, H, D])
        wq, wv, wk, wo = w_left[0:DH], w_left[DH:2 * DH], w_right[0:DH], w_right[DH:2 * DH]
        a_w = sb("a_w", [D, H, D])
        row_sel = sb("row_sel", [ROW2, COLS])
        pair_sel = sb("pair_sel", [ROW2 + HP, HP, 2 * SQ])
        xn = sb("xn", [128, PAIRS, D])
        xnT = sb("xnT", [128, PAIRS, D])
        xq = sb("xq", [D, ROWS])
        q_next = sb("q_next", [D, COLS])
        raw_kT = sb("raw_kT", [D, SK])
        raw_v = sb("raw_v", [KT, NT * D])
        raw_mask = sb("raw_mask", [2 * SQ, SK], U8)
        bias_rows = sb("bias_rows", [2 * SQ, SK], BF16)
        masked = [sb(f"masked{i}", [2 * SQ, CH], BF16) for i in range(2)]
        max_part = sb("max_part", [2 * SQ, HP, NCH])
        max_all = sb("max_all", [2 * SQ, HP])

        def by_batch(i):
            return (sb(f"kT_hi{i}", [D, SK], F32R), sb(f"kT_lo{i}", [D, SK], F32R),
                    sb(f"bias_k{i}", [ROW2 + HP, SK], F32R),
                    sb(f"shift{i}", [ROW2 + HP, COLS], F32R), sb(f"q_hi{i}", [D, COLS], F32R),
                    sb(f"q_lo{i}", [D, COLS], F32R), sb(f"v_hi{i}", [KT, NT * D], F32R), sb(f"v_lo{i}", [KT, NT * D], F32R))

        kT_hi, kT_lo, bias_k, shift, q_hi, q_lo, v_hi, v_lo = zip(by_batch(0), by_batch(1))
        ones = sb("ones", [128, 128])
        b_w = sb("b_w", [D, H, D])
        p = [sb(f"p{i}", [KT, HALF]) for i in range(NP)]
        p_hi = [sb(f"p_hi{i}", [KT, HALF], F32R) for i in range(NP)]
        p_lo = [sb(f"p_lo{i}", [KT, HALF], F32R) for i in range(NP)]
        sums = [sb(f"sums{i}", [KT, COLS]) for i in range(2)]
        o_pair = sb("o_pair", [D, H, 128])
        inv = sb("inv", [128, H])
        y_rows = sb("y_rows", [128, D])

        cross.close()

        z = kept("z", [128, PAIRS, D])
        zn = kept("zn", [128, PAIRS, D])
        hT = kept("hT", [D, PAIRS * 128])
        rank_tri = kept("rank_tri", [128, E, E])
        up_raw = kept("up_raw", [D, 2, WIDE])
        down_raw = kept("down_raw", [MT, NM, D])
        expert_sel_f = kept("expert_sel_f", [LOW + E, DUOS, SPREADS, MT])

        hT_twice = own("hT_twice", [D, B, 2 * SQ])
        turn_a, turn_b = own("turn_a", [D, 512]), own("turn_b", [D, 512])
        qT, kT = own("qT", [D, PAIRS * 128]), own("kT", [D, PAIRS * 128])
        causal_f = own("causal_f", [SQ, COLS])
        causal = own("causal", [SQ, COLS], BF16)
        ident_b = own("ident_b", [SQ, ROWS], BF16)
        v_heads = own("v_heads", [2 * SQ, B, HA // 2, 2 * DA + 2])
        k_heads = [own(f"k_heads{i}", [D, HA, SQ]) for i in range(4)]
        att_max = own("att_max", [128, PAIRS, HA])
        att_inv = own("att_inv", [128, PAIRS, HA])
        ao = [own(f"ao{i}", [128, D]) for i in range(2)]
        aoT = [own(f"aoT{i}", [D, ROWS]) for i in range(2)]
        att = [own(f"att{i}", [128, HA, SQ]) for i in range(3)]
        attT = [own(f"attT{i}", [2 * SQ, HA // 2, ROWS]) for i in range(2)]
        attention.close()

        h_hi, h_lo = kept("h_hi", [D, PAIRS * 128], F32R), kept("h_lo", [D, PAIRS * 128], F32R)
        gates = kept("gates", [128, PAIRS, E])
        gate_max, gate_sum = kept("gate_max", [128, PAIRS]), kept("gate_sum", [128, PAIRS])
        above, same = kept("above", [128, PAIRS, E, E]), kept("same", [128, PAIRS, E, E])
        rank = kept("rank", [128, PAIRS, E])
        gateT = kept("gateT", [LOW + E, PAIRS * 128], F32R)
        gate_cols = [kept(f"gate_cols{i}", [MT, HALF]) for i in range(2)]
        silu = [kept(f"silu{i}", [MT, HALF]) for i in range(NA)]
        act_raw = [kept(f"act_raw{i}", [MT, HALF]) for i in range(NA)]
        act_f = [kept(f"act_f{i}", [MT, HALF]) for i in range(NA)]
        act_hi = [kept(f"act_hi{i}", [MT, HALF], F32R) for i in range(NA)]
        act_lo = [kept(f"act_lo{i}", [MT, HALF], F32R) for i in range(NA)]
        moeT = kept("moeT", [D, PAIRS * 128])
        expert_sel = kept("expert_sel", [LOW + E, DUOS, SPREADS, MT], F32R)
        up_hi = [kept(f"up_hi{i}", [D, 2, WIDE], F32R) for i in range(2)]
        up_lo = [kept(f"up_lo{i}", [D, 2, WIDE], F32R) for i in range(2)]
        down_hi = [kept(f"down_hi{i}", [MT, NM, D], F32R) for i in range(2)]
        down_lo = [kept(f"down_lo{i}", [MT, NM, D], F32R) for i in range(2)]

        def bank(name):
            return ctx.enter_context(nc.psum_tensor(name, [128, 512], F32))

        scores = [bank(f"scores{i}") for i in range(2)]
        outT = [bank(f"outT{i}") for i in range(2)]
        maxs = [bank(f"maxs{i}") for i in range(2)]
        misc = [bank(f"misc{i}") for i in range(2)]

        s_x = sem("s_x")
        s_wqk, s_wvo, s_const = sem("s_wqk"), sem("s_wvo"), sem("s_const")
        s_set = sem("s_set")
        s_step = sem("s_step")
        s_v_ones = sem("s_v_ones")
        s_clear = sem("s_clear")
        s_square = sem("s_square")
        s_gset = sem("s_gset")
        s_shset = sem("s_shset")
        s_fold = sem("s_fold")
        s_folded = sem("s_folded")
        s_xn = sem("s_xn")
        s_xT, s_xT_used = sem("s_xT"), sem("s_xT_used")
        s_raw_kT, s_raw_v, s_raw_mask = sem("s_raw_kT"), sem("s_raw_v"), sem("s_raw_mask")
        s_kT_hi, s_kT_lo, s_v_hi, s_v_lo = sem("s_kT_hi"), sem("s_kT_lo"), sem("s_v_hi"), sem("s_v_lo")
        s_bias_rows, s_bias_k = sem("s_bias_rows"), sem("s_bias_k")
        s_xq, s_q, s_q_hi, s_q_lo = sem("s_xq"), sem("s_q"), sem("s_q_hi"), sem("s_q_lo")
        s_q_next = sem("s_q_next")
        s_max, s_max_used, s_max_all = sem("s_max"), sem("s_max_used"), sem("s_max_all")
        s_max_seen = sem("s_max_seen")
        s_maxT, s_shift = sem("s_maxT"), sem("s_shift")
        s_scores, s_p, s_p_lo = sem("s_scores"), sem("s_p"), sem("s_p_lo")
        s_pv = sem("s_pv")
        s_sum = sem("s_sum")
        s_den, s_inv, s_o = sem("s_den"), sem("s_inv"), sem("s_o")
        s_y, s_y_add = sem("s_y"), sem("s_y_add")
        s_out = sem("s_out")
        s_small, s_mixed = sem("s_small"), sem("s_mixed")
        s_cast, s_twice = sem("s_cast"), sem("s_twice")
        s_zn, s_hT, s_hT_sb = sem("s_zn"), sem("s_hT"), sem("s_hT_sb")
        s_qk, s_rope, s_v, s_v_sb = sem("s_qk"), sem("s_rope"), sem("s_v"), sem("s_v_sb")
        s_kh, s_att, s_att_sub, s_att_exp = sem("s_kh"), sem("s_att"), sem("s_att_sub"), sem("s_att_exp")
        s_attT, s_attT_sb, s_ao, s_ao_sb = sem("s_attT"), sem("s_attT_sb"), sem("s_ao"), sem("s_ao_sb")
        s_aoT, s_aoT_sb, s_wo, s_z = sem("s_aoT"), sem("s_aoT_sb"), sem("s_wo"), sem("s_z")
        s_zn2, s_h2, s_h_hi, s_h_lo = sem("s_zn2"), sem("s_h2"), sem("s_h_hi"), sem("s_h_lo")
        s_h2_sb = sem("s_h2_sb")
        s_logits, s_lmax, s_lexp, s_gates = sem("s_logits"), sem("s_lmax"), sem("s_lexp"), sem("s_gates")
        s_gT, s_gT_hi, s_gT_lo = sem("s_gT"), sem("s_gT_hi"), sem("s_gT_lo")
        s_up_raw, s_down_raw, s_sel = sem("s_up_raw"), sem("s_down_raw"), sem("s_sel")
        s_w_hi, s_w_lo, s_w_lo_first = sem("s_w_hi"), sem("s_w_lo"), sem("s_w_lo_first")
        s_gc, s_gc_sb = sem("s_gc"), sem("s_gc_sb")
        s_gate, s_up, s_silu = sem("s_gate"), sem("s_up"), sem("s_silu")
        s_act_raw, s_actf = sem("s_act_raw"), sem("s_actf")
        s_act_hi, s_act_lo, s_down = sem("s_act_hi"), sem("s_act_lo"), sem("s_down")
        s_moe_set, s_gT_set = sem("s_moe_set"), sem("s_gT_set")
        s_moeT, s_moe, s_res, s_final = sem("s_moeT"), sem("s_moe"), sem("s_res"), sem("s_final")

        def out_banks(i):
            return (6, 7, 7) if i < PAIRS - 1 else (0, 2, 3)

        def spread_of(n):
            return n // NM * SPREADS + sum(n % NM >= m for m in SPREAD_AT) - 1

        def low_parts(e, k):
            return (s_w_lo_first, k) if e == 0 else (s_w_lo, 3 * (e - 1) + k)

        block = ctx.enter_context(nc.Block())

        @block.sync
        def _(sp):
            sp.wait_ge(s_set, 1)
            for half in range(2):
                sp.dma_start(x_rows[ROW2 * half:ROW2 * half + SQ, :, :],
                             t["x"].rearrange("(t two) q d -> two q t d", two=2)[half]).then_inc(s_x, 16)
            for w, name in ((wq, "wqT"), (wk, "wkT")):
                sp.dma_start(w, t[name]).then_inc(s_wqk, 16)
            for c, name in ((ident, "ident"), (row_sel, "row_sel")):
                sp.dma_start(c[:], t[name]).then_inc(s_const, 16)
            sp.dma_start(pair_sel[ROW2:ROW2 + HP], t["pair_sel"]).then_inc(s_const, 16)

            def load(b):
                sp.dma_start(raw_kT[:], t["ctxT"][b]).then_inc(s_raw_kT, 16)
                for half in range(2):
                    sp.dma_start(raw_mask[SQ * half:SQ * half + SQ], t["mask"][b]).then_inc(s_raw_mask, 16)
                sp.dma_start(raw_v[:], t["ctx"][b]).then_inc(s_raw_v, 16)

            load(0)
            for w, name in ((wv, "wvT"), (wo, "wo")):
                sp.dma_start(w, t[name]).then_inc(s_wvo, 16)
            sp.wait_ge(s_bias_k, NCH)
            for n, w in attn_w.items():
                sp.dma_start(w[:], t[f"attn_{n}"]).then_inc(s_small, 16)
            for c, name in ((router, "router"), (ln_w, "ln_w"), (cos_t, "cos"), (sin_t, "sin"),
                            (head_sel, "head_sel"), (v_sel, "v_sel")):
                sp.dma_start(c[:], t[name]).then_inc(s_small, 16)
            with sp.Fori(1, B) as b:
                sp.wait_ge(s_kT_lo, NCH * b)
                sp.dma_start(raw_kT[:], t["ctxT"][bass.ds(b, 1)].rearrange("o p n -> (o p) n")).then_inc(s_raw_kT, 16)
                sp.wait_ge(s_v_lo, NCH * b)
                sp.dma_start(raw_v[:], t["ctx"][bass.ds(b, 1)].rearrange("o p n -> (o p) n")).then_inc(s_raw_v, 16)
                for half in range(2):
                    sp.dma_start(raw_mask[SQ * half:SQ * half + SQ],
                                 t["mask"][bass.ds(b, 1)].rearrange("o p n -> (o p) n")).then_inc(s_raw_mask, 16)
            sp.wait_ge(s_o, 2 * B - 2)
            for c, name in ((causal_f, "causal"), (rank_tri, "rank_tri"), (expert_sel_f, "expert_sel")):
                sp.dma_start(c[:], t[name]).then_inc(s_mixed, 16)
            for e in range(DUOS):
                if e:
                    sp.wait_ge(*low_parts(e - 1, 3))
                sp.dma_start(up_raw[:], t["w_up"][e]).then_inc(s_up_raw, 16)
                sp.dma_start(down_raw[:], t["w_down"][e]).then_inc(s_down_raw, 16)
            for c in range(2):
                sp.wait_ge(s_final, c + 1)
                for half in range(2):
                    sp.dma_start(out.rearrange("(t two) q d -> two q t d", two=2)[half][:, 4 * c:4 * c + 4],
                                 z[ROW2 * half:ROW2 * half + SQ, 4 * c:4 * c + 4, :]).then_inc(s_out, 16)
            sp.wait_ge(s_out, 64)

        @block.tensor
        def _(pe):
            banks = scores + outT

            def fold_weights(which, g):
                w1, w2, loaded = ((wq, wk, s_wqk), (wv, wo, s_wvo))[which]
                pe.wait_ge(loaded, 32)
                if which:
                    pe.wait_ge(s_folded, g + 1)
                for k in range(HEADS_FOLD):
                    mm = nc.tensor.matmul(banks[g][:, k * D:(k + 1) * D], w1[:, HEADS_FOLD * g + k, :],
                                          w2[:, HEADS_FOLD * g + k, :], start=True, stop=True)
                mm.then_inc(s_fold, 1)

            def fold_queries(pair, g):
                if g == 0:
                    pe.wait_ge(s_xq, pair + 1)
                elif g > 1:
                    pe.wait_ge(s_q_lo, 6 * pair + g - 1)
                for k in range(HEADS_FOLD):
                    mm = nc.tensor.matmul(misc[g % 2][:, k * ROWS:(k + 1) * ROWS], a_w[:, HEADS_FOLD * g + k, :], xq[:],
                                          start=True, stop=True)
                mm.then_inc(s_q, 1)

            def max_scores(b, q, d, first=False):
                c, r = d // HP, d % HP
                if first and r == 0:
                    pe.wait_ge(s_kT_hi, c + 1)
                if q == 0 and d in (0, 2, 4, 6):
                    pe.wait_ge(s_q_hi, 3 * b + 1 + d // 2)
                elif q == 1 and d in (0, 4):
                    pe.wait_ge(s_q_hi, 3 * (b - 1) + 5 + d // 4)
                if not (first and d < 2):
                    pe.wait_ge(s_max_used, MAXES * b + d - 1)
                nc.tensor.matmul(maxs[d % 2][0:2 * SQ, 0:CH], q_hi[q][:, r * 2 * SQ:(r + 1) * 2 * SQ],
                                 kT_hi[q][:, c * CH:(c + 1) * CH], start=True, stop=True).then_inc(s_max, 1)

            def turn_maxima(b):
                pe.wait_ge(s_max_all, b + 1)
                nc.tensor.matmul(misc[0][ROW2:ROW2 + HP, 0:2 * SQ], max_all[:], ident[0:2 * SQ, 0:2 * SQ],
                                 start=True, stop=True).then_inc(s_maxT, 1)

            def score(b, q, u, first):
                ks, cs, out_ = slice(u // 2 * KT, u // 2 * KT + KT), slice(u % 2 * HALF, u % 2 * HALF + HALF), \
                    scores[u % 2][0:KT, 0:HALF]
                if first and u == 0:
                    pe.wait_ge(s_kT_lo, NCH)
                    pe.wait_ge(s_q_lo, 4)
                    pe.wait_ge(s_bias_k, NCH)
                if not (first and u < 2):
                    pe.wait_ge(s_p, UNITS * b + u - 1)
                nc.tensor.matmul(out_, kT_hi[q][:, ks], q_hi[q][:, cs], start=True, stop=False)
                nc.tensor.matmul(out_, kT_hi[q][:, ks], q_lo[q][:, cs], start=False, stop=False)
                nc.tensor.matmul(out_, kT_lo[q][:, ks], q_hi[q][:, cs], start=False, stop=False)
                if u < 2:
                    pe.wait_ge(s_shift, 2 * b + u + 1)
                nc.tensor.matmul(out_, bias_k[q][:, ks], shift[q][:, cs], start=False, stop=True).then_inc(s_scores, 1)

            def weigh(b, q, u, first):
                j, half = u // 2, u % 2
                vs, out_ = slice(j * D, (j + 1) * D), outT[half][:, 0:HALF]
                if first and u == 0:
                    pe.wait_ge(s_v_lo, NCH)
                if j == 0 and not first:
                    pe.wait_ge(s_o, 2 * b - 1 + half)
                pe.wait_ge(s_p_lo, UNITS * b + u + 1)
                nc.tensor.matmul(out_, v_hi[q][:, vs], p_hi[u % NP][:], start=(j == 0), stop=False)
                nc.tensor.matmul(out_, v_hi[q][:, vs], p_lo[u % NP][:], start=False, stop=False)
                nc.tensor.matmul(out_, v_lo[q][:, vs], p_hi[u % NP][:], start=False, stop=(j == NT - 1)) \
                    .then_inc(s_pv, 1)

            def denominators(b, q):
                pe.wait_ge(s_sum, SUMS * (b + 1))
                for h in range(H):
                    mm = nc.tensor.matmul(misc[1][ROW2 * q:ROW2 * q + SQ, h:h + 1], sums[q][:, h * SQ:(h + 1) * SQ],
                                          ones[0:KT, 0:1], start=True, stop=True)
                mm.then_inc(s_den, 1)

            def project(pair, g):
                if g == 1:
                    pe.wait_ge(s_inv, 2 * pair + 2)
                elif g > 1:
                    pe.wait_ge(s_y_add, H * pair + HEADS_OUT * (g - 1))
                for k in range(HEADS_OUT):
                    h = HEADS_OUT * g + k
                    mm = nc.tensor.matmul(misc[g % 2][0:ROWS, k * D:(k + 1) * D], o_pair[:, h, 0:ROWS], b_w[:, h, :],
                                          start=True, stop=True)
                mm.then_inc(s_y, 1)

            def step(b, q, pair=0, first=False, last=False):
                for u in range(UNITS):
                    chunks = [] if last else MAX_AT[q][u]
                    score(b, q, u, first)
                    for d in chunks[:-1]:
                        max_scores(b + 1, 1 - q, d)
                    if u >= LAG:
                        weigh(b, q, u - LAG, first)
                    elif not first:
                        weigh(b - 1, 1 - q, UNITS - LAG + u, False)
                    if not last:
                        if u in FOLD_AT and q == 1:
                            fold_queries(pair + 1, FOLD_AT.index(u))
                        for d in chunks[-1:]:
                            max_scores(b + 1, 1 - q, d)
                    if u == DEN_AT and not first:
                        denominators(b - 1, 1 - q)
                    if u in PROJECT_AT and q == 0 and not first:
                        project(pair, PROJECT_AT.index(u))
                    if u == TURN_AT and not last:
                        turn_maxima(b + 1)
                    if u == TURN_ROWS_AT and last:
                        turn_rows(0, s_zn, s_hT)
                    if u in QK_AT and last:
                        query_key(0, QK_AT.index(u))

            bank = scores + outT + maxs + misc

            def turn_rows(c, done, sem_):
                for i in range(4 * c, 4 * c + 4):
                    pe.wait_ge(done, i + 1)
                    mm = nc.tensor.transpose(bank[4 + c][:, i % 4 * 128:i % 4 * 128 + 128], zn[:, i, :], ident[:])
                mm.then_inc(sem_, 1)

            def query_key(c, k):
                if k == 0:
                    pe.wait_ge(s_small, 16 * SMALL)
                    pe.wait_ge(s_hT_sb, c + 1)
                if c and k == 1:
                    pe.wait_ge(s_v_sb, 2)
                nc.tensor.matmul(bank[QK_BANKS[k]][:], attn_w[("k", "k_turned", "q", "q_turned")[k]][:],
                                 hT[:, 512 * c:512 * c + 512], start=True, stop=True).then_inc(s_qk, 1)

            for g in range(len(banks)):
                fold_weights(0, g)
            pe.wait_ge(s_const, 48)
            for i in range(PAIRS):
                pe.wait_ge(s_xn, i + 1)
                mm = nc.tensor.transpose(maxs[i // 4][:, (i % 4) * D:(i % 4) * D + D], xn[:, i, :], ident[:])
                if i % 4 == 3:
                    mm.then_inc(s_xT, 1)
            for g in range(2):
                fold_weights(1, g)
            pe.wait_ge(s_folded, len(banks))
            pe.wait_ge(s_xT_used, 2)
            for g in range(H // HEADS_FOLD):
                fold_queries(0, g)
            for d in range(MAXES):
                max_scores(0, 0, d, first=True)
                if d in (MAXES // 2, MAXES // 2 + 4):
                    fold_weights(1, 2 + (d - MAXES // 2) // 4)
            pe.wait_ge(s_folded, 2 * len(banks))
            pe.wait_ge(s_q_lo, 4)
            turn_maxima(0)
            step(0, 0, first=True)
            with pe.Fori(0, PAIRS - 1) as i:
                step(2 * i + 1, 1, pair=i)
                step(2 * i + 2, 0, pair=i)
            step(B - 1, 1, last=True)
            for u in range(UNITS - LAG, UNITS):
                weigh(B - 1, 1, u, False)
            def batch(tile, b):
                return tile[:, ROW2 * b:ROW2 * b + SQ]

            def values(c):
                pe.wait_ge(s_twice, 2 * (c + 1))
                if c:
                    pe.wait_ge(s_rope, 12)
                for b in range(8 * c, 8 * c + 8):
                    mm = nc.tensor.matmul(bank[6 + b // 4 % 2][0:2 * SQ, b % 4 * D:b % 4 * D + D],
                                          hT_twice[:, b, :], attn_w["v"][:], start=True, stop=True)
                    if b % 4 == 3:
                        mm.then_inc(s_v, 1)

            def attend(i):
                if i < 2:
                    pe.wait_ge((s_p, s_o)[i], (UNITS * B, 2 * B)[i])
                    pe.wait_ge(s_cast, 3)
                else:
                    pe.wait_ge(s_att_sub, i - 1)
                for c in range(2):
                    nc.tensor.matmul(bank[2 * (i % 2) + c][0:ROWS, 0:HALF], ident_b[:],
                                     causal[:, c * HALF:(c + 1) * HALF], start=True, stop=False)
                for h in range(2):
                    b = 2 * i + h
                    pe.wait_ge(s_kh, b + 1)
                    for c in range(2):
                        mm = nc.tensor.matmul(bank[2 * (i % 2) + c][ROW2 * h:ROW2 * h + SQ, 0:HALF], batch(qT, b),
                                              k_heads[b % 4][:, HP * c:HP * (c + 1), :], start=False, stop=True)
                mm.then_inc(s_att, 1)

            def turn_attention(i):
                pe.wait_ge(s_att_exp, i + 1)
                if i:
                    pe.wait_ge(s_attT_sb, 2 * i)
                for hp in range(HA // 2):
                    mm = nc.tensor.transpose(bank[4 + hp // 4][0:2 * SQ, hp % 4 * ROWS:hp % 4 * ROWS + ROWS],
                                             att[i % 3][0:ROWS, 2 * hp:2 * hp + 2, :], ident[0:ROWS, 0:ROWS])
                mm.then_inc(s_attT, 1)

            def weigh_values(i):
                pe.wait_ge(s_attT_sb, 2 * (i + 1))
                pe.wait_ge(s_v_sb, 4)
                pe.wait_ge(s_v_ones, 1)
                if 0 < i < PAIRS - 1:
                    pe.wait_ge(s_ao_sb, i)
                for hp in range(HA // 2):
                    mm = nc.tensor.matmul(bank[out_banks(i)[0]][0:ROWS, AW * hp:AW * (hp + 1)], attT[i % 2][:, hp, :],
                                          v_heads[:, 2 * i:2 * i + 2, hp, :], start=True, stop=True)
                mm.then_inc(s_ao, 1)

            def turn_output(i):
                pe.wait_ge(s_ao_sb, i + 1)
                if 0 < i < PAIRS - 1:
                    pe.wait_ge(s_z, i)
                nc.tensor.transpose(bank[out_banks(i)[1]][:, 0:ROWS], ao[i % 2][0:ROWS, :], ident[0:ROWS, 0:ROWS]) \
                    .then_inc(s_aoT, 1)

            def project_output(i):
                pe.wait_ge(s_aoT_sb, i + 1)
                nc.tensor.matmul(bank[out_banks(i)[2]][0:ROWS, 128:256], aoT[i % 2][:], attn_w["o"][:],
                                 start=True, stop=True).then_inc(s_wo, 1)

            pe.wait_ge(s_rope, 6)
            denominators(B - 1, 1)
            pe.wait_ge(s_o, 2 * B)
            for g in range(H // HEADS_OUT):
                if g == 4:
                    attend(0)
                project(PAIRS - 1, g)
            for i in range(PAIRS + 1):
                if i == 1:
                    attend(1)
                    pe.wait_ge(s_y_add, H * PAIRS)
                    values(0)
                    turn_rows(1, s_zn, s_hT)
                    for k in range(4):
                        query_key(1, k)
                    values(1)
                elif 1 < i < PAIRS:
                    attend(i)
                if 3 <= i:
                    turn_output(i - 3)
                if 1 <= i <= PAIRS:
                    turn_attention(i - 1)
                if 3 <= i:
                    project_output(i - 3)
                if 2 <= i:
                    weigh_values(i - 2)
            weigh_values(PAIRS - 1)
            for i in (PAIRS - 2, PAIRS - 1):
                turn_output(i)
            for i in (PAIRS - 2, PAIRS - 1):
                project_output(i)

            for c in range(2):
                turn_rows(c, s_zn2, s_h2)
            for i in range(PAIRS):
                pe.wait_ge(s_h2_sb, i // 4 + 1)
                mm = nc.tensor.matmul(bank[6][0:ROWS, E * i:E * i + E], hT[:, 128 * i:128 * i + ROWS], router[:],
                                      start=True, stop=True)
            mm.then_inc(s_logits, 1)
            def columns(tile, half):
                return tile[:, half * 512:half * 512 + 512].rearrange("p (b n) -> p b n", n=ROW2)[:, :, 0:SQ]

            def spread_gates(w):
                e, half = w // (2 * SPREADS), w // SPREADS % 2
                pe.wait_ge(s_gT_lo, 2)
                pe.wait_ge(s_sel, 1)
                if w >= 2:
                    pe.wait_ge(s_gc_sb, w - 1)
                o = bank[6 + w % 2][0:MT, 0:HALF]
                nc.tensor.matmul(o, expert_sel[:, e, w % SPREADS, :], columns(gateT, half), start=True, stop=True) \
                    .then_inc(s_gc, 1)

            def hidden(n):
                e, half, m = n // (2 * NM), n // NM % 2, n % NM
                ms = slice(MT * m, MT * m + MT)
                if n % (2 * NM) == 0:
                    pe.wait_ge(*low_parts(e, 2))
                if n in (0, NM):
                    pe.wait_ge(s_h_lo, half + 1)
                if m in SPREAD_AT and n:
                    spread_gates(spread_of(n))
                for k, (sem_, used) in enumerate(((s_gate, s_silu), (s_up, s_act_raw))):
                    if n >= 2:
                        pe.wait_ge(used, n - 1)
                    o = bank[2 * k + n % 2][0:MT, 0:HALF]
                    nc.tensor.matmul(o, up_hi[e % 2][:, k, ms], columns(h_hi, half), start=True, stop=False)
                    nc.tensor.matmul(o, up_hi[e % 2][:, k, ms], columns(h_lo, half), start=False, stop=False)
                    nc.tensor.matmul(o, up_lo[e % 2][:, k, ms], columns(h_hi, half), start=False, stop=True) \
                        .then_inc(sem_, 1)

            def down(n):
                e, half, m = n // (2 * NM), n // NM % 2, n % NM
                pe.wait_ge(*low_parts(e, 3))
                pe.wait_ge(s_act_lo, n + 1)
                o = bank[4 + half][:, 0:HALF]
                first, last = e == 0 and m == 0, e == DUOS - 1 and m == NM - 1
                nc.tensor.matmul(o, down_hi[e % 2][:, m, :], act_hi[n % NA][:], start=first, stop=False)
                nc.tensor.matmul(o, down_hi[e % 2][:, m, :], act_lo[n % NA][:], start=False, stop=False)
                nc.tensor.matmul(o, down_lo[e % 2][:, m, :], act_hi[n % NA][:], start=False, stop=last) \
                    .then_inc(s_down, 1)

            def turn_back(c):
                pe.wait_ge(s_moeT, c + 1)
                pe.wait_ge(s_gc_sb, DUOS * 2 * SPREADS)
                for k in range(4):
                    mm = nc.tensor.transpose(bank[7 - c][0:ROWS, D * k:D * (k + 1)],
                                             moeT[:, 128 * (4 * c + k):128 * (4 * c + k) + ROWS], ident[:])
                mm.then_inc(s_moe, 1)

            hidden(0)
            hidden(1)
            pe.wait_ge(s_gates, 1)
            for i in range(PAIRS):
                mm = nc.tensor.transpose(bank[4 + i // 4][0:E, i % 4 * 128:i % 4 * 128 + ROWS], gates[0:ROWS, i, :],
                                         ident[0:ROWS, 0:ROWS])
                if i % 4 == 3:
                    mm.then_inc(s_gT, 1)
            hidden(2)
            spread_gates(0)
            hidden(3)
            for n in range(EARLY, STEPS + LAG_E):
                if EARLY <= n < STEPS:
                    hidden(n)
                if n >= LAG_E:
                    down(n - LAG_E)
                if n == STEPS + LAG_E - 2:
                    turn_back(0)
            turn_back(1)

        @block.scalar
        def _(act):
            banks = scores + outT

            def take_weights(which, g):
                act.wait_ge(s_fold, len(banks) * which + g + 1)
                nc.scalar.copy((a_w, b_w)[which][:, HEADS_FOLD * g:HEADS_FOLD * (g + 1), :], banks[g][:]) \
                    .then_inc(s_folded, 1)

            def split_keys(b, q, c):
                if c == 0:
                    act.wait_ge(s_raw_kT, 16 * (b + 1))
                nc.scalar.copy(kT_hi[q][:, c * CH:(c + 1) * CH], raw_kT[:, c * CH:(c + 1) * CH]).then_inc(s_kT_hi, 1)

            def split_values(b, q, c):
                if c == 0:
                    act.wait_ge(s_raw_v, 16 * (b + 1))
                nc.scalar.copy(v_hi[q][:, c * SPLIT_V:(c + 1) * SPLIT_V], raw_v[:, c * SPLIT_V:(c + 1) * SPLIT_V]) \
                    .then_inc(s_v_hi, 1)

            def mask_rows(b, c):
                if c == 0:
                    act.wait_ge(s_raw_mask, 32 * (b + 1))
                nc.scalar.activation(bias_rows[:, c * CH:(c + 1) * CH], raw_mask[:, c * CH:(c + 1) * CH], ACT.Copy,
                                     bias=-BIG, scale=BIG).then_inc(s_bias_rows, 1)

            def mask_keys(b, q, c, first=False):
                if first and c == 0:
                    act.wait_ge(s_gset, GSETS)
                nc.scalar.activation(bias_k[q][0:SQ, c * CH:(c + 1) * CH], raw_mask[0:SQ, c * CH:(c + 1) * CH],
                                     ACT.Copy, bias=-BIG, scale=BIG).then_inc(s_bias_k, 1)

            def take_queries(pair, g):
                act.wait_ge(s_q, 4 * pair + g + 1)
                hs = slice(HEADS_FOLD * SQ * g, HEADS_FOLD * SQ * (g + 1))
                folded = misc[g % 2][:, 0:HEADS_FOLD * ROWS].rearrange("p (h n) -> p h n", h=HEADS_FOLD)
                nc.scalar.copy(q_hi[0][:, hs].rearrange("p (h n) -> p h n", n=SQ), folded[:, :, 0:SQ]).then_inc(s_q_hi, 1)
                nc.scalar.copy(q_next[:, hs].rearrange("p (h n) -> p h n", n=SQ), folded[:, :, ROW2:ROWS]) \
                    .then_inc(s_q_next, 1)

            def take_next_queries(half):
                hs = slice(half * HALF, (half + 1) * HALF)
                nc.scalar.copy(q_hi[1][:, hs], q_next[:, hs]).then_inc(s_q_hi, 1)

            def exponentials(b, u, first):
                act.wait_ge(s_scores, UNITS * b + u + 1)
                nc.scalar.activation(p_hi[u % NP][:], scores[u % 2][0:KT, 0:HALF], ACT.Exp, scale=SCALE)
                if not (first and u < NP):
                    w = (u - NP) % UNITS
                    act.wait_ge(s_sum, SUMS * (b if u >= NP else b - 1) + (w - 1 if w >= 2 else w + 1))
                nc.scalar.activation(p[u % NP][:], scores[u % 2][0:KT, 0:HALF], ACT.Exp, scale=SCALE).then_inc(s_p, 1)

            def take_output(b, q, half):
                act.wait_ge(s_pv, UNITS * b + UNITS - 1 + half)
                nc.scalar.copy(o_pair[:, HP * half:HP * (half + 1), ROW2 * q:ROW2 * q + SQ],
                               outT[half][:, 0:HALF].rearrange("p (h n) -> p h n", h=HP)).then_inc(s_o, 1)

            def step(b, q, pair=0, first=False, last=False):
                n = 1 - q
                for u in range(UNITS):
                    exponentials(b, u, first)
                    if u in (LAG - 2, LAG - 1) and not first:
                        take_output(b - 1, n, u - LAG + 2)
                    if last:
                        continue
                    if u in (0, 5, 7):
                        split_keys(b + 1, n, (0, 5, 7).index(u))
                    if u in (2, 3, 4, 5) and q == 1:
                        take_queries(pair + 1, u - 2)
                    if u in (3, 4) and q == 0:
                        take_next_queries(u - 3)
                    if u in (0, 6, 8):
                        mask_rows(b + 1, (0, 6, 8).index(u))
                    if u in (9, 10, 11):
                        mask_keys(b + 1, n, u - 9)
                    if u in (13, 15, 17):
                        split_values(b + 1, n, (u - 13) // 2)

            for g in range(len(banks)):
                take_weights(0, g)
                if g < NCH:
                    split_keys(0, 0, g)
            mask_rows(0, 0)
            for g in range(H // HEADS_FOLD):
                take_queries(0, g)
            for c in range(1, NCH):
                mask_rows(0, c)
            for g in range(2):
                take_weights(1, g)
            for c in range(NCH):
                mask_keys(0, 0, c, first=True)
            for g in range(2, len(banks)):
                take_weights(1, g)
            for c in range(NCH):
                split_values(0, 0, c)
            step(0, 0, first=True)
            with act.Fori(0, PAIRS - 1) as i:
                step(2 * i + 1, 1, pair=i)
                step(2 * i + 2, 0)
            step(B - 1, 1, last=True)
            for half in range(2):
                take_output(B - 1, 1, half)

            bank = scores + outT + maxs + misc

            def twice(c):
                act.wait_ge(s_hT_sb, c + 1)
                for k in range(2):
                    nc.scalar.copy(hT_twice[:, 8 * c:8 * c + 8, SQ * k:SQ * k + SQ],
                                   hT[:, 512 * c:512 * c + 512].rearrange("p (b n) -> p b n", n=ROW2)[:, :, 0:SQ]) \
                        .then_inc(s_twice, 1)

            twice(0)
            act.wait_ge(s_small, 16 * SMALL)
            nc.scalar.copy(v_heads[:, :, :, 2 * DA:], v_sel[:].rearrange("p (h two d) -> p h two d", two=2, d=DA)[:, :, :, 0]
                           .unsqueeze(1).to_broadcast([2 * SQ, B, HA // 2, 2])).then_inc(s_v_ones, 1)
            act.wait_ge(s_mixed, 48)
            nc.scalar.copy(causal[:], causal_f[:]).then_inc(s_cast, 1)
            nc.scalar.copy(ident_b[:, 0:ROW2], ident[0:SQ, 0:ROW2]).then_inc(s_cast, 1)
            nc.scalar.copy(ident_b[:, ROW2:], ident[0:SQ, 0:SQ]).then_inc(s_cast, 1)

            def exponentials_a(i):
                act.wait_ge(s_att_sub, i + 1)
                nc.scalar.activation(att[i % 3][0:ROWS], att[i % 3][0:ROWS], ACT.Exp, scale=SCALE_A).then_inc(s_att_exp, 1)

            def take_attT(i):
                act.wait_ge(s_attT, i + 1)
                if i >= 2:
                    act.wait_ge(s_ao, i - 1)
                for c in range(2):
                    nc.scalar.copy(attT[i % 2][:, 4 * c:4 * c + 4, :],
                                   bank[4 + c][0:2 * SQ, 0:4 * ROWS].rearrange("p (h n) -> p h n", h=4)) \
                        .then_inc(s_attT_sb, 1)

            def take_aoT(i):
                act.wait_ge(s_aoT, i + 1)
                if i >= 2:
                    act.wait_ge(s_wo, i - 1)
                nc.scalar.copy(aoT[i % 2][:], bank[out_banks(i)[1]][:, 0:ROWS]).then_inc(s_aoT_sb, 1)

            def split_expert(e, k):
                act.wait_ge((s_up_raw, s_up_raw, s_down_raw)[k], 16 * (e + 1))
                if e >= 2:
                    act.wait_ge(s_down if k == 2 else s_up, 2 * NM * (e - 1))
                if k < 2:
                    nc.scalar.copy(up_hi[e % 2][:, k, :], up_raw[:, k, :]).then_inc(s_w_hi, 1)
                else:
                    nc.scalar.copy(down_hi[e % 2][:], down_raw[:]).then_inc(s_w_hi, 1)

            for i in range(PAIRS + 3):
                if i == 1:
                    twice(1)
                if 3 <= i:
                    take_aoT(i - 3)
                if i < PAIRS:
                    exponentials_a(i)
                if 1 <= i <= PAIRS:
                    take_attT(i - 1)
                if i in WEIGHTS_AT:
                    split_expert(0, WEIGHTS_AT.index(i))

            def take_gates(w):
                act.wait_ge(s_gc, w + 1)
                if w >= 2:
                    act.wait_ge(s_actf, NM * ((w - 1) // SPREADS) + SPREAD_AT[(w - 1) % SPREADS])
                nc.scalar.copy(gate_cols[w % 2][:], bank[6 + w % 2][0:MT, 0:HALF]).then_inc(s_gc_sb, 1)

            def silu_of(n):
                act.wait_ge(s_gate, n + 1)
                if n >= NA:
                    act.wait_ge(s_act_raw, n - NA + 1)
                nc.scalar.activation(silu[n % NA][:], bank[n % 2][0:MT, 0:HALF], ACT.Silu).then_inc(s_silu, 1)

            def high(n):
                act.wait_ge(s_actf, n + 1)
                if n >= NA:
                    act.wait_ge(s_down, n - NA + 1)
                nc.scalar.copy(act_hi[n % NA][:], act_f[n % NA][:]).then_inc(s_act_hi, 1)

            def take_sum(c):
                act.wait_ge(s_moe_set, 1)
                act.wait_ge(s_down, STEPS - (1 - c) * NM)
                nc.scalar.copy(moeT[:, 512 * c:512 * c + 512].rearrange("p (b n) -> p b n", n=ROW2)[:, :, 0:SQ],
                               bank[4 + c][:, 0:HALF].rearrange("p (b n) -> p b n", n=SQ)).then_inc(s_moeT, 1)

            nc.scalar.copy(expert_sel[:], expert_sel_f[:]).then_inc(s_sel, 1)
            for c in range(2):
                act.wait_ge(s_h2_sb, c + 1)
                nc.scalar.copy(h_hi[:, 512 * c:512 * c + 512], hT[:, 512 * c:512 * c + 512]).then_inc(s_h_hi, 1)
            act.wait_ge(s_lmax, 1)
            nc.scalar.activation(gates[0:ROWS], gates[0:ROWS], ACT.Exp).then_inc(s_lexp, 1)
            silu_of(0)
            silu_of(1)
            act.wait_ge(s_gT_set, 1)
            for c in range(2):
                act.wait_ge(s_gT, c + 1)
                nc.scalar.copy(gateT[0:E, 512 * c:512 * c + 512].rearrange("p (b n) -> p b n", n=128)[:, :, 0:ROWS],
                               bank[4 + c][0:E, :].rearrange("p (b n) -> p b n", n=128)[:, :, 0:ROWS]).then_inc(s_gT_hi, 1)
            silu_of(2)
            silu_of(3)
            for n in range(STEPS + 1):
                if n < STEPS:
                    if n % NM in SPREAD_AT:
                        take_gates(spread_of(n))
                    if n >= EARLY:
                        silu_of(n)
                if n >= 1:
                    high(n - 1)
                if n % (2 * NM) in SPLIT_AT and n // (2 * NM) < DUOS - 1:
                    split_expert(n // (2 * NM) + 1, SPLIT_AT.index(n % (2 * NM)))
            for c in range(2):
                take_sum(c)

        @block.vector
        def _(dve):
            nc.vector.memset(x_rows[:], 0.0).then_inc(s_set, 1)
            nc.vector.memset(ones[:], 1.0).then_inc(s_set, 1)
            chained = [0]

            def then(ins, *more):
                for x in (ins, *more):
                    chained[0] += 1
                    x.then_inc(s_step, 1)
                dve.wait_ge(s_step, chained[0])

            def rsqrt_seed(v, y, a):
                vi, yi, ai = (w.bitcast(I32) for w in (v, y, a))
                then(nc.vector.tensor_scalar(ai, vi, 1, None, ALU.logical_shift_right))
                then(nc.vector.tensor_scalar(yi, ai, -1, RSQRT_SEED, ALU.mult, ALU.add))

            def newton(v, y, a):
                then(nc.vector.scalar_tensor_tensor(out=a, in0=y, scalar=-0.5, in1=y, op0=ALU.mult, op1=ALU.mult))
                then(nc.vector.tensor_tensor(a, a, v, ALU.mult))
                then(nc.vector.scalar_tensor_tensor(out=y, in0=a, scalar=1.5, in1=y, op0=ALU.add, op1=ALU.mult))

            def rsqrt(v, y, a):
                rsqrt_seed(v, y, a)
                for _ in range(NEWTON_STEPS):
                    newton(v, y, a)

            def variances(first, end):
                then(*[nc.vector.bn_aggr(moments[:, i, :], stats[:, i, :]) for i in range(first, end)])
                then(nc.vector.tensor_scalar(nrm[:, 0, first:end], moments[:, first:end, 1], LN_EPS, None, ALU.add))

            dve.wait_ge(s_x, 32)
            then(*[nc.vector.bn_stats(stats[:, i, :], x_rows[:, i, :]) for i in range(PAIRS)])
            variances(0, PAIRS)
            rsqrt(nrm[:, 0, :], nrm[:, 1, :], nrm[:, 2, :])
            for i in range(PAIRS):
                nc.vector.tensor_scalar(xn[:, i, :], x_rows[:, i, :], moments[:, i, 0:1], nrm[:, 1, i:i + 1],
                                        ALU.subtract, ALU.mult).then_inc(s_xn, 1)
            dve.wait_ge(s_const, 48)
            for q in range(2):
                nc.vector.tensor_copy(shift[q][0:ROW2, :], row_sel[:]).then_inc(s_shset, 1)
            for half in range(2):
                dve.wait_ge(s_xT, half + 1)
                nc.vector.tensor_copy(xnT[:, 4 * half:4 * half + 4, :], maxs[half][:]).then_inc(s_xT_used, 1)

            def pick_queries(pair, first=False):
                if first:
                    dve.wait_ge(s_xT_used, 2)
                nc.vector.tensor_copy(xq[:], xnT[:, bass.ds(pair, 1), 0:ROWS].rearrange("p o n -> p (o n)")) \
                    .then_inc(s_xq, 1)

            def split_queries(pair, g):
                dve.wait_ge(s_q_next, 4 * pair + g + 1)
                hs = slice(HEADS_FOLD * SQ * g, HEADS_FOLD * SQ * (g + 1))
                folded = misc[g % 2][:, 0:HEADS_FOLD * ROWS].rearrange("p (h n) -> p h n", h=HEADS_FOLD)
                nc.vector.tensor_tensor(q_lo[0][:, hs].rearrange("p (h n) -> p h n", n=SQ), folded[:, :, 0:SQ],
                                        q_hi[0][:, hs].rearrange("p (h n) -> p h n", n=SQ), ALU.subtract) \
                    .then_inc(s_q_lo, 1)

            def split_next_queries(half):
                hs = slice(half * HALF, (half + 1) * HALF)
                nc.vector.tensor_tensor(q_lo[1][:, hs], q_next[:, hs], q_hi[1][:, hs], ALU.subtract).then_inc(s_q_lo, 1)

            def take_maxima(b, d, first=False):
                c, r = d // HP, d % HP
                if first:
                    dve.wait_ge(s_max, d + 1)
                    dve.wait_ge(s_bias_rows, c + 1)
                    if d > 1:
                        dve.wait_ge(s_max_used, d - 1)
                nc.vector.tensor_tensor_reduce(out=masked[d % 2][:], in0=maxs[d % 2][0:2 * SQ, 0:CH],
                                               in1=bias_rows[:, c * CH:(c + 1) * CH], scale=1.0, scalar=-BIG / 2,
                                               op0=ALU.add, op1=ALU.max, accum_out=max_part[:, r, c:c + 1]) \
                    .then_inc(s_max_used, 1)

            def join_maxima(b):
                dve.wait_ge(s_max_used, MAXES * (b + 1))
                nc.vector.tensor_reduce(max_all[:], max_part[:], AX_X, ALU.max).then_inc(s_max_all, 1)

            def shift_rows(b, q):
                dve.wait_ge(s_maxT, b + 1)
                for half in range(2):
                    nc.vector.tensor_tensor(
                        shift[q][ROW2:ROW2 + HP, half * HALF:half * HALF + HALF].rearrange("p (r n) -> p r n", n=2 * SQ),
                        pair_sel[ROW2:ROW2 + HP, HP // 2 * half:HP // 2 * (half + 1)],
                        misc[0][ROW2:ROW2 + HP, 0:2 * SQ].unsqueeze(1).to_broadcast([HP, HP // 2, 2 * SQ]), ALU.mult) \
                        .then_inc(s_shift, 1)

            def split_probabilities(b, u, first):
                dve.wait_ge(s_p, UNITS * b + u + 1)
                nc.vector.tensor_tensor(p_lo[u % NP][:], p[u % NP][:], p_hi[u % NP][:], ALU.subtract) \
                    .then_inc(s_p_lo, 1)

            def invert(b, q, last=False):
                if last:
                    dve.wait_ge(s_den, b + 1)
                rows = slice(ROW2 * q, ROW2 * q + SQ)
                nc.vector.reciprocal(inv[rows, :], misc[1][rows, 0:H]).then_inc(s_inv, 1)

            def add_heads(pair, g, last=False):
                rows = x_rows[0:ROWS, bass.ds(pair, 1), :].rearrange("p o n -> p (o n)")
                if last:
                    dve.wait_ge(s_y, H // HEADS_OUT * pair + g + 1)
                for k in range(HEADS_OUT):
                    h = HEADS_OUT * g + k
                    if h == 0:
                        dve.wait_ge(s_inv, 2 * (pair + 1))
                    else:
                        dve.wait_ge(s_y_add, H * pair + h)
                    ins = nc.vector.scalar_tensor_tensor(
                        out=rows if h == H - 1 else y_rows[0:ROWS, :], in0=misc[g % 2][0:ROWS, k * D:(k + 1) * D],
                        scalar=inv[0:ROWS, h:h + 1], in1=y_rows[0:ROWS, :] if h else rows,
                        op0=ALU.mult, op1=ALU.add)
                    ins.then_inc(s_y_add, 1)

            mean_sq, inv_rms = nrm[:, 2, :], nrm[:, 3, :]

            def layernorm(first, end):
                then(*[nc.vector.tensor_scalar(z[:, i, :], x_rows[:, i, :], moments[:, i, 0:1], nrm[:, 1, i:i + 1],
                                               ALU.subtract, ALU.mult) for i in range(first, end)])

            def squares(first, end):
                for i in range(first, end):
                    nc.vector.tensor_tensor_reduce(out=zn[:, i, :], in0=z[:, i, :], in1=z[:, i, :], scale=1.0,
                                                   scalar=0.0, op0=ALU.mult, op1=ALU.add,
                                                   accum_out=nrm[:, 2, i:i + 1]).then_inc(s_square, 1)

            def mean_squares(first, end):
                then(nc.vector.tensor_scalar(mean_sq[:, first:end], mean_sq[:, first:end], 1.0 / D, RMS_EPS,
                                             ALU.mult, ALU.add))

            def rmsnorm(first, end, sem_):
                for i in range(first, end):
                    nc.vector.tensor_scalar(zn[:, i, :], z[:, i, :], nrm[:, 3, i:i + 1], None, ALU.mult).then_inc(sem_, 1)

            bank = scores + outT + maxs + misc

            def take_turned(which, c, done, sem_):
                dve.wait_ge(done, c + 1)
                nc.vector.tensor_scalar(hT[:, 512 * c:512 * c + 512], bank[4 + c][:], ln_w[:, which:which + 1], None,
                                        ALU.mult).then_inc(sem_, 1)

            def rotate(c, k):
                dst, at = (kT, qT)[k], 6 * c + 3 * k
                dve.wait_ge(s_qk, 4 * c + 2 * k + 2)
                for j, (o, table) in enumerate(((turn_a, cos_t), (turn_b, sin_t))):
                    if at:
                        dve.wait_ge(s_rope, at)
                    nc.vector.tensor_tensor(o[:].rearrange("p (b n) -> p b n", n=ROW2),
                                            bank[QK_BANKS[2 * k + j]][:].rearrange("p (b n) -> p b n", n=ROW2),
                                            table[:].unsqueeze(1).to_broadcast([D, 8, ROW2]), ALU.mult) \
                        .then_inc(s_rope, 1)
                dve.wait_ge(s_rope, at + 2)
                nc.vector.tensor_tensor(dst[:, 512 * c:512 * c + 512], turn_a[:], turn_b[:], ALU.add).then_inc(s_rope, 1)

            def norms_step(u):
                done = PAIRS - 1
                late = [w[:, 0:done] for w in (nrm[:, 0, :], nrm[:, 1, :], mean_sq, inv_rms)]
                if u == 3:
                    dve.wait_ge(s_y_add, H * done)
                    then(*[nc.vector.bn_stats(stats[:, i, :], x_rows[:, i, :]) for i in range(done)])
                if u == 4:
                    variances(0, done)
                    rsqrt_seed(late[0], late[1], late[2])
                if u in (5, 6, 7):
                    newton(late[0], late[1], late[2])
                if u == 8:
                    layernorm(0, done)
                if u == 9:
                    squares(0, done)
                if u == 10:
                    dve.wait_ge(s_square, done)
                    mean_squares(0, done)
                    rsqrt_seed(late[2], late[3], late[0])
                if u in (11, 12, 13):
                    newton(late[2], late[3], late[0])
                if u == 14:
                    rmsnorm(0, done, s_zn)
                if u == 16:
                    for w in ao + att:
                        nc.vector.memset(w[:], 0.0).then_inc(s_clear, 1)
                if u == TURN_ROWS_AT + 1:
                    dve.wait_ge(s_small, 16 * SMALL)
                    take_turned(0, 0, s_hT, s_hT_sb)
                if u in (QK_AT[2], QK_AT[3] + 1):
                    rotate(0, (QK_AT[2], QK_AT[3] + 1).index(u))

            def step(b, q, pair=0, first=False, last=False):
                n = 1 - q
                for u in range(UNITS):
                    if u == 0 and q == 1 and not last:
                        pick_queries(pair + 1)
                    split_probabilities(b, u, first)
                    if MAX_AT[q][u] and not last:
                        dve.wait_ge(s_max, MAXES * (b + 1) + MAX_AT[q][u][-1] + 1)
                        dve.sem_inc(s_max_seen, 1)
                        for d in MAX_AT[q][u]:
                            take_maxima(b + 1, d)
                    if u == TURN_AT + 1 and not last:
                        shift_rows(b + 1, n)
                    if not first:
                        if u == DEN_AT + 1:
                            invert(b - 1, n)
                        if u - 1 in PROJECT_AT and q == 0:
                            add_heads(pair, PROJECT_AT.index(u - 1))
                    if last:
                        norms_step(u)
                        continue
                    if u in (2, 3, 4, 5) and q == 1:
                        split_queries(pair + 1, u - 2)
                    if u in (4, 5) and q == 0:
                        split_next_queries(u - 4)
                    if u == TURN_AT - 1:
                        join_maxima(b + 1)

            pick_queries(0, first=True)
            for g in range(H // HEADS_FOLD):
                split_queries(0, g)
            for d in range(MAXES):
                take_maxima(0, d, first=True)
            join_maxima(0)
            shift_rows(0, 0)
            step(0, 0, first=True)
            with dve.Fori(0, PAIRS - 1) as i:
                step(2 * i + 1, 1, pair=i)
                step(2 * i + 2, 0, pair=i)
            step(B - 1, 1, pair=PAIRS - 1, last=True)
            invert(B - 1, 1, last=True)

            def place_values(c):
                for g in (2 * c, 2 * c + 1):
                    dve.wait_ge(s_v, g + 1)
                    nc.vector.tensor_tensor(
                        v_heads[:, 4 * g:4 * g + 4, :, 0:2 * DA],
                        bank[6 + g % 2][0:2 * SQ, :].rearrange("p (b h n) -> p b h n", b=4, n=2 * DA),
                        v_sel[:].rearrange("p (h n) -> p h n", n=2 * DA).unsqueeze(1)
                        .to_broadcast([2 * SQ, 4, HA // 2, 2 * DA]), ALU.mult) \
                        .then_inc(s_v_sb, 1)

            for g in range(H // HEADS_OUT):
                add_heads(PAIRS - 1, g, last=True)
            dve.wait_ge(s_y_add, H * PAIRS)
            then(nc.vector.bn_stats(stats[:, PAIRS - 1, :], x_rows[:, PAIRS - 1, :]))
            variances(PAIRS - 1, PAIRS)
            latest = [w[:, PAIRS - 1:PAIRS] for w in (nrm[:, 0, :], nrm[:, 1, :], mean_sq, inv_rms)]
            rsqrt(latest[0], latest[1], latest[2])
            layernorm(PAIRS - 1, PAIRS)
            squares(PAIRS - 1, PAIRS)
            dve.wait_ge(s_square, PAIRS)
            mean_squares(PAIRS - 1, PAIRS)
            rsqrt(latest[2], latest[3], latest[0])
            rmsnorm(PAIRS - 1, PAIRS, s_zn)
            place_values(0)
            take_turned(0, 1, s_hT, s_hT_sb)
            dve.wait_ge(s_clear, 5)

            def subtract_max(i):
                dve.wait_ge(s_att, i + 1)
                s_ = [bank[2 * (i % 2) + c][0:ROWS, 0:HALF].rearrange("p (h n) -> p h n", h=HP) for c in range(2)]
                then(*[nc.vector.tensor_reduce(att_max[0:ROWS, i, HP * c:HP * c + HP], s_[c], AX_X, ALU.max)
                       for c in range(2)])
                if i >= 3:
                    dve.wait_ge(s_attT, i - 2)
                for c in range(2):
                    ins = nc.vector.tensor_tensor(
                        att[i % 3][0:ROWS, HP * c:HP * c + HP, :], s_[c],
                        att_max[0:ROWS, i, HP * c:HP * c + HP].unsqueeze(2).to_broadcast([ROWS, HP, SQ]), ALU.subtract)
                ins.then_inc(s_att_sub, 1)

            def take_ao(i):
                dve.wait_ge(s_ao, i + 1)
                if i >= 2:
                    dve.wait_ge(s_aoT, i - 1)
                own = [bank[out_banks(i)[0]][ROW2 * h:ROW2 * h + SQ, 0:AW * HA // 2]
                       .rearrange("p (h b n) -> p h b n", b=2, n=2 * DA + 2)[:, :, h, :] for h in range(2)]
                inv_ = [att_inv[ROW2 * h:ROW2 * h + SQ, i, :].rearrange("p (h two) -> p h two", two=2) for h in range(2)]
                then(*[nc.vector.reciprocal(inv_[h], own[h][:, :, 2 * DA:]) for h in range(2)])
                for h in range(2):
                    ins = nc.vector.tensor_tensor(
                        ao[i % 2][ROW2 * h:ROW2 * h + SQ, :].rearrange("p (h two d) -> p h two d", two=2, d=DA),
                        own[h][:, :, 0:2 * DA].rearrange("p h (two d) -> p h two d", d=DA),
                        inv_[h].unsqueeze(3).to_broadcast([SQ, HA // 2, 2, DA]), ALU.mult)
                ins.then_inc(s_ao_sb, 1)

            def add_attention(i):
                dve.wait_ge(s_wo, i + 1)
                nc.vector.tensor_tensor(z[0:ROWS, i, :], bank[out_banks(i)[2]][0:ROWS, 128:256], z[0:ROWS, i, :], ALU.add) \
                    .then_inc(s_z, 1)
                dve.wait_ge(s_z, i + 1)
                squares(i, i + 1)

            for i in range(PAIRS + 4):
                if 4 <= i:
                    add_attention(i - 4)
                if i < PAIRS:
                    subtract_max(i)
                if i == 0:
                    rotate(1, 0)
                    rotate(1, 1)
                    place_values(1)
                if 2 <= i <= PAIRS + 1:
                    take_ao(i - 2)

            dve.wait_ge(s_square, 2 * PAIRS)
            mean_squares(0, PAIRS)
            rsqrt(mean_sq, inv_rms, nrm[:, 0, :])
            rmsnorm(0, PAIRS, s_zn2)
            for c in range(2):
                take_turned(1, c, s_h2, s_h2_sb)

            def split_expert(e, k):
                dve.wait_ge(s_w_hi, 3 * e + k + 1)
                if k < 2:
                    nc.vector.tensor_tensor(up_lo[e % 2][:, k, :], up_raw[:, k, :], up_hi[e % 2][:, k, :],
                                            ALU.subtract).then_inc(s_w_lo, 1)
                else:
                    nc.vector.tensor_tensor(down_lo[e % 2][:], down_raw[:], down_hi[e % 2][:],
                                            ALU.subtract).then_inc(s_w_lo, 1)

            dve.wait_ge(s_logits, 1)
            logits = bank[6][0:ROWS, 0:PAIRS * E].rearrange("p (t e) -> p t e", e=E)
            R = [ROWS, PAIRS, E]
            then(nc.vector.tensor_reduce(gate_max[0:ROWS], logits, AX_X, ALU.max))
            nc.vector.tensor_tensor(gates[0:ROWS], logits, gate_max[0:ROWS].unsqueeze(2).to_broadcast(R),
                                    ALU.subtract).then_inc(s_lmax, 1)
            dve.wait_ge(s_lexp, 1)
            dve.wait_ge(s_mixed, 48)
            R4 = [ROWS, PAIRS, E, E]
            mine = gates[0:ROWS].unsqueeze(3).to_broadcast(R4)
            others = gates[0:ROWS].unsqueeze(2).to_broadcast(R4)
            then(nc.vector.tensor_tensor(above[0:ROWS], others, mine, ALU.is_gt),
                 nc.vector.tensor_tensor(same[0:ROWS], others, mine, ALU.is_equal))
            then(nc.vector.tensor_tensor(same[0:ROWS], same[0:ROWS],
                                         rank_tri[0:ROWS].unsqueeze(1).to_broadcast(R4), ALU.mult))
            then(nc.vector.tensor_tensor(above[0:ROWS], above[0:ROWS], same[0:ROWS], ALU.add))
            then(nc.vector.tensor_reduce(rank[0:ROWS], above[0:ROWS], AX_X, ALU.add))
            then(nc.vector.scalar_tensor_tensor(out=rank[0:ROWS], in0=rank[0:ROWS], scalar=1.5, in1=gates[0:ROWS],
                                                op0=ALU.is_lt, op1=ALU.mult))
            then(nc.vector.tensor_reduce(gate_sum[0:ROWS], rank[0:ROWS], AX_X, ALU.add))
            then(nc.vector.reciprocal(gate_sum[0:ROWS], gate_sum[0:ROWS]))
            nc.vector.tensor_tensor(gates[0:ROWS], rank[0:ROWS], gate_sum[0:ROWS].unsqueeze(2).to_broadcast(R),
                                    ALU.mult).then_inc(s_gates, 1)

            def activate(n):
                dve.wait_ge(s_up, n + 1)
                dve.wait_ge(s_silu, n + 1)
                if n >= NA:
                    dve.wait_ge(s_actf, n - NA + 1)
                nc.vector.tensor_tensor(act_raw[n % NA][:], bank[2 + n % 2][0:MT, 0:HALF], silu[n % NA][:], ALU.mult) \
                    .then_inc(s_act_raw, 1)

            activate(0)
            activate(1)
            for c in range(2):
                dve.wait_ge(s_gT_hi, c + 1)
                cols = slice(512 * c, 512 * c + 512)
                pick = lambda w: w.rearrange("p (b n) -> p b n", n=128)[:, :, 0:ROWS]
                nc.vector.tensor_tensor(pick(gateT[LOW:LOW + E, cols]), pick(bank[4 + c][0:E, :]), pick(gateT[0:E, cols]),
                                        ALU.subtract).then_inc(s_gT_lo, 1)

            activate(2)
            activate(3)
            for n in range(STEPS):
                if n >= EARLY:
                    activate(n)
                dve.wait_ge(s_act_raw, n + 1)
                dve.wait_ge(s_gc_sb, spread_of(n) + 1)
                if n >= NA:
                    dve.wait_ge(s_act_lo, n - NA + 1)
                nc.vector.tensor_tensor(act_f[n % NA][:], act_raw[n % NA][:], gate_cols[spread_of(n) % 2][:], ALU.mult) \
                    .then_inc(s_actf, 1)
                if n % (2 * NM) in SPLIT_AT and n // (2 * NM) < DUOS - 1:
                    split_expert(n // (2 * NM) + 1, SPLIT_AT.index(n % (2 * NM)))
                if n == 2 * NM:
                    nc.vector.tensor_tensor(z[0:ROWS], z[0:ROWS], x_rows[0:ROWS], ALU.add).then_inc(s_res, 1)
            dve.wait_ge(s_res, 1)
            for c in range(2):
                dve.wait_ge(s_moe, c + 1)
                rows = z[0:ROWS, 4 * c:4 * c + 4, :]
                nc.vector.tensor_tensor(rows, bank[7 - c][0:ROWS, :].rearrange("p (t n) -> p t n", n=D), rows, ALU.add) \
                    .then_inc(s_final, 1)

        @block.gpsimd
        def _(pool):
            for q in range(2):
                nc.gpsimd.memset(bias_k[q][0:ROW2, :].bitcast(F32), 0.0).then_inc(s_gset, 1)
                nc.gpsimd.memset(bias_k[q][ROW2:ROW2 + HP, :].bitcast(F32), 1.0).then_inc(s_gset, 1)
            pool.wait_ge(s_gset, GSETS - 2)
            nc.gpsimd.memset(o_pair[:], 0.0).then_inc(s_gset, 1)
            nc.gpsimd.memset(inv[:], 0.0).then_inc(s_gset, 1)

            def split_values(b, q, c):
                pool.wait_ge(s_v_hi, NCH * b + c + 1)
                cs = slice(c * SPLIT_V, (c + 1) * SPLIT_V)
                nc.gpsimd.tensor_tensor(v_lo[q][:, cs], raw_v[:, cs], v_hi[q][:, cs], ALU.subtract).then_inc(s_v_lo, 1)

            def split_keys(b, q, c):
                pool.wait_ge(s_kT_hi, NCH * b + c + 1)
                nc.gpsimd.tensor_tensor(kT_lo[q][:, c * CH:(c + 1) * CH], raw_kT[:, c * CH:(c + 1) * CH],
                                        kT_hi[q][:, c * CH:(c + 1) * CH], ALU.subtract).then_inc(s_kT_lo, 1)

            def sum_probabilities(b, q, u):
                acc = sums[q][:, u % 2 * HALF:u % 2 * HALF + HALF]
                pool.wait_ge(s_p, UNITS * b + u + 1)
                if u < 4:
                    nc.gpsimd.tensor_tensor(acc, p[u - 2][:], p[u][:], ALU.add).then_inc(s_sum, 1)
                else:
                    pool.wait_ge(s_sum, SUMS * b + u - 3)
                    nc.gpsimd.tensor_tensor(acc, acc, p[u % NP][:], ALU.add).then_inc(s_sum, 1)

            def step(b, q, last=False):
                for u in range(UNITS):
                    if u >= 2:
                        sum_probabilities(b, q, u)
                    if u in (7, 9, 11) and not last:
                        split_keys(b + 1, 1 - q, (u - 7) // 2)
                    if u in (14, 16, 18) and not last:
                        split_values(b + 1, 1 - q, (u - 14) // 2)

            for c in range(NCH):
                split_keys(0, 0, c)
            for c in range(NCH):
                split_values(0, 0, c)
            step(0, 0)
            with pool.Fori(0, PAIRS - 1) as i:
                step(2 * i + 1, 1)
                step(2 * i + 2, 0)
            step(B - 1, 1, last=True)

            for b in range(B):
                if b % 8 == 0:
                    pool.wait_ge(s_rope, 6 * (b // 8) + 3)
                if b >= 4:
                    pool.wait_ge(s_att, (b - 4) // 2 + 1)
                nc.gpsimd.tensor_tensor(k_heads[b % 4][:],
                                        kT[:, ROW2 * b:ROW2 * b + SQ].unsqueeze(1).to_broadcast([D, HA, SQ]),
                                        head_sel[:].unsqueeze(2).to_broadcast([D, HA, SQ]), ALU.mult).then_inc(s_kh, 1)

            for k in range(3):
                pool.wait_ge(s_w_hi, k + 1)
                low, raw, high = ((up_lo[0][:, k, :], up_raw[:, k, :], up_hi[0][:, k, :]) if k < 2 else
                                  (down_lo[0][:], down_raw[:], down_hi[0][:]))
                nc.gpsimd.tensor_tensor(low, raw, high, ALU.subtract).then_inc(s_w_lo_first, 1)
            pool.wait_ge(s_zn2, PAIRS)
            nc.gpsimd.memset(gateT[:].bitcast(F32), 0.0).then_inc(s_gT_set, 1)
            for c in range(2):
                pool.wait_ge(s_h_hi, c + 1)
                nc.gpsimd.tensor_tensor(h_lo[:, 512 * c:512 * c + 512], hT[:, 512 * c:512 * c + 512],
                                        h_hi[:, 512 * c:512 * c + 512], ALU.subtract).then_inc(s_h_lo, 1)
            nc.gpsimd.memset(moeT[:], 0.0).then_inc(s_moe_set, 1)
            for n in range(STEPS):
                pool.wait_ge(s_act_hi, n + 1)
                if n >= NA:
                    pool.wait_ge(s_down, n - NA + 1)
                nc.gpsimd.tensor_tensor(act_lo[n % NA][:], act_f[n % NA][:], act_hi[n % NA][:], ALU.subtract) \
                    .then_inc(s_act_lo, 1)


def _constants():
    import numpy as np
    row_sel = np.zeros((ROW2, H, SQ), np.float32)
    row_sel[np.arange(SQ), :, np.arange(SQ)] = 1.0
    pair_sel = np.zeros((HP, HP, 2 * SQ), np.float32)
    pair_sel[np.arange(HP), np.arange(HP)] = -1.0
    place = np.arange(ROW2, dtype=np.float32)[:, None]
    freq = (np.float32(1.0) / np.float32(10000.0) ** (np.arange(0, DA, 2, dtype=np.float32) / np.float32(DA)))
    angle = (place * freq[None, :].astype(np.float32)).astype(np.float32)
    cos = np.tile(np.cos(angle), (1, 2 * HA)).T
    sin = np.tile(np.concatenate([-np.sin(angle), np.sin(angle)], axis=1), (1, HA)).T
    causal = np.where(np.arange(SQ)[None, :] > np.arange(SQ)[:, None], np.float32(-BIG), np.float32(0.0))
    v_sel = np.zeros((2, SQ, HA // 2, 2, DA), np.float32)
    v_sel[0, :, :, 0], v_sel[1, :, :, 1] = 1.0, 1.0
    whose = np.arange(DUOS)[:, None, None] * 2 + (np.array(SPREAD_AT)[:, None] * MT + np.arange(MT)) // M
    expert_sel = (np.arange(E)[:, None, None, None] == whose).astype(np.float32)
    high_and_low = np.zeros((LOW + E,) + expert_sel.shape[1:], np.float32)
    high_and_low[0:E] = high_and_low[LOW:] = expert_sel
    return {"cos": cos.astype(np.float32), "sin": sin.astype(np.float32),
            "causal": np.tile(causal, (1, HA)).astype(np.float32), "v_sel": v_sel.reshape(2 * SQ, D),
            "head_sel": np.repeat(np.eye(HA, dtype=np.float32), DA, axis=0), "expert_sel": high_and_low,
            "rank_tri": np.broadcast_to(np.tril(np.ones((E, E), np.float32), -1), (128, E, E)).copy(),
            "ident": np.eye(128, dtype=np.float32), "row_sel": row_sel.reshape(ROW2, COLS), "pair_sel": pair_sel}


def kernel(x, ctx_1024, mask_BxSxS2_bf1, L0_xattn_Wq, L0_xattn_Wk, L0_xattn_Wv, L0_xattn_Wo, L0_ffn_ln1_w,
           L0_ffn_ln2_w, L0_ffn_wq, L0_ffn_wk, L0_ffn_wv, L0_ffn_wo, L0_ffn_router_w, L0_ffn_w_gate, L0_ffn_w_up,
           L0_ffn_w_down):
    import numpy as np
    import concourse.bacc as bacc
    from concourse.bass_utils import run_bass_kernel_spmd

    c = np.ascontiguousarray
    ctx = np.asarray(ctx_1024)
    wk = np.asarray(L0_ffn_wk)
    turned = np.arange(D) // DA * DA + (np.arange(D) + DA // 2) % DA
    arrays = {
        "x": c(x),
        "ctxT": c(ctx.transpose(0, 2, 1)),
        "ctx": c(ctx.reshape(B, NT, KT, D).transpose(0, 2, 1, 3)).reshape(B, KT, NT * D),
        "mask": c(mask_BxSxS2_bf1).view(np.uint8),
        "wqT": c(np.asarray(L0_xattn_Wq).transpose(2, 0, 1)),
        "wkT": c(np.asarray(L0_xattn_Wk).transpose(2, 0, 1)),
        "wvT": c(np.asarray(L0_xattn_Wv).transpose(2, 0, 1)),
        "wo": c(np.asarray(L0_xattn_Wo).reshape(H, DH, D).transpose(1, 0, 2)),
        "attn_q": c(L0_ffn_wq),
        "attn_q_turned": c(np.asarray(L0_ffn_wq)[:, turned]),
        "attn_k": c(np.repeat(wk.reshape(D, KV, DA), HA // KV, axis=1).reshape(D, D)),
        "attn_k_turned": c(np.repeat(wk.reshape(D, KV, DA), HA // KV, axis=1).reshape(D, D)[:, turned]),
        "attn_v": c(np.repeat(np.asarray(L0_ffn_wv).reshape(D, KV, DA), HA // KV, axis=1).reshape(D, D)),
        "attn_o": c(L0_ffn_wo),
        "router": c(L0_ffn_router_w),
        "ln_w": c(np.stack([np.asarray(L0_ffn_ln1_w), np.asarray(L0_ffn_ln2_w)], axis=1)),
        "w_up": c(np.stack([np.asarray(w).reshape(DUOS, 2, D, M).transpose(0, 2, 1, 3).reshape(DUOS, D, WIDE)
                            for w in (L0_ffn_w_gate, L0_ffn_w_up)], axis=2)),
        "w_down": c(np.asarray(L0_ffn_w_down).reshape(DUOS, NM, MT, D).transpose(0, 2, 1, 3)),
        **_constants(),
    }
    nc = bacc.Bacc("TRN2", target_bir_lowering=False, num_devices=1)
    t = {n: nc.dram_tensor(f"in_{n}", a.shape, mybir.dt.from_np(a.dtype), kind="ExternalInput").ap()
         for n, a in arrays.items()}
    out = nc.dram_tensor("out", (B, SQ, D), F32, kind="ExternalOutput").ap()
    xattn_ffn_kernel(nc, t, out)
    r = run_bass_kernel_spmd(nc, [{f"in_{n}": a for n, a in arrays.items()}], core_ids=[0])
    return r.results[0]["out"]
```
